# Optimizing a Trainium2 kernel written in Bass

```python
import numpy as np
import jax
import jax.numpy as jnp

def _softmax(x, axis=-1):
    return jax.nn.softmax(x, axis=axis)

def _gelu(x):
    return jax.nn.gelu(x, approximate=True)

def _silu(x):
    return jax.nn.silu(x)

def _sigmoid(x):
    return jax.nn.sigmoid(x)

def _layernorm(x, axis=-1, eps=1e-05):
    m = jnp.mean(x, axis=axis, keepdims=True)
    v = jnp.var(x, axis=axis, keepdims=True)
    return (x - m) / jnp.sqrt(v + eps)

def _scatter_add(tgt, idx, src, axis=0):
    return tgt.at[idx].add(src)

def _segment_sum(src, seg, n):
    return jax.ops.segment_sum(src, seg, n)
kernel_name = 'mk_seq_postln_d4_jaxref_r8_340263'

def setup_inputs(seed: int=0):
    np.random.seed(seed)
    _w = jnp.asarray

    def _L0_attn_setup():
        import jax, jax.numpy as jnp
        import numpy as np
        D_MODEL = 128
        NUM_HEADS = 16
        HEAD_DIM = D_MODEL // NUM_HEADS
        ALPHA = 1.0
        key = jax.random.key(seed)
        ks = jax.random.split(key, 9)
        B, T, D = (2, 256, D_MODEL)
        s = 1.0 / np.sqrt(D)
        inp = {'x': jax.random.normal(ks[0], (B, T, D), dtype=jnp.float32), 'Wq': jax.random.uniform(ks[1], (D, D), jnp.float32, -s, s), 'bq': jax.random.uniform(ks[2], (D,), jnp.float32, -s, s), 'Wk': jax.random.uniform(ks[3], (D, D), jnp.float32, -s, s), 'bk': jax.random.uniform(ks[4], (D,), jnp.float32, -s, s), 'Wv': jax.random.uniform(ks[5], (D, D), jnp.float32, -s, s), 'bv': jax.random.uniform(ks[6], (D,), jnp.float32, -s, s), 'Wo': jax.random.uniform(ks[7], (D, D), jnp.float32, -s, s), 'bo': jax.random.uniform(ks[8], (D,), jnp.float32, -s, s)}
        return inp
    _L0_attn_in = _L0_attn_setup()

    def _L0_ffn_setup():
        import jax, jax.numpy as jnp
        import numpy as np
        D = 128
        E = 12
        HS = 2 * D
        HR = 3 * D
        TAU = 1.5

        def _geglu(h):
            a, g = jnp.split(h, 2, axis=-1)
            return a * jax.nn.gelu(g, approximate=False)
        key = jax.random.key(seed)
        ks = jax.random.split(key, 12)

        def xavier(k, shape):
            fan_in, fan_out = (shape[-2], shape[-1])
            lim = jnp.sqrt(6.0 / (fan_in + fan_out))
            return jax.random.uniform(k, shape, jnp.float32, -lim, lim)
        x = jax.random.normal(ks[0], (2, 128, D), jnp.float32)
        Ws1 = xavier(ks[1], (D, 2 * HS))
        bs1 = jnp.zeros((2 * HS,), jnp.float32)
        Ws2 = xavier(ks[2], (HS, D))
        bs2 = jnp.zeros((D,), jnp.float32)
        We1 = xavier(ks[3], (E, D, 2 * HR))
        be1 = jnp.zeros((E, 2 * HR), jnp.float32)
        We2 = xavier(ks[4], (E, HR, D))
        be2 = jnp.zeros((E, D), jnp.float32)
        Wr = xavier(ks[5], (D, E))
        br = jnp.zeros((E,), jnp.float32)
        return {'x': x, 'Ws1': Ws1, 'bs1': bs1, 'Ws2': Ws2, 'bs2': bs2, 'We1': We1, 'be1': be1, 'We2': We2, 'be2': be2, 'Wr': Wr, 'br': br}
    _L0_ffn_in = _L0_ffn_setup()

    def _L1_attn_setup():
        import jax, jax.numpy as jnp
        import numpy as np
        B, T, D = (1, 256, 128)
        H, DH, DV, DF = (16, 64, 64, 512)
        EPS_LN = 1e-05
        EPS_DEN = 1e-06

        def _layernorm(x, g, b):
            m = jnp.mean(x, axis=-1, keepdims=True)
            v = jnp.mean((x - m) ** 2, axis=-1, keepdims=True)
            return (x - m) / jnp.sqrt(v + EPS_LN) * g + b

        def _phi(x):
            return jax.nn.elu(x) + 1.0

        def _linear_attention(x, Wq, Wk, Wv, Wo):
            b, t, d = x.shape
            Q = _phi((x @ Wq).reshape(b, t, H, DH)).transpose(0, 2, 1, 3)
            K = _phi((x @ Wk).reshape(b, t, H, DH)).transpose(0, 2, 1, 3)
            V = (x @ Wv).reshape(b, t, H, DV).transpose(0, 2, 1, 3)
            KV = jnp.einsum('bhti,bhtj->bhtij', K, V)
            S = jnp.cumsum(KV, axis=2)
            z = jnp.cumsum(K, axis=2)
            num = jnp.einsum('bhti,bhtij->bhtj', Q, S)
            den = jnp.maximum(jnp.einsum('bhti,bhti->bht', Q, z), EPS_DEN)[..., None]
            out = (num / den).transpose(0, 2, 1, 3).reshape(b, t, H * DV)
            return out @ Wo
        key = jax.random.key(seed)
        ks = jax.random.split(key, 8)
        s = 0.02
        return {'x': jax.random.normal(ks[0], (B, T, D), dtype=jnp.float32), 'ln1_g': jnp.ones((D,), jnp.float32), 'ln1_b': jnp.zeros((D,), jnp.float32), 'Wq': jax.random.normal(ks[1], (D, H * DH), jnp.float32) * s, 'Wk': jax.random.normal(ks[2], (D, H * DH), jnp.float32) * s, 'Wv': jax.random.normal(ks[3], (D, H * DV), jnp.float32) * s, 'Wo': jax.random.normal(ks[4], (H * DV, D), jnp.float32) * s, 'ln2_g': jnp.ones((D,), jnp.float32), 'ln2_b': jnp.zeros((D,), jnp.float32), 'Wf1': jax.random.normal(ks[5], (D, DF), jnp.float32) * s, 'Wf2': jax.random.normal(ks[6], (DF, D), jnp.float32) * s}
    _L1_attn_in = _L1_attn_setup()

    def _L1_ffn_setup():
        import jax, jax.numpy as jnp
        import numpy as np
        EPS = 1e-06
        LN_EPS = 1e-05

        def _absmean_core(W):
            gamma = jnp.mean(jnp.abs(W)) + EPS
            Ws = W / gamma
            Wq = jnp.sign(Ws) * jnp.minimum(jnp.round(jnp.abs(Ws)), 1.0)
            return (Wq, gamma)

        @jax.custom_vjp
        def absmean(W):
            return _absmean_core(W)[0]

        def _absmean_fwd(W):
            Wq, gamma = _absmean_core(W)
            return (Wq, gamma)

        def _absmean_bwd(gamma, g):
            return (g / gamma,)
        absmean.defvjp(_absmean_fwd, _absmean_bwd)

        def layernorm(x, w, b, eps=LN_EPS):
            mu = jnp.mean(x, axis=-1, keepdims=True)
            var = jnp.mean((x - mu) ** 2, axis=-1, keepdims=True)
            return (x - mu) * jax.lax.rsqrt(var + eps) * w + b
        key = jax.random.key(seed)
        k1, k2, k3 = jax.random.split(key, 3)
        d, h = (128, 512)
        B, T = (8, 256)
        return {'x': jax.random.normal(k1, (B, T, d), jnp.float32), 'W_fc': jax.random.normal(k2, (h, d), jnp.float32), 'ln_w': jnp.ones((h,), jnp.float32), 'ln_b': jnp.zeros((h,), jnp.float32), 'W_proj': jax.random.normal(k3, (d, h), jnp.float32)}
    _L1_ffn_in = _L1_ffn_setup()

    def _L2_attn_setup():
        import jax, jax.numpy as jnp
        import numpy as np
        B, S, H, NH = (1, 512, 128, 16)
        DH = H // NH

        def _split_heads(x):
            b, s, h = x.shape
            return jnp.transpose(x.reshape(b, s, NH, DH), (0, 2, 1, 3))
        key = jax.random.key(seed)
        ks = jax.random.split(key, 9)
        sc = 0.02
        return {'queries': jax.random.normal(ks[0], (B, S, H), jnp.float32), 'keys': jax.random.normal(ks[1], (B, S, H), jnp.float32), 'values': jax.random.normal(ks[2], (B, S, H), jnp.float32), 'Wq_w': jax.random.normal(ks[3], (H, H), jnp.float32) * sc, 'Wq_b': jax.random.normal(ks[4], (H,), jnp.float32) * sc, 'Wk_w': jax.random.normal(ks[5], (H, H), jnp.float32) * sc, 'Wk_b': jax.random.normal(ks[6], (H,), jnp.float32) * sc, 'Wv_w': jax.random.normal(ks[7], (H, H), jnp.float32) * sc, 'Wv_b': jax.random.normal(ks[8], (H,), jnp.float32) * sc}
    _L2_attn_in = _L2_attn_setup()

    def _L2_ffn_setup():
        import jax, jax.numpy as jnp
        import numpy as np
        B, S, D = (2, 256, 128)
        DFF = 256
        E_FFN = 8
        E_ZERO = 4
        E_TOT = E_FFN + E_ZERO
        TOP_K = 2
        key = jax.random.key(seed)
        k1, k2, k3, k4 = jax.random.split(key, 4)
        x = jax.random.normal(k1, (B, S, D), dtype=jnp.float32)
        gate_w = jax.random.normal(k2, (E_TOT, D), dtype=jnp.float32) * (1.0 / np.sqrt(D))
        expert_bias = jnp.zeros((E_TOT,), dtype=jnp.float32)
        w1 = jax.random.normal(k3, (E_FFN, DFF, D), dtype=jnp.float32) * (1.0 / np.sqrt(D))
        w2 = jax.random.normal(k4, (E_FFN, D, DFF), dtype=jnp.float32) * (1.0 / np.sqrt(DFF))
        return {'x': x, 'gate_w': gate_w, 'expert_bias': expert_bias, 'w1': w1, 'w2': w2}
    _L2_ffn_in = _L2_ffn_setup()

    def _L3_attn_setup():
        import jax, jax.numpy as jnp
        import numpy as np
        B, N, C = (2, 256, 128)
        H = 16
        HD = C // H
        R = 16
        LORA_SCALE = 32.0 / R
        ATTN_SCALE = HD ** (-0.5)
        key = jax.random.key(seed)
        ks = jax.random.split(key, 10)
        s = lambda fan_in: 1.0 / np.sqrt(fan_in)
        return {'x': jax.random.normal(ks[0], (B, N, C), dtype=jnp.float32), 'w_qkv': jax.random.normal(ks[1], (C, 3 * C), dtype=jnp.float32) * s(C), 'b_qkv': jax.random.normal(ks[2], (3 * C,), dtype=jnp.float32) * 0.02, 'a_q': jax.random.normal(ks[3], (HD, R), dtype=jnp.float32) * s(HD), 'b_q': jax.random.normal(ks[4], (R, HD), dtype=jnp.float32) * 0.02, 'a_v': jax.random.normal(ks[5], (HD, R), dtype=jnp.float32) * s(HD), 'b_v': jax.random.normal(ks[6], (R, HD), dtype=jnp.float32) * 0.02, 'w_proj': jax.random.normal(ks[7], (C, C), dtype=jnp.float32) * s(C), 'b_proj': jax.random.normal(ks[8], (C,), dtype=jnp.float32) * 0.02}
    _L3_attn_in = _L3_attn_setup()

    def _L3_ffn_setup():
        import jax, jax.numpy as jnp
        import numpy as np
        B, N, D = (4, 256, 128)
        SPARSITY = 0.01
        key = jax.random.key(seed)
        k1, k2, k3 = jax.random.split(key, 3)
        x = jax.random.normal(k1, (B, N, D), dtype=jnp.float32)
        spatial = jax.random.normal(k2, (D, D), dtype=jnp.float32) * 0.02
        freq = jnp.fft.fft(spatial, axis=-1)
        k = int(D * SPARSITY)
        mag = jnp.abs(freq)
        kth = jax.lax.top_k(mag, k)[0][:, -1:]
        w_sparse = jnp.where(mag >= kth, freq, 0.0 + 0j)
        bias = jax.random.normal(k3, (D,), dtype=jnp.float32) * 0.01
        return {'x': x, 'w_freq_real': jnp.real(w_sparse).astype(jnp.float32), 'w_freq_imag': jnp.imag(w_sparse).astype(jnp.float32), 'bias': bias}
    _L3_ffn_in = _L3_ffn_setup()
    _d = {'L0_attn_x': _L0_attn_in['x'], 'L0_attn_Wq': _L0_attn_in['Wq'], 'L0_attn_bq': _L0_attn_in['bq'], 'L0_attn_Wk': _L0_attn_in['Wk'], 'L0_attn_bk': _L0_attn_in['bk'], 'L0_attn_Wv': _L0_attn_in['Wv'], 'L0_attn_bv': _L0_attn_in['bv'], 'L0_attn_Wo': _L0_attn_in['Wo'], 'L0_attn_bo': _L0_attn_in['bo'], 'L0_ffn_Ws1': _L0_ffn_in['Ws1'], 'L0_ffn_bs1': _L0_ffn_in['bs1'], 'L0_ffn_Ws2': _L0_ffn_in['Ws2'], 'L0_ffn_bs2': _L0_ffn_in['bs2'], 'L0_ffn_We1': _L0_ffn_in['We1'], 'L0_ffn_be1': _L0_ffn_in['be1'], 'L0_ffn_We2': _L0_ffn_in['We2'], 'L0_ffn_be2': _L0_ffn_in['be2'], 'L0_ffn_Wr': _L0_ffn_in['Wr'], 'L0_ffn_br': _L0_ffn_in['br'], 'L1_attn_ln1_g': _L1_attn_in['ln1_g'], 'L1_attn_ln1_b': _L1_attn_in['ln1_b'], 'L1_attn_Wq': _L1_attn_in['Wq'], 'L1_attn_Wk': _L1_attn_in['Wk'], 'L1_attn_Wv': _L1_attn_in['Wv'], 'L1_attn_Wo': _L1_attn_in['Wo'], 'L1_attn_ln2_g': _L1_attn_in['ln2_g'], 'L1_attn_ln2_b': _L1_attn_in['ln2_b'], 'L1_attn_Wf1': _L1_attn_in['Wf1'], 'L1_attn_Wf2': _L1_attn_in['Wf2'], 'L1_ffn_W_fc': _L1_ffn_in['W_fc'], 'L1_ffn_ln_w': _L1_ffn_in['ln_w'], 'L1_ffn_ln_b': _L1_ffn_in['ln_b'], 'L1_ffn_W_proj': _L1_ffn_in['W_proj'], 'L2_attn_keys': _L2_attn_in['keys'], 'L2_attn_values': _L2_attn_in['values'], 'L2_attn_Wq_w': _L2_attn_in['Wq_w'], 'L2_attn_Wq_b': _L2_attn_in['Wq_b'], 'L2_attn_Wk_w': _L2_attn_in['Wk_w'], 'L2_attn_Wk_b': _L2_attn_in['Wk_b'], 'L2_attn_Wv_w': _L2_attn_in['Wv_w'], 'L2_attn_Wv_b': _L2_attn_in['Wv_b'], 'L2_ffn_gate_w': _L2_ffn_in['gate_w'], 'L2_ffn_expert_bias': _L2_ffn_in['expert_bias'], 'L2_ffn_w1': _L2_ffn_in['w1'], 'L2_ffn_w2': _L2_ffn_in['w2'], 'L3_attn_w_qkv': _L3_attn_in['w_qkv'], 'L3_attn_b_qkv': _L3_attn_in['b_qkv'], 'L3_attn_a_q': _L3_attn_in['a_q'], 'L3_attn_b_q': _L3_attn_in['b_q'], 'L3_attn_a_v': _L3_attn_in['a_v'], 'L3_attn_b_v': _L3_attn_in['b_v'], 'L3_attn_w_proj': _L3_attn_in['w_proj'], 'L3_attn_b_proj': _L3_attn_in['b_proj'], 'L3_ffn_w_freq_real': _L3_ffn_in['w_freq_real'], 'L3_ffn_w_freq_imag': _L3_ffn_in['w_freq_imag'], 'L3_ffn_bias': _L3_ffn_in['bias']}
    _x0 = _d['L0_attn_x']
    _d['L0_attn_x'] = jax.random.normal(jax.random.fold_in(jax.random.key(seed), 1), (8, 512, 128), dtype=_x0.dtype)
    del _x0
    return _d

def reference(L0_attn_x, L0_attn_Wq, L0_attn_bq, L0_attn_Wk, L0_attn_bk, L0_attn_Wv, L0_attn_bv, L0_attn_Wo, L0_attn_bo, L0_ffn_Ws1, L0_ffn_bs1, L0_ffn_Ws2, L0_ffn_bs2, L0_ffn_We1, L0_ffn_be1, L0_ffn_We2, L0_ffn_be2, L0_ffn_Wr, L0_ffn_br, L1_attn_ln1_g, L1_attn_ln1_b, L1_attn_Wq, L1_attn_Wk, L1_attn_Wv, L1_attn_Wo, L1_attn_ln2_g, L1_attn_ln2_b, L1_attn_Wf1, L1_attn_Wf2, L1_ffn_W_fc, L1_ffn_ln_w, L1_ffn_ln_b, L1_ffn_W_proj, L2_attn_keys, L2_attn_values, L2_attn_Wq_w, L2_attn_Wq_b, L2_attn_Wk_w, L2_attn_Wk_b, L2_attn_Wv_w, L2_attn_Wv_b, L2_ffn_gate_w, L2_ffn_expert_bias, L2_ffn_w1, L2_ffn_w2, L3_attn_w_qkv, L3_attn_b_qkv, L3_attn_a_q, L3_attn_b_q, L3_attn_a_v, L3_attn_b_v, L3_attn_w_proj, L3_attn_b_proj, L3_ffn_w_freq_real, L3_ffn_w_freq_imag, L3_ffn_bias):

    def _L0_attn_ref(x, Wq, bq, Wk, bk, Wv, bv, Wo, bo):
        import jax, jax.numpy as jnp
        import numpy as np
        D_MODEL = 128
        NUM_HEADS = 16
        HEAD_DIM = D_MODEL // NUM_HEADS
        ALPHA = 1.0
        B, T, D = x.shape
        H, hd = (NUM_HEADS, HEAD_DIM)

        def split_heads(y):
            return y.reshape(B, T, H, hd).transpose(0, 2, 1, 3)
        Q = split_heads(x @ Wq.T + bq)
        K = split_heads(x @ Wk.T + bk)
        V = split_heads(x @ Wv.T + bv)
        scores = jnp.einsum('bhid,bhjd->bhij', Q, K) / jnp.sqrt(jnp.float32(hd))
        t = jnp.arange(T)
        delta = t[:, None] - t[None, :]
        causal_mask = delta < 0
        decay = jnp.where(causal_mask, 0.0, -delta.astype(jnp.float32) ** ALPHA)
        scores = jnp.where(causal_mask, -jnp.inf, scores) + decay
        attn = jax.nn.softmax(scores, axis=-1)
        out = jnp.einsum('bhij,bhjd->bhid', attn, V)
        out = out.transpose(0, 2, 1, 3).reshape(B, T, D)
        return out @ Wo.T + bo

    def _L0_ffn_ref(x, Ws1, bs1, Ws2, bs2, We1, be1, We2, be2, Wr, br):
        import jax, jax.numpy as jnp
        import numpy as np
        D = 128
        E = 12
        HS = 2 * D
        HR = 3 * D
        TAU = 1.5

        def _geglu(h):
            a, g = jnp.split(h, 2, axis=-1)
            return a * jax.nn.gelu(g, approximate=False)
        B, T, Dm = x.shape
        xf = x.reshape(-1, Dm)
        ys = _geglu(xf @ Ws1 + bs1) @ Ws2 + bs2
        logits = (xf @ Wr + br) / TAU
        top_val, top_idx = jax.lax.top_k(logits, 2)
        top_w = jax.nn.softmax(top_val, axis=-1)
        onehot = jax.nn.one_hot(top_idx, E, dtype=x.dtype)
        w = jnp.einsum('nke,nk->ne', onehot, top_w)
        h = jnp.einsum('nd,edh->enh', xf, We1) + be1[:, None, :]
        act = _geglu(h)
        yE = jnp.einsum('enh,ehd->end', act, We2) + be2[:, None, :]
        yr = jnp.einsum('end,ne->nd', yE, w)
        return (ys + yr).reshape(B, T, Dm)

    def _L1_attn_ref(x, ln1_g, ln1_b, Wq, Wk, Wv, Wo, ln2_g, ln2_b, Wf1, Wf2):
        import jax, jax.numpy as jnp
        import numpy as np
        B, T, D = (1, 256, 128)
        H, DH, DV, DF = (16, 64, 64, 512)
        EPS_LN = 1e-05
        EPS_DEN = 1e-06

        def _layernorm(x, g, b):
            m = jnp.mean(x, axis=-1, keepdims=True)
            v = jnp.mean((x - m) ** 2, axis=-1, keepdims=True)
            return (x - m) / jnp.sqrt(v + EPS_LN) * g + b

        def _phi(x):
            return jax.nn.elu(x) + 1.0

        def _linear_attention(x, Wq, Wk, Wv, Wo):
            b, t, d = x.shape
            Q = _phi((x @ Wq).reshape(b, t, H, DH)).transpose(0, 2, 1, 3)
            K = _phi((x @ Wk).reshape(b, t, H, DH)).transpose(0, 2, 1, 3)
            V = (x @ Wv).reshape(b, t, H, DV).transpose(0, 2, 1, 3)
            KV = jnp.einsum('bhti,bhtj->bhtij', K, V)
            S = jnp.cumsum(KV, axis=2)
            z = jnp.cumsum(K, axis=2)
            num = jnp.einsum('bhti,bhtij->bhtj', Q, S)
            den = jnp.maximum(jnp.einsum('bhti,bhti->bht', Q, z), EPS_DEN)[..., None]
            out = (num / den).transpose(0, 2, 1, 3).reshape(b, t, H * DV)
            return out @ Wo
        x = x + _linear_attention(_layernorm(x, ln1_g, ln1_b), Wq, Wk, Wv, Wo)
        h = _layernorm(x, ln2_g, ln2_b)
        x = x + jax.nn.gelu(h @ Wf1, approximate=False) @ Wf2
        return x

    def _L1_ffn_ref(x, W_fc, ln_w, ln_b, W_proj):
        import jax, jax.numpy as jnp
        import numpy as np
        EPS = 1e-06
        LN_EPS = 1e-05

        def _absmean_core(W):
            gamma = jnp.mean(jnp.abs(W)) + EPS
            Ws = W / gamma
            Wq = jnp.sign(Ws) * jnp.minimum(jnp.round(jnp.abs(Ws)), 1.0)
            return (Wq, gamma)

        @jax.custom_vjp
        def absmean(W):
            return _absmean_core(W)[0]

        def _absmean_fwd(W):
            Wq, gamma = _absmean_core(W)
            return (Wq, gamma)

        def _absmean_bwd(gamma, g):
            return (g / gamma,)
        absmean.defvjp(_absmean_fwd, _absmean_bwd)

        def layernorm(x, w, b, eps=LN_EPS):
            mu = jnp.mean(x, axis=-1, keepdims=True)
            var = jnp.mean((x - mu) ** 2, axis=-1, keepdims=True)
            return (x - mu) * jax.lax.rsqrt(var + eps) * w + b
        h = jnp.einsum('btd,hd->bth', x, absmean(W_fc))
        h = jax.nn.gelu(h, approximate=False)
        h = layernorm(h, ln_w, ln_b)
        return jnp.einsum('bth,dh->btd', h, absmean(W_proj))

    def _L2_attn_ref(queries, keys, values, Wq_w, Wq_b, Wk_w, Wk_b, Wv_w, Wv_b):
        import jax, jax.numpy as jnp
        import numpy as np
        B, S, H, NH = (1, 512, 128, 16)
        DH = H // NH

        def _split_heads(x):
            b, s, h = x.shape
            return jnp.transpose(x.reshape(b, s, NH, DH), (0, 2, 1, 3))
        q = jax.nn.relu(queries @ Wq_w.T + Wq_b)
        k = jax.nn.relu(keys @ Wk_w.T + Wk_b)
        v = jax.nn.relu(values @ Wv_w.T + Wv_b)
        qh, kh, vh = (_split_heads(q), _split_heads(k), _split_heads(v))
        score = jnp.einsum('bhsd,bhtd->bhst', qh, kh) / jnp.sqrt(jnp.float32(DH))
        attn = jax.nn.softmax(score, axis=-1)
        a = jnp.einsum('bhst,bhtd->bhsd', attn, vh)
        a = jnp.transpose(a, (0, 1, 3, 2)).reshape(q.shape[0], q.shape[1], q.shape[2])
        return a + queries

    def _L2_ffn_ref(x, gate_w, expert_bias, w1, w2):
        import jax, jax.numpy as jnp
        import numpy as np
        B, S, D = (2, 256, 128)
        DFF = 256
        E_FFN = 8
        E_ZERO = 4
        E_TOT = E_FFN + E_ZERO
        TOP_K = 2
        logits = jnp.einsum('btd,ed->bte', x, gate_w) + expert_bias
        topk_logits, topk_idx = jax.lax.top_k(logits, TOP_K)
        topk_w = jax.nn.softmax(topk_logits, axis=-1)
        onehot = jax.nn.one_hot(topk_idx, E_TOT, dtype=x.dtype)
        w = jnp.einsum('btk,btke->bte', topk_w, onehot)
        w_ffn = w[..., :E_FFN]
        w_zero = jnp.sum(w[..., E_FFN:], axis=-1)
        h = jax.nn.silu(jnp.einsum('btd,efd->btef', x, w1))
        y = jnp.einsum('btef,edf->bted', h, w2)
        out = jnp.einsum('bte,bted->btd', w_ffn, y) + w_zero[..., None] * x
        return out

    def _L3_attn_ref(x, w_qkv, b_qkv, a_q, b_q, a_v, b_v, w_proj, b_proj):
        import jax, jax.numpy as jnp
        import numpy as np
        B, N, C = (2, 256, 128)
        H = 16
        HD = C // H
        R = 16
        LORA_SCALE = 32.0 / R
        ATTN_SCALE = HD ** (-0.5)
        Bb, Nn, Cc = x.shape
        qkv = (x @ w_qkv + b_qkv).reshape(Bb, Nn, 3, H, HD).transpose(2, 0, 3, 1, 4)
        q, k, v = (qkv[0], qkv[1], qkv[2])
        q = q + jnp.einsum('bhnr,rd->bhnd', jnp.einsum('bhnd,dr->bhnr', q, a_q), b_q) * LORA_SCALE
        v = v + jnp.einsum('bhnr,rd->bhnd', jnp.einsum('bhnd,dr->bhnr', v, a_v), b_v) * LORA_SCALE
        attn = jax.nn.softmax(jnp.einsum('bhnd,bhmd->bhnm', q, k) * ATTN_SCALE, axis=-1)
        out = jnp.einsum('bhnm,bhmd->bhnd', attn, v)
        out = out.transpose(0, 2, 1, 3).reshape(Bb, Nn, Cc)
        return out @ w_proj + b_proj

    def _L3_ffn_ref(x, w_freq_real, w_freq_imag, bias):
        import jax, jax.numpy as jnp
        import numpy as np
        B, N, D = (4, 256, 128)
        SPARSITY = 0.01
        w = jax.lax.complex(w_freq_real, w_freq_imag)
        x_freq = jnp.fft.fft(x, axis=-1)
        y_freq = jnp.einsum('bnd,do->bno', x_freq, w)
        y = jnp.real(jnp.fft.ifft(y_freq, axis=-1))
        return y + bias
    x = L0_attn_x
    x = _layernorm(x + _L0_attn_ref(x, L0_attn_Wq, L0_attn_bq, L0_attn_Wk, L0_attn_bk, L0_attn_Wv, L0_attn_bv, L0_attn_Wo, L0_attn_bo), axis=-1)
    x = _layernorm(x + _L0_ffn_ref(x, L0_ffn_Ws1, L0_ffn_bs1, L0_ffn_Ws2, L0_ffn_bs2, L0_ffn_We1, L0_ffn_be1, L0_ffn_We2, L0_ffn_be2, L0_ffn_Wr, L0_ffn_br), axis=-1)
    x = _layernorm(x + _L1_attn_ref(x, L1_attn_ln1_g, L1_attn_ln1_b, L1_attn_Wq, L1_attn_Wk, L1_attn_Wv, L1_attn_Wo, L1_attn_ln2_g, L1_attn_ln2_b, L1_attn_Wf1, L1_attn_Wf2), axis=-1)
    x = _layernorm(x + _L1_ffn_ref(x, L1_ffn_W_fc, L1_ffn_ln_w, L1_ffn_ln_b, L1_ffn_W_proj), axis=-1)
    x = _layernorm(x + _L2_attn_ref(x, L2_attn_keys, L2_attn_values, L2_attn_Wq_w, L2_attn_Wq_b, L2_attn_Wk_w, L2_attn_Wk_b, L2_attn_Wv_w, L2_attn_Wv_b), axis=-1)
    x = _layernorm(x + _L2_ffn_ref(x, L2_ffn_gate_w, L2_ffn_expert_bias, L2_ffn_w1, L2_ffn_w2), axis=-1)
    x = _layernorm(x + _L3_attn_ref(x, L3_attn_w_qkv, L3_attn_b_qkv, L3_attn_a_q, L3_attn_b_q, L3_attn_a_v, L3_attn_b_v, L3_attn_w_proj, L3_attn_b_proj), axis=-1)
    x = _layernorm(x + _L3_ffn_ref(x, L3_ffn_w_freq_real, L3_ffn_w_freq_imag, L3_ffn_bias), axis=-1)
    return x

_drawn_inputs = setup_inputs


def setup_inputs(seed=0):
    import zlib

    import numpy as np

    out = dict(_drawn_inputs(seed))
    spreads = {'L0_ffn_bs1': (0.0, 0.1),
     'L0_ffn_bs2': (0.0, 0.1),
     'L0_ffn_be1': (0.0, 0.1),
     'L0_ffn_be2': (0.0, 0.1),
     'L0_ffn_br': (0.0, 0.1),
     'L1_attn_ln1_g': (1.0, 0.6),
     'L1_attn_ln1_b': (0.0, 0.298),
     'L1_attn_ln2_g': (1.0, 0.6),
     'L1_attn_ln2_b': (0.0, 0.598),
     'L1_ffn_ln_w': (1.0, 0.2),
     'L1_ffn_ln_b': (0.0, 0.1),
     'L2_ffn_expert_bias': (0.0, 0.1)}
    factors = {'L0_attn_bq': 2.965,
     'L0_attn_bk': 8.0,
     'L1_attn_Wq': 8.0,
     'L1_attn_Wk': 8.0,
     'L2_attn_keys': 8.0,
     'L2_attn_values': 8.0,
     'L2_attn_Wq_w': 8.0,
     'L2_attn_Wq_b': 8.0,
     'L2_attn_Wk_w': 8.0,
     'L2_attn_Wk_b': 8.0,
     'L2_attn_Wv_w': 8.0,
     'L2_attn_Wv_b': 8.0,
     'L3_attn_a_q': 2.703,
     'L3_attn_b_proj': 2.689,
     'L3_ffn_bias': 6.191}
    for name, (base, spread) in spreads.items():
        noise = np.random.default_rng([zlib.crc32(name.encode()), seed]).standard_normal(out[name].shape)
        drawn = base * np.exp(spread * noise) if base else spread * noise
        out[name] = jnp.asarray(drawn.astype(out[name].dtype))
    for name, factor in factors.items():
        out[name] = (out[name] * factor).astype(out[name].dtype)
    return out
```

```python
from contextlib import ExitStack

import concourse.bass as bass
import numpy as np
from concourse import mybir

F32 = mybir.dt.float32
BF16 = mybir.dt.bfloat16
U32 = mybir.dt.uint32
ALU = mybir.AluOpType
ACT = mybir.ActivationFunctionType
AX = mybir.AxisListType

P = 128
B = 8
T = 512
NT = T // P
H = 16
HD = P // H
GH = 4
NG = H // GH
LN_EPS = 1e-5
MASKED = -1e30

DECAY_ROWS = 4
PARTS = 3
MAX_ROW = 96


class Flag:

    def __init__(self, sem, per, lead=1, first=0):
        self.sem, self.per, self.lead, self.first = sem, per, lead, first

    def upto(self, turn, k):
        return turn * self.per + (self.lead * self.per + k)

    def wait(self, engine, turn, k=None):
        engine.wait_ge(self.sem, self.upto(turn, self.per if k is None else k))


class Chain:

    def __init__(self, signal, engine, turn):
        self.flag, self.engine, self.turn, self.n = signal, engine, turn, 0

    def step(self, instruction):
        self.n += 1
        assert self.n <= self.flag.per, (self.n, self.flag.per)
        instruction.then_inc(self.flag.sem, 1)

    def wait(self):
        self.flag.wait(self.engine, self.turn, self.n)

    def end(self):
        assert self.n == self.flag.per, (self.n, self.flag.per)


class Stage:

    def __init__(self, nc, ctx, tag):
        self.nc, self.ctx, self.tag, self.flags, self.sems = nc, ctx, tag, [], []

    def sb(self, name, shape, dt=F32):
        return self.ctx.enter_context(self.nc.sbuf_tensor(f"{self.tag}_{name}", shape, dt))

    def ps(self, name, shape):
        return self.ctx.enter_context(self.nc.psum_tensor(f"{self.tag}_{name}", shape, F32))

    def sem(self, name):
        self.sems.append(self.ctx.enter_context(self.nc.semaphore(f"{self.tag}_{name}")))
        return self.sems[-1]

    def flag(self, name, per, lead=1, first=0):
        s = Flag(self.sem(name), per, lead, first)
        self.flags.append(s)
        return s

    def credit(self):
        with self.nc.Block() as block:
            @block.sync
            def _(sp):
                for s in self.flags:
                    if s.lead + s.first:
                        sp.sem_inc(s.sem, (s.lead + s.first) * s.per)
        self.ctx.callback(self.retire)

    def retire(self):
        with self.nc.Block() as block:
            @block.sync
            def _(sp):
                for s in self.sems:
                    sp.sem_clear(s)


def stand(engine, passed):
    engine.sem_inc(passed, 1)


def turns(engine, n):
    return engine.Fori(0, n)


def batch(array, b):
    return array[:, bass.ds(b, 1), :, :].rearrange("p a t d -> p (a t) d")



class Load:

    def __init__(self, m, G, src, normalised=True, affine=None):
        self.m, self.G, self.src, self.normalised, self.affine = m, G, src, normalised, affine
        self.xs = m.sb("xs", [P, NT, P])
        self.xT = m.sb("xT", [P, T])
        self.psX = m.ps("psX", [P, T])
        self.xs_ready = m.flag("xs_ready", 1)
        self.x_kept = m.flag("x_kept", 1)
        self.turned = m.flag("turned", 1)
        self.xT_ready = m.flag("xT_ready", 1)

    def scalar(self, e, b):
        self.turned.wait(e, b - 1)
        self.x_kept.wait(e, b - 1)
        x = batch(self.src, b)
        if not self.normalised:
            e.activation(self.xs[:], x, ACT.Copy).then_inc(self.xs_ready.sem, 1)
            return
        for t in range(NT):
            last = e.activation(self.xs[:, t, :], x[:, t, :], ACT.Identity,
                                scale=self.G.rstd[:, bass.ds(b, 1), t], bias=self.G.shift[:, bass.ds(b, 1), t])
        last.then_inc(self.xs_ready.sem, 1)

    def pool(self, e, b):
        self.xs_ready.wait(e, b)
        e.tensor_copy(batch(self.src, b), self.xs[:]).then_inc(self.x_kept.sem, 1)

    def tensor(self, e, b):
        self.xs_ready.wait(e, b)
        self.xT_ready.wait(e, b - 1)
        for t in range(NT):
            last = e.transpose(self.psX[:, t * P:(t + 1) * P], self.xs[:, t, :], self.G.ident[:])
        last.then_inc(self.turned.sem, 1)

    def vector(self, e, b, users):
        self.turned.wait(e, b)
        for s in users:
            s.wait(e, b - 1)
        out, turned = self.xT[:].rearrange("d (p t) -> d t p", t=NT), self.psX[:].rearrange("d (t p) -> d t p", t=NT)
        if self.affine is None:
            e.tensor_copy(out, turned).then_inc(self.xT_ready.sem, 1)
        else:
            gain, offset = self.affine
            e.tensor_scalar(out, turned, gain[:, 0:1], offset[:, 0:1], ALU.mult, ALU.add)\
             .then_inc(self.xT_ready.sem, 1)


class Post:

    def __init__(self, m, G):
        self.G = G
        self.stats = m.sb("stats", [P, NT, 6])
        self.mv = m.sb("mv", [P, NT, 2])
        self.summed = m.flag("summed", 1)
        self.stat = m.flag("stat", 1)
        self.passed = m.sem("passed")
        self.aggregated = m.flag("aggregated", 1)
        self.mv_kept = m.flag("mv_kept", 1)

    def vector(self, e, b, row):
        self.summed.wait(e, b)
        stand(e, self.passed)
        for t in range(NT):
            last = e.bn_stats(self.stats[:, t, :], row[:, t, :])
        last.then_inc(self.stat.sem, 1)
        self.stat.wait(e, b)
        stand(e, self.passed)
        for t in range(NT):
            last = e.bn_aggr(self.mv[:, t, :], self.stats[:, t, :])
        last.then_inc(self.aggregated.sem, 1)
        self.aggregated.wait(e, b)
        e.tensor_copy(batch(self.G.mv, b), self.mv[:]).then_inc(self.mv_kept.sem, 1)

    def finish(self, e, sem):
        G = self.G
        self.mv_kept.wait(e, B - 1)
        rstd, shift = G.rstd[:], G.shift[:]
        e.tensor_scalar(rstd, G.mv[:, :, :, 1], LN_EPS, None, ALU.add).then_inc(sem, 1)
        e.wait_ge(sem, 1)
        e.tensor_tensor(rstd, rstd, G.minus_half[:], ALU.pow).then_inc(sem, 1)
        e.wait_ge(sem, 2)
        e.tensor_tensor(shift, G.mv[:, :, :, 0], rstd, ALU.mult).then_inc(sem, 1)
        e.wait_ge(sem, 3)
        e.tensor_scalar(shift, shift, -1.0, None, ALU.mult).then_inc(sem, 1)
        e.wait_ge(sem, 4)


class Globals:
    pass


def setup(nc, ctx, a):
    G = Globals()
    m = Stage(nc, ctx, "g")
    G.X = m.sb("X", [P, B, NT, P])
    G.X1 = m.sb("X1", [P, B, NT, P])
    G.mv = m.sb("mv", [P, B, NT, 2])
    G.rstd = m.sb("rstd", [P, B, NT])
    G.shift = m.sb("shift", [P, B, NT])
    G.minus_half = m.sb("minus_half", [P, B, NT])
    G.ident = m.sb("ident", [P, P])
    G.identb = m.sb("identb", [P, P], BF16)
    loaded, filled = m.sem("loaded"), m.sem("filled")
    with nc.Block() as block:
        @block.sync
        def _(sp):
            sp.dma_start(G.ident[:], a["c_ident"]).then_inc(loaded, 16)
            sp.dma_start(G.X[:], a["L0_attn_x"].rearrange("b (p t) d -> p b t d", t=NT)).then_inc(loaded, 16)
            sp.wait_ge(loaded, 32)

        @block.gpsimd
        def _(pool):
            pool.memset(G.rstd[:], 1.0)
            pool.memset(G.shift[:], 0.0)
            pool.memset(G.minus_half[:], -0.5).then_inc(filled, 1)

        @block.vector
        def _(dve):
            dve.wait_ge(loaded, 32)
            dve.tensor_copy(G.identb[:], G.ident[:]).then_inc(filled, 1)
    return G



def project(nc, G, tag, src, n, q=None, k=None, v=None, normalised=True):
    with ExitStack() as ctx:
        m = Stage(nc, ctx, tag)
        load = Load(m, G, src, normalised)
        sides = [s for s in (q, k) if s]
        loaded, prepared = m.sem("loaded"), m.sem("prepared")
        nload = 0
        for i, s in enumerate(sides):
            s["W"] = m.sb(f"W{i}", [P, P])
            s["bias"] = m.sb(f"bias{i}", [P, 1])
            s["sbias"] = m.sb(f"sbias{i}", [P, 1])
            s["full"] = m.sb(f"full{i}", [P, T])
            s["raw"] = m.sb(f"raw{i}", [P, T]) if s["mix"] else None
            s["rest"] = m.sb(f"rest{i}", [P, T])
            s["bf"] = m.sb(f"bf{i}", [P, PARTS, T], BF16)
            s["ps"] = m.ps(f"ps{i}", [P, T])
            s["projected"] = m.flag(f"projected{i}", 1)
            s["raw_ready"] = m.flag(f"raw_ready{i}", 1)
            s["mixed"] = m.flag(f"mixed{i}", 1)
            s["full_ready"] = m.flag(f"full_ready{i}", 1)
            s["high_ready"] = m.flag(f"high_ready{i}", 1)
            s["rest_ready"] = m.flag(f"rest_ready{i}", 1)
            s["mid_ready"] = m.flag(f"mid_ready{i}", 1)
            s["low_ready"] = m.flag(f"low_ready{i}", 1)
            s["stored"] = m.flag(f"stored{i}", 16 * PARTS)
        if v:
            Wv = m.sb("Wv", [P, P])
            bv = m.sb("bv", [P, P])
            bvc = m.sb("bvc", [P, 1])
            psV = m.ps("psV", [P, NT, P])
            vraw = m.sb("vraw", [P, T]) if v["mix"] else None
            v_projected = m.flag("v_projected", 1)
            v_raw_ready = m.flag("v_raw_ready", 1)
            v_mixed = m.flag("v_mixed", 1)
            v_added = m.flag("v_added", 1)
            v_ready = m.flag("v_ready", 1)
        m.credit()
        xT, xT_users = load.xT, [s["projected"] for s in sides] + ([v_projected] if v else [])
        nload = 32 * len(sides) + (48 if v else 0)
        with nc.Block() as block:
            @block.sync
            def _(sp):
                for s in sides:
                    sp.dma_start(s["W"][:], s["w"]).then_inc(loaded, 16)
                    sp.dma_start(s["bias"][:], s["b"].rearrange("(p a) -> p a", a=1)).then_inc(loaded, 16)
                if v:
                    sp.dma_start(Wv[:], v["w"]).then_inc(loaded, 16)
                    row = v["b"].rearrange("(a n) -> a n", a=1)
                    sp.dma_start(bv[:], row.broadcast_to([P, P])).then_inc(loaded, 16)
                    sp.dma_start(bvc[:], v["b"].rearrange("(p a) -> p a", a=1)).then_inc(loaded, 16)
                with turns(sp, n) as b:
                    for s in sides:
                        s["high_ready"].wait(sp, b)
                        s["mid_ready"].wait(sp, b)
                        s["low_ready"].wait(sp, b)
                        for j in range(PARTS):
                            dst = s["parts"][bass.ds(b, 1), j, :, :, :].rearrange("a d h n -> h (a d) n")
                            sp.dma_start(dst, s["bf"][:, j, :]).then_inc(s["stored"].sem, 16)
                for s in sides:
                    s["stored"].wait(sp, n - 1)

            @block.scalar
            def _(act):
                act.wait_ge(loaded, nload)
                act.wait_ge(prepared, max(len(sides), 1))
                with turns(act, n) as b:
                    load.scalar(act, b)
                    if v and v["mix"] is not None:
                        v_projected.wait(act, b)
                        v_mixed.wait(act, b - 1)
                        act.activation(vraw[:], psV[:].rearrange("p t d -> p (t d)"), ACT.Identity,
                                       bias=bvc[:, 0:1]).then_inc(v_raw_ready.sem, 1)
                    for s in sides:
                        if s["mix"] is not None:
                            s["projected"].wait(act, b)
                            s["mixed"].wait(act, b - 1)
                            act.activation(s["raw"][:], s["ps"][:], ACT.Identity,
                                           bias=s["bias"][:, 0:1]).then_inc(s["raw_ready"].sem, 1)
                            s["mixed"].wait(act, b)
                            kw = dict(scale=s["scale"])
                        else:
                            s["projected"].wait(act, b)
                            kw = dict(scale=s["scale"], bias=s["sbias"][:, 0:1])
                        s["rest_ready"].wait(act, b - 1)
                        act.activation(s["full"][:], s["ps"][:], s["func"], **kw).then_inc(s["full_ready"].sem, 1)
                        s["stored"].wait(act, b - 1)
                        act.activation(s["bf"][:, 0, :], s["ps"][:], s["func"], **kw).then_inc(s["high_ready"].sem, 1)

            @block.gpsimd
            def _(pool):
                with turns(pool, n) as b:
                    load.pool(pool, b)
                    for s in sides:
                        s["mid_ready"].wait(pool, b)
                        s["stored"].wait(pool, b - 1)
                        pool.tensor_tensor(s["bf"][:, 2, :], s["rest"][:], s["bf"][:, 1, :],
                                           ALU.subtract).then_inc(s["low_ready"].sem, 1)

            @block.tensor
            def _(pe):
                pe.wait_ge(loaded, nload)
                with turns(pe, n) as b:
                    load.tensor(pe, b)
                    load.xT_ready.wait(pe, b)
                    for s in sides:
                        s["high_ready"].wait(pe, b - 1)
                        pe.matmul(s["ps"][:], s["W"][:], xT[:], start=True, stop=True)\
                          .then_inc(s["projected"].sem, 1)
                    if v:
                        v_added.wait(pe, b - 1)
                        if v["mix"] is None:
                            for t in range(NT):
                                last = pe.matmul(psV[:, t, :], xT[:, t * P:(t + 1) * P], Wv[:],
                                                 start=True, stop=True)
                            last.then_inc(v_projected.sem, 1)
                        else:
                            pe.matmul(psV[:].rearrange("p t d -> p (t d)"), Wv[:], xT[:], start=True, stop=True)\
                              .then_inc(v_projected.sem, 1)
                            v_raw_ready.wait(pe, b)
                            for t in range(NT):
                                last = pe.matmul(psV[:, t, :], vraw[:, t * P:(t + 1) * P], v["mix"][:],
                                                 start=True, stop=True)
                            last.then_inc(v_mixed.sem, 1)
                    for s in sides:
                        if s["mix"] is not None:
                            s["raw_ready"].wait(pe, b)
                            pe.matmul(s["ps"][:], s["mix"][:], s["raw"][:], start=True, stop=True)\
                              .then_inc(s["mixed"].sem, 1)

            @block.vector
            def _(dve):
                dve.wait_ge(loaded, nload)
                for s in sides:
                    dve.tensor_scalar(s["sbias"][:], s["bias"][:], s["scale"], None, ALU.mult)\
                       .then_inc(prepared, 1)
                if not sides:
                    dve.sem_inc(prepared, 1)
                with turns(dve, n) as b:
                    load.vector(dve, b, xT_users)
                    if v:
                        (v_projected if v["mix"] is None else v_mixed).wait(dve, b)
                        out = batch(v["out"], b)
                        if v["mix"] is None:
                            dve.tensor_tensor(out, psV[:], bv[:].unsqueeze(1).broadcast_to([P, NT, P]), ALU.add)\
                               .then_inc(v_added.sem, 1)
                        else:
                            dve.tensor_copy(out, psV[:]).then_inc(v_added.sem, 1)
                        if v["relu"]:
                            v_added.wait(dve, b)
                            dve.tensor_scalar(out, out, 0.0, None, ALU.max).then_inc(v_ready.sem, 1)
                    for s in sides:
                        s["full_ready"].wait(dve, b)
                        s["high_ready"].wait(dve, b)
                        s["low_ready"].wait(dve, b - 1)
                        dve.tensor_tensor(s["rest"][:], s["full"][:], s["bf"][:, 0, :], ALU.subtract)\
                           .then_inc(s["rest_ready"].sem, 1)
                        s["rest_ready"].wait(dve, b)
                        s["stored"].wait(dve, b - 1)
                        dve.tensor_copy(s["bf"][:, 1, :], s["rest"][:]).then_inc(s["mid_ready"].sem, 1)


class Stacked:

    def __init__(self, m, name, copies):
        self.tiles = [m.sb(f"{name}{i}", [P, H, T], BF16) for i in range(copies)]


def stack_rows(parts, b, query, j):
    if query:
        return [(DECAY_ROWS + 24 * j + HD * i, parts[b, j, :, :, :]) for i in range(PARTS)]
    return [(DECAY_ROWS + 24 * j + HD * i, parts[b, i, :, :, :]) for i in range(PARTS)]


def attend(nc, G, tag, a, qparts, kparts, Vc, O, causal, shared_keys):
    units = NT
    with ExitStack() as ctx:
        m = Stage(nc, ctx, tag)
        KC = 1 if shared_keys else 2
        QS = Stacked(m, "QS", 2).tiles
        KS = Stacked(m, "KS", KC).tiles
        VA = [m.sb(f"VA{i}", [P, NT, H, 32]) for i in range(KC)]
        PT = [m.sb(f"PT{i}", [P, GH, T]) for i in range(2)]
        negmax = [m.sb(f"negmax{i}", [P, GH, NT]) for i in range(2)]
        mrest = m.sb("mrest", [NT * GH, P])
        mparts = m.sb("mparts", [NT * GH, PARTS, P], BF16)
        Osb = m.sb("Osb", [P, T])
        rden = m.sb("rden", [P, NT, GH, 1])
        masks = m.sb("masks", [P, 2, P], BF16)
        psA = [m.ps(f"psA{i}", [P, T]) for i in range(2)]
        psB = [m.ps(f"psB{i}", [P, 2, T]) for i in range(2)]
        psO = m.ps("psO", [P, T])
        psT = m.ps("psT", [P, T])

        queries_in = m.flag("queries_in", 16 * PARTS * PARTS)
        keys_in = m.flag("keys_in", 16 * PARTS * PARTS)
        values_in = m.flag("values_in", 1)
        row_scores = m.flag("row_scores", 16)
        maxed = m.flag("maxed", 16)
        max_turned = m.flag("max_turned", 1)
        max_split = m.flag("max_split", 4)
        max_in = m.flag("max_in", 16 * PARTS)
        col_scores = m.flag("col_scores", 8)
        exped = m.flag("exped", 8)
        weighted = m.flag("weighted", 4, lead=5)
        out_copied = m.flag("out_copied", 1)
        out_turned = m.flag("out_turned", 1, first=-1)
        out_scaled = m.flag("out_scaled", 2, lead=3, first=-1)
        constant = m.sem("constant")
        cleared = m.sem("cleared")
        m.credit()

        def tokens(t):
            return slice(t * P, (t + 1) * P)

        with nc.Block() as block:
            @block.gpsimd
            def _(pool):
                for tile in QS + KS:
                    pool.memset(tile[:], 0.0)
                for tile in VA:
                    pool.memset(tile[:], 0.0)
                pool.memset(Osb[:], 1.0).then_inc(cleared, 1)

            @block.sync
            def _(sp):
                sp.wait_ge(cleared, 1)
                if causal:
                    for tile in QS:
                        sp.dma_start(tile[0:DECAY_ROWS, :, :], a["c_qdecay"]).then_inc(constant, 16)
                    for tile in KS:
                        sp.dma_start(tile[0:DECAY_ROWS, :, :], a["c_kdecay"]).then_inc(constant, 16)
                    sp.dma_start(masks[:], a["c_masks"]).then_inc(constant, 16)
                    sp.wait_ge(constant, 16 * (2 + KC + 1))

            @block.vector
            def _(dve):
                dve.wait_ge(cleared, 1)
                for tile in KS:
                    dve.memset(tile[MAX_ROW:MAX_ROW + PARTS, :, :], 1.0)
                for tile in VA:
                    dve.memset(tile[:, :, :, HD:HD + 1], 1.0)

        def slots(body):
            def walk(engine):
                with engine.Fori(0, B - 2, 2) as b:
                    for i in range(2):
                        body(engine, b + i, i, False, False)
                for i in range(2):
                    body(engine, B - 2 + i, i, i == 1, i == 1)
            return walk

        with nc.Block() as block:
            @block.sync
            def _(sp):
                def load(b, i, first=False):
                    if not first:
                        col_scores.wait(sp, 4 * (b - 2) + 3)
                    for j in range(PARTS):
                        for row, src in stack_rows(qparts, b, True, j):
                            sp.dma_start(QS[i][row:row + HD, :, :], src).then_inc(queries_in.sem, 16)
                        if not shared_keys:
                            for row, src in stack_rows(kparts, b, False, j):
                                sp.dma_start(KS[i][row:row + HD, :, :], src).then_inc(keys_in.sem, 16)

                if shared_keys:
                    for j in range(PARTS):
                        for row, src in stack_rows(kparts, 0, False, j):
                            sp.dma_start(KS[0][row:row + HD, :, :], src).then_inc(keys_in.sem, 16)
                load(0, 0, True)

                def max_rows(b, i, g):
                    max_split.wait(sp, 4 * b + g)
                    for j in range(PARTS):
                        dst = QS[i][MAX_ROW + j:MAX_ROW + j + 1, GH * g:GH * g + GH, :]
                        sp.dma_start(dst, mparts[:, j, :]).then_inc(max_in.sem, 16)

                def body(sp, b, i, last, _):
                    max_rows(b, i, 0)
                    if not last:
                        load(b + 1, (i + 1) % 2)
                    for g in range(1, NG):
                        max_rows(b, i, g)
                slots(body)(sp)

            @block.gpsimd
            def _(pool):
                if shared_keys:
                    src = Vc[:, 0, :, :].rearrange("p t (h d) -> p t h d", d=HD)
                    pool.tensor_copy(VA[0][:, :, :, 0:HD], src).then_inc(values_in.sem, 1)
                else:
                    def body(pool, b, i, last, _):
                        weighted.wait(pool, 4 * (b - 2) + 3)
                        src = Vc[:, bass.ds(b, 1), :, :].rearrange("p a t (h d) -> p (a t) h d", d=HD)
                        pool.tensor_copy(VA[i][:, :, :, 0:HD], src).then_inc(values_in.sem, 1)
                    slots(body)(pool)

            @block.tensor
            def _(pe):
                def rows(G4, b, i, g, it):
                    N = (it + 1) * P if causal else T
                    for hh in range(GH):
                        n, h = it * GH + hh, GH * g + hh
                        maxed.wait(pe, G4, n - 1)
                        out = psA[n % 2]
                        mm = pe.matmul(out[:, 0:N], QS[i][0:MAX_ROW, h, tokens(it)],
                                       KS[i % KC][0:MAX_ROW, h, 0:N], start=True, stop=not causal,
                                       skip_group_check=causal)
                        if causal:
                            mm = pe.matmul(out[:, tokens(it)], G.identb[:], masks[:, 0, :], start=False,
                                           stop=True, skip_group_check=True)
                        mm.then_inc(row_scores.sem, 1)

                def turn_max(G4, i):
                    maxed.wait(pe, G4)
                    out_scaled.wait(pe, G4 - 3)
                    pe.transpose(psT[0:NT * GH, 0:P], negmax[i][:].rearrange("p h t -> p (h t)"), G.ident[:])\
                      .then_inc(max_turned.sem, 1)

                def columns(G4, i, g, jt):
                    lo = jt * P if causal else 0
                    N = T - lo
                    for pair in range(2):
                        n = 2 * jt + pair
                        exped.wait(pe, G4, n - 1)
                        for k in range(2):
                            h = GH * g + 2 * pair + k
                            mm = pe.matmul(psB[pair][:, k, 0:N], KS[i % KC][:, h, tokens(jt)],
                                           QS[i][:, h, lo:T], start=True, stop=not causal,
                                           skip_group_check=causal)
                            if causal:
                                mm = pe.matmul(psB[pair][:, k, 0:P], G.identb[:], masks[:, 1, :], start=False,
                                               stop=True, skip_group_check=True)
                        mm.then_inc(col_scores.sem, 1)

                def weigh(G4, i, g, jt):
                    lo = jt * P if causal else 0
                    N = T - lo
                    if jt == 0:
                        out_copied.wait(pe, G4 - 1)
                    exped.wait(pe, G4, 2 * jt + 2)
                    for hh in range(GH):
                        mm = pe.matmul(psO[32 * hh:32 * hh + 32, lo:T], VA[i % KC][:, jt, GH * g + hh, :],
                                       PT[jt % 2][:, hh, 0:N], start=(jt == 0), stop=(jt == NT - 1),
                                       tile_position=(0, 32 * hh), skip_group_check=True)
                    mm.then_inc(weighted.sem, 1)

                def turn_out(G4):
                    out_copied.wait(pe, G4)
                    max_split.wait(pe, G4 + 2)
                    for t in range(NT):
                        mm = pe.transpose(psT[:, tokens(t)], Osb[:, tokens(t)], G.ident[:])
                    mm.then_inc(out_turned.sem, 1)

                def operands(b):
                    queries_in.wait(pe, b)
                    if not shared_keys:
                        keys_in.wait(pe, b)

                if shared_keys:
                    keys_in.wait(pe, 0)
                    values_in.wait(pe, 0)
                operands(0)
                for g in range(2):
                    for it in range(units):
                        rows(g, 0, 0, g, it)
                    if g == 0:
                        turn_max(0, 0)

                def body(pe, b, i, last, _):
                    for g in range(NG):
                        G4 = 4 * b + g
                        ahead = not (last and g >= 2)
                        ai, ag = (i, g + 2) if g < 2 else ((i + 1) % 2, g - 2)
                        if g == 2 and ahead:
                            operands(b + 1)
                        if g == 0 and not shared_keys:
                            values_in.wait(pe, b)
                        max_in.wait(pe, G4)
                        for u in range(units):
                            columns(G4, i, g, u)
                            if ahead:
                                rows(G4 + 2, None, ai, ag, u)
                            if u == 1 and not (last and g == 3):
                                turn_max(G4 + 1, (g + 1) % 2)
                            if u == 2:
                                turn_out(G4 - 1) if not (last and g == 3) else turn_out_last(G4 - 1)
                            weigh(G4, i, g, u)
                    if last:
                        turn_out_last(4 * b + 3)

                def turn_out_last(G4):
                    out_copied.wait(pe, G4)
                    out_scaled.wait(pe, G4 - 1)
                    for t in range(NT):
                        mm = pe.transpose(psT[:, tokens(t)], Osb[:, tokens(t)], G.ident[:])
                    mm.then_inc(out_turned.sem, 1)
                slots(body)(pe)

            @block.scalar
            def _(act):
                def body(act, b, i, last, _):
                    for g in range(NG):
                        G4 = 4 * b + g
                        for u in range(units):
                            N = T - u * P if causal else T
                            weighted.wait(act, G4, u - 1)
                            for pair in range(2):
                                col_scores.wait(act, G4, 2 * u + pair + 1)
                                act.activation(PT[u % 2][:, 2 * pair:2 * pair + 2, 0:N], psB[pair][:, :, 0:N],
                                               ACT.Exp).then_inc(exped.sem, 1)
                        weighted.wait(act, G4)
                        out_turned.wait(act, G4 - 1)
                        act.activation(Osb[:], psO[:], ACT.Copy).then_inc(out_copied.sem, 1)
                slots(body)(act)

            @block.vector
            def _(dve):
                def maxima(G4, i, it):
                    N = (it + 1) * P if causal else T
                    for hh in range(GH):
                        n = it * GH + hh
                        row_scores.wait(dve, G4, n + 1)
                        if n == 0:
                            max_turned.wait(dve, G4 - 2) if not isinstance(G4, int) or G4 >= 2 else None
                        dve.tensor_reduce(negmax[i][:, hh, it:it + 1], psA[n % 2][:, 0:N], AX.X, ALU.max,
                                          negate=True).then_inc(maxed.sem, 1)

                def split_max(G4):
                    c = Chain(max_split, dve, G4)
                    max_turned.wait(dve, G4)
                    max_in.wait(dve, G4 - 1)
                    rows16 = psT[0:NT * GH, 0:P]
                    c.step(dve.tensor_copy(mparts[:, 0, :], rows16))
                    c.wait()
                    c.step(dve.tensor_tensor(mrest[:], rows16, mparts[:, 0, :], ALU.subtract))
                    c.wait()
                    c.step(dve.tensor_copy(mparts[:, 1, :], mrest[:]))
                    c.wait()
                    c.step(dve.tensor_tensor(mparts[:, 2, :], mrest[:], mparts[:, 1, :], ALU.subtract))
                    c.end()

                def scale_out(b, g, G4):
                    c = Chain(out_scaled, dve, G4)
                    out_turned.wait(dve, G4)
                    turned = psT[:].rearrange("p (t h c) -> p t h c", t=NT, h=GH)
                    c.step(dve.reciprocal(rden[:], turned[:, :, :, HD:HD + 1]))
                    c.wait()
                    dst = O[:, bass.ds(b + 1, 1), :, GH * HD * g:GH * HD * (g + 1)]\
                        .rearrange("p a t (h d) -> p (a t) h d", d=HD)
                    c.step(dve.tensor_tensor(dst, turned[:, :, :, 0:HD], rden[:].broadcast_to([P, NT, GH, HD]),
                                             ALU.mult))
                    c.end()

                for g in range(2):
                    for it in range(units):
                        maxima(g, g, it)
                    if g == 0:
                        split_max(0)

                def body(dve, b, i, last, _):
                    for g in range(NG):
                        G4 = 4 * b + g
                        for u in range(units):
                            if not (last and g >= 2):
                                maxima(G4 + 2, g % 2, u)
                            if u == 1 and not (last and g == 3):
                                split_max(G4 + 1)
                            if u == 2:
                                scale_out(b if g else b - 1, (g - 1) % NG, G4 - 1)
                    if last:
                        scale_out(b, 3, 4 * b + 3)
                slots(body)(dve)


def attention_output(nc, G, tag, a, O, w, bias):
    with ExitStack() as ctx:
        m = Stage(nc, ctx, tag)
        post = Post(m, G)
        os_ = m.sb("os", [P, NT, P])
        oT = m.sb("oT", [P, T])
        base = m.sb("base", [P, NT, P])
        psT = m.ps("psT", [P, T])
        psY = m.ps("psY", [P, NT, P])
        copied = m.flag("copied", 1)
        turned = m.flag("turned", 1)
        oT_ready = m.flag("oT_ready", 1)
        projected = m.flag("projected", 1)
        base_ready = m.flag("base_ready", 1)
        loaded, finished = m.sem("loaded"), m.sem("finished")
        m.credit()
        if w is not None:
            W = m.sb("W", [P, P])
            bo = m.sb("bo", [P, P])
        with nc.Block() as block:
            if w is not None:
                @block.sync
                def _(sp):
                    sp.dma_start(W[:], w).then_inc(loaded, 16)
                    sp.dma_start(bo[:], bias.rearrange("(a n) -> a n", a=1).broadcast_to([P, P])).then_inc(loaded, 16)
                    sp.wait_ge(loaded, 32)

            @block.gpsimd
            def _(pool):
                if w is not None:
                    pool.wait_ge(loaded, 32)
                with turns(pool, B) as b:
                    post.summed.wait(pool, b - 1)
                    x = batch(G.X, b)
                    if w is not None:
                        pool.tensor_tensor(base[:], x, bo[:].unsqueeze(1).broadcast_to([P, NT, P]), ALU.add)\
                            .then_inc(base_ready.sem, 1)
                    else:
                        pool.tensor_tensor(base[:], x, x, ALU.add).then_inc(base_ready.sem, 1)
                post.finish(pool, finished)

            @block.scalar
            def _(act):
                with turns(act, B) as b:
                    turned.wait(act, b - 1)
                    act.activation(os_[:], batch(O, b + 1), ACT.Copy).then_inc(copied.sem, 1)
                    if w is not None:
                        turned.wait(act, b)
                        projected.wait(act, b - 1)
                        act.activation(oT[:], psT[:], ACT.Copy).then_inc(oT_ready.sem, 1)

            @block.tensor
            def _(pe):
                if w is not None:
                    pe.wait_ge(loaded, 32)
                with turns(pe, B) as b:
                    copied.wait(pe, b)
                    if w is not None:
                        oT_ready.wait(pe, b - 1)
                    else:
                        post.summed.wait(pe, b - 1)
                    for t in range(NT):
                        last = pe.transpose(psT[:, t * P:(t + 1) * P], os_[:, t, :], G.ident[:])
                    last.then_inc(turned.sem, 1)
                    if w is not None:
                        oT_ready.wait(pe, b)
                        post.summed.wait(pe, b - 1)
                        for t in range(NT):
                            last = pe.matmul(psY[:, t, :], oT[:, t:T:NT], W[:], start=True, stop=True)
                        last.then_inc(projected.sem, 1)

            @block.vector
            def _(dve):
                with turns(dve, B) as b:
                    base_ready.wait(dve, b)
                    x = batch(G.X, b)
                    if w is not None:
                        projected.wait(dve, b)
                        dve.tensor_tensor(x, psY[:], base[:], ALU.add).then_inc(post.summed.sem, 1)
                    else:
                        turned.wait(dve, b)
                        dve.tensor_tensor(x, psT[:].rearrange("p (t c) -> p t c", t=NT), base[:], ALU.add)\
                           .then_inc(post.summed.sem, 1)
                    post.vector(dve, b, x)


def attention_stage(nc, G, tag, a, kind):
    scale = float(np.float32(1.0) / np.sqrt(np.float32(HD)))
    with ExitStack() as ctx:
        m = Stage(nc, ctx, tag)
        one = kind == "cross"
        O = m.sb("O", [P, B + 1, NT, P])
        Vc = m.sb("Vc", [P, 1 if one else B, NT, P])
        qparts = nc.dram_tensor(f"{tag}_qparts", [B, PARTS, HD, H, T], BF16, kind="Internal").ap()
        kparts = nc.dram_tensor(f"{tag}_kparts", [1 if one else B, PARTS, HD, H, T], BF16, kind="Internal").ap()
        if kind == "decay":
            q = dict(w=a["L0_attn_Wq"], b=a["L0_attn_bq"], scale=scale, func=ACT.Identity, mix=None, parts=qparts)
            k = dict(w=a["L0_attn_Wk"], b=a["L0_attn_bk"], scale=1.0, func=ACT.Identity, mix=None, parts=kparts)
            v = dict(w=a["L0_attn_Wv"], b=a["L0_attn_bv"], relu=False, mix=None, out=Vc)
            project(nc, G, tag + "p", G.X, B, q, k, v)
            attend(nc, G, tag + "a", a, qparts, kparts, Vc, O, True, False)
            attention_output(nc, G, tag + "o", a, O, a["L0_attn_Wo"], a["L0_attn_bo"])
        elif kind == "cross":
            q = dict(w=a["L2_attn_Wq_w"], b=a["L2_attn_Wq_b"], scale=scale, func=ACT.Relu, mix=None, parts=qparts)
            k = dict(w=a["L2_attn_Wk_w"], b=a["L2_attn_Wk_b"], scale=1.0, func=ACT.Relu, mix=None, parts=kparts)
            v = dict(w=a["L2_attn_Wv_w"], b=a["L2_attn_Wv_b"], relu=True, mix=None, out=Vc)
            KV = m.sb("KV", [P, 2, NT, P])
            kv_in = m.sem("kv_in")
            ctx.callback(m.retire)
            with nc.Block() as block:
                @block.sync
                def _(sp):
                    for i, name in enumerate(("L2_attn_keys", "L2_attn_values")):
                        sp.dma_start(KV[:, i, :, :], a[name].rearrange("a (p t) d -> p (a t) d", t=NT))\
                          .then_inc(kv_in, 16)
                    sp.wait_ge(kv_in, 32)
            project(nc, G, tag + "k", KV[:, 0:1, :, :], 1, k=k, normalised=False)
            project(nc, G, tag + "v", KV[:, 1:2, :, :], 1, v=v, normalised=False)
            project(nc, G, tag + "p", G.X, B, q=q)
            attend(nc, G, tag + "a", a, qparts, kparts, Vc, O, False, True)
            attention_output(nc, G, tag + "o", a, O, None, None)
        else:
            mixes = lora(nc, G, m, a)
            ctx.callback(m.retire)
            q = dict(w=a["L3_wq"], b=a["L3_bq"], scale=scale, func=ACT.Identity, mix=mixes[0], parts=qparts)
            k = dict(w=a["L3_wk"], b=a["L3_bk"], scale=1.0, func=ACT.Identity, mix=None, parts=kparts)
            v = dict(w=a["L3_wv"], b=a["L3_bv"], relu=False, mix=mixes[1], out=Vc)
            project(nc, G, tag + "p", G.X, B, q, k, v)
            attend(nc, G, tag + "a", a, qparts, kparts, Vc, O, False, False)
            attention_output(nc, G, tag + "o", a, O, a["L3_attn_w_proj"], a["L3_attn_b_proj"])


def lora(nc, G, m, a):
    LORA_SCALE = 2.0
    R = 16
    A = [m.sb(f"A{i}", [R, P]) for i in range(2)]
    Bm = [m.sb(f"B{i}", [R, P]) for i in range(2)]
    blocks = m.sb("blocks", [P, P])
    out = [m.sb(f"mix{i}", [P, P]) for i in range(2)]
    loaded, made, masked, added = m.sem("l_in"), m.sem("l_mm"), m.sem("l_mask"), m.sem("l_add")
    with ExitStack() as ctx:
        ps = [ctx.enter_context(nc.psum_tensor(f"{m.tag}_psL{i}", [P, T], F32)) for i in range(2)]
        with nc.Block() as block:
            @block.sync
            def _(sp):
                sp.dma_start(blocks[:], a["c_blocks"]).then_inc(loaded, 16)
                for i, side in enumerate("qv"):
                    sp.dma_start(A[i][:].rearrange("r (h d) -> r h d", h=H),
                                 a[f"L3_a{side}T"].unsqueeze(1).broadcast_to([R, H, HD])).then_inc(loaded, 16)
                    sp.dma_start(Bm[i][:].rearrange("r (h d) -> r h d", h=H),
                                 a[f"L3_attn_b_{side}"].unsqueeze(1).broadcast_to([R, H, HD])).then_inc(loaded, 16)
                sp.wait_ge(loaded, 80)

            @block.tensor
            def _(pe):
                pe.wait_ge(loaded, 80)
                for i in range(2):
                    pe.matmul(ps[i][:, 0:P], A[i][:], Bm[i][:], start=True, stop=True).then_inc(made, 1)

            @block.vector
            def _(dve):
                dve.wait_ge(loaded, 80)
                for i in range(2):
                    dve.wait_ge(made, i + 1)
                    dve.scalar_tensor_tensor(out=out[i][:], in0=ps[i][:, 0:P], scalar=LORA_SCALE, in1=blocks[:],
                                             op0=ALU.mult, op1=ALU.mult).then_inc(masked, 1)
                    dve.wait_ge(masked, i + 1)
                    dve.tensor_tensor(out[i][:], out[i][:], G.ident[:], ALU.add).then_inc(added, 1)
    return out



def expert_stage(nc, G, tag, a, gated):
    E = 12
    if gated:
        C, FF, temperature = 3, 3 * P, 1.5
        order = [(E, 2)] + [(e, C) for e in range(E)]
    else:
        C, FF, temperature = 2, 2 * P, 1.0
        order = [(e, C) for e in range(8)]
    chunks = [(x, c) for x, (_, n) in enumerate(order) for c in range(n)]
    NCH, NX = len(chunks), len(order)
    first_chunk = [sum(n for _, n in order[:x]) for x in range(NX + 1)]
    with ExitStack() as ctx:
        m = Stage(nc, ctx, tag)
        load, post = Load(m, G, G.X), Post(m, G)
        NE = 12 if gated else 8
        W1 = m.sb("W1", [P, NE, (2 if gated else 1) * FF])
        W2 = m.sb("W2", [P, NE, C, P])
        Wr = m.sb("Wr", [P, E])
        br = m.sb("br", [P, E])
        iota = m.sb("iota", [P, E])
        if gated:
            Ws1, Ws2 = m.sb("Ws1", [P, 4 * P]), m.sb("Ws2", [P, 2, P])
            b1, bs1 = m.sb("b1", [P, NE, 2 * C]), m.sb("bs1", [P, 4])
            b2 = m.sb("b2", [E + 1, P])
            gate = [m.sb(f"gate{i}", [P, T]) for i in range(2)]
            wT = m.sb("wT", [E + 1, NT, P])
        act_ = [m.sb(f"act{i}", [P, C, T]) for i in range(2)]
        acc = m.sb("acc", [P, NT, P])
        logits = m.sb("logits", [P, NT, E])
        top = m.sb("top", [P, NT, 8])
        index = m.sb("index", [P, NT, 8], U32)
        indexf = m.sb("indexf", [P, NT, 2])
        margin = m.sb("margin", [P, NT])
        th = m.sb("th", [P, NT, 1])
        share = m.sb("share", [P, 2, NT])
        hit = m.sb("hit", [P, 2, NT, E])
        w = m.sb("w", [P, NT, E + 1])
        through = m.sb("through", [P, NT])
        psa = [m.ps(f"psa{i}", [P, T]) for i in range(2)]
        psg = [m.ps(f"psg{i}", [P, T]) for i in range(2)]
        psY = [m.ps(f"psY{i}", [P, NT, P]) for i in range(2)]
        psR = m.ps("psR", [P, T])
        hidden = m.flag("hidden", NCH)
        gelued = m.flag("gelued", NCH)
        activated = m.flag("activated", NCH)
        yielded = m.flag("yielded", NX)
        added = m.flag("added", NX + 2)
        scored = m.flag("scored", 1)
        ranked = m.flag("ranked", 5)
        tanhed = m.flag("tanhed", 1)
        routed = m.flag("routed", 4 if gated else 6)
        turned_w = m.flag("turned_w", 1)
        copied_w = m.flag("copied_w", 1)
        biased = m.flag("biased", 1)
        small_in, ones, finished = m.sem("small_in"), m.sem("ones"), m.sem("finished")
        expert_in = [m.sem(f"expert_in{x}") for x in range(NX)]
        m.credit()
        nsmall = 16 * (6 if gated else 3)
        prefix = "L0_ffn" if gated else "L2_ffn"
        with nc.Block() as block:
            @block.sync
            def _(sp):
                rows = lambda v: v.rearrange("(a n) -> a n", a=1).broadcast_to([P, E])
                if gated:
                    sp.dma_start(Wr[:], a["L0_ffn_Wr"]).then_inc(small_in, 16)
                    sp.dma_start(br[:], rows(a["L0_ffn_br"])).then_inc(small_in, 16)
                    sp.dma_start(b1[:], a["L0_be1"]).then_inc(small_in, 16)
                    sp.dma_start(bs1[:], a["L0_bs1"]).then_inc(small_in, 16)
                    sp.dma_start(b2[:], a["L0_b2"]).then_inc(small_in, 16)
                else:
                    sp.dma_start(Wr[:], a["L2_ffn_gate_w"]).then_inc(small_in, 16)
                    sp.dma_start(br[:], rows(a["L2_ffn_expert_bias"])).then_inc(small_in, 16)
                sp.dma_start(iota[:], a["c_iota"]).then_inc(small_in, 16)
                for x, (e, n) in enumerate(order):
                    if e == E:
                        sp.dma_start(Ws1[:], a["L0_ffn_Ws1"]).then_inc(expert_in[x], 16)
                        sp.dma_start(Ws2[:], a["L0_ffn_Ws2"].rearrange("(c f) d -> f c d", f=P))\
                          .then_inc(expert_in[x], 16)
                    else:
                        w1, w2 = (a["L0_ffn_We1"], a["L0_ffn_We2"]) if gated else (a["L2_ffn_w1"], a["L2_ffn_w2"])
                        sp.dma_start(W1[:, e, :], w1[e, :, :]).then_inc(expert_in[x], 16)
                        sp.dma_start(W2[:, e, :, :], w2[e, :, :].rearrange("(c f) d -> f c d", f=P))\
                          .then_inc(expert_in[x], 16)
                for s in expert_in:
                    sp.wait_ge(s, 32)

            @block.scalar
            def _(act):
                act.wait_ge(small_in, nsmall)
                with turns(act, B) as b:
                    load.scalar(act, b)
                    for n, (x, c) in enumerate(chunks):
                        e, C_ = order[x]
                        hidden.wait(act, b, n + 1)
                        if gated:
                            activated.wait(act, b, n - 1)
                            bias = bs1[:, 2 + c:3 + c] if e == E else b1[:, e, C + c:C + c + 1]
                            act.activation(gate[n % 2][:], psg[n % 2][:], ACT.Gelu, bias=bias)\
                               .then_inc(gelued.sem, 1)
                        else:
                            yielded.wait(act, b, max(x - 1, 0))
                            ps = (psa + psg)[n % 4]
                            act.activation(act_[x % 2][:, c, :], ps[:], ACT.Silu).then_inc(activated.sem, 1)
                        if n == 3:
                            ranked.wait(act, b)
                            act.activation(th[:, :, 0], margin[:], ACT.Tanh, scale=0.5 / temperature)\
                               .then_inc(tanhed.sem, 1)

            @block.gpsimd
            def _(pool):
                pool.memset(w[:], 1.0).then_inc(ones, 1)
                with turns(pool, B) as b:
                    load.pool(pool, b)
                post.finish(pool, finished)

            @block.tensor
            def _(pe):
                pe.wait_ge(small_in, nsmall)

                def hidden_of(b, x):
                    e, C_ = order[x]
                    pe.wait_ge(expert_in[x], 32)
                    for c in range(C_):
                        n = first_chunk[x] + c
                        w1 = Ws1[:, :] if e == E else W1[:, e, :]
                        if gated:
                            activated.wait(pe, b, n - 1)
                            pe.matmul(psa[n % 2][:], w1[:, c * P:(c + 1) * P], load.xT[:], start=True, stop=True)
                            pe.matmul(psg[n % 2][:], w1[:, (C_ + c) * P:(C_ + c + 1) * P], load.xT[:],
                                      start=True, stop=True).then_inc(hidden.sem, 1)
                        else:
                            activated.wait(pe, b, n - 3)
                            pe.matmul((psa + psg)[n % 4][:], w1[:, c * P:(c + 1) * P], load.xT[:],
                                      start=True, stop=True).then_inc(hidden.sem, 1)

                def output_of(b, x):
                    e, C_ = order[x]
                    activated.wait(pe, b, first_chunk[x + 1])
                    added.wait(pe, b, max(x - 1, 0))
                    for t in range(NT):
                        for c in range(C_):
                            w2 = Ws2[:, c, :] if e == E else W2[:, e, c, :]
                            mm = pe.matmul(psY[x % 2][:, t, :], act_[x % 2][:, c, t:T:NT], w2,
                                           start=(c == 0), stop=(c == C_ - 1))
                    mm.then_inc(yielded.sem, 1)

                with turns(pe, B) as b:
                    load.tensor(pe, b)
                    load.xT_ready.wait(pe, b)
                    added.wait(pe, b - 1)
                    for t in range(NT):
                        mm = pe.matmul(psR[:, t * E:(t + 1) * E], load.xT[:, t:T:NT], Wr[:], start=True, stop=True)
                    mm.then_inc(scored.sem, 1)
                    for x in range(NX):
                        hidden_of(b, x)
                        if x:
                            output_of(b, x - 1)
                        if x == 3 and gated:
                            routed.wait(pe, b)
                            for t in range(NT):
                                mm = pe.transpose(psR[0:E + 1, t * P:(t + 1) * P], w[:, t, :], G.ident[:])
                            mm.then_inc(turned_w.sem, 1)
                        if x == 5 and gated:
                            copied_w.wait(pe, b)
                            for t in range(NT):
                                mm = pe.matmul(psR[:, t * P:(t + 1) * P], wT[:, t, :], b2[:], start=True, stop=True)
                            mm.then_inc(biased.sem, 1)
                    output_of(b, NX - 1)

            @block.vector
            def _(dve):
                dve.wait_ge(small_in, nsmall)
                dve.wait_ge(ones, 1)

                def rank(b):
                    c = Chain(ranked, dve, b)
                    scored.wait(dve, b)
                    c.step(dve.tensor_tensor(logits[:], psR[:, 0:NT * E].rearrange("p (t e) -> p t e", t=NT),
                                             br[:].unsqueeze(1).broadcast_to([P, NT, E]), ALU.add))
                    c.wait()
                    stand(dve, post.passed)
                    for t in range(NT):
                        last = dve.max(top[:, t, :], logits[:, t, :])
                    c.step(last)
                    c.wait()
                    stand(dve, post.passed)
                    for t in range(NT):
                        last = dve.max_index(index[:, t, :], top[:, t, :], logits[:, t, :])
                    c.step(last)
                    tanhed.wait(dve, b - 1)
                    c.step(dve.tensor_tensor(margin[:], top[:, :, 0], top[:, :, 1], ALU.subtract))
                    c.wait()
                    c.step(dve.tensor_copy(indexf[:], index[:, :, 0:2]))
                    c.end()

                def route(b):
                    c = Chain(routed, dve, b)
                    tanhed.wait(dve, b)
                    ranked.wait(dve, b)
                    if gated:
                        turned_w.wait(dve, b - 1)
                    for i, half in enumerate((0.5, -0.5)):
                        dve.tensor_scalar(share[:, i, :], th[:, :, 0], half, 0.5, ALU.mult, ALU.add)
                    for i in range(2):
                        last = dve.tensor_tensor(hit[:, i, :, :], iota[:].unsqueeze(1).broadcast_to([P, NT, E]),
                                                 indexf[:, :, i:i + 1].broadcast_to([P, NT, E]), ALU.is_equal)
                    c.step(last)
                    c.wait()
                    for i in range(2):
                        c.step(dve.tensor_tensor(hit[:, i, :, :], hit[:, i, :, :],
                                                 share[:, i, :].unsqueeze(2).broadcast_to([P, NT, E]), ALU.mult))
                    c.wait()
                    c.step(dve.tensor_tensor(w[:, :, 0:E], hit[:, 0, :, :], hit[:, 1, :, :], ALU.add))
                    c.wait()
                    if not gated:
                        c.step(dve.tensor_reduce(through[:], w[:, :, 8:E], AX.X, ALU.add))
                        c.wait()
                        load.x_kept.wait(dve, b)
                        c.step(dve.tensor_tensor(acc[:], batch(G.X, b),
                                                 through[:].unsqueeze(2).broadcast_to([P, NT, P]), ALU.mult))
                        c.wait()
                    c.end()

                def add(b, x):
                    e, _ = order[x]
                    yielded.wait(dve, b, x + 1)
                    if x:
                        added.wait(dve, b, x)
                    for t in range(NT):
                        if e == E:
                            last = dve.tensor_copy(acc[:, t, :], psY[x % 2][:, t, :])
                        else:
                            last = dve.scalar_tensor_tensor(out=acc[:, t, :], in0=psY[x % 2][:, t, :],
                                                            scalar=w[:, t, e:e + 1], in1=acc[:, t, :],
                                                            op0=ALU.mult, op1=ALU.add)
                    last.then_inc(added.sem, 1)

                with turns(dve, B) as b:
                    load.vector(dve, b, [hidden, scored])
                    for x in range(NX):
                        e, C_ = order[x]
                        if gated:
                            for c in range(C_):
                                n = first_chunk[x] + c
                                hidden.wait(dve, b, n + 1)
                                gelued.wait(dve, b, n + 1)
                                yielded.wait(dve, b, max(x - 1, 0))
                                bias = bs1[:, c:c + 1] if e == E else b1[:, e, c:c + 1]
                                dve.scalar_tensor_tensor(out=act_[x % 2][:, c, :], in0=psa[n % 2][:], scalar=bias,
                                                         in1=gate[n % 2][:], op0=ALU.add, op1=ALU.mult)\
                                   .then_inc(activated.sem, 1)
                        if x == 0:
                            rank(b)
                        if x == 1:
                            route(b)
                        if x:
                            add(b, x - 1)
                        if x == 4 and gated:
                            turned_w.wait(dve, b)
                            biased.wait(dve, b - 1)
                            dve.tensor_copy(wT[:], psR[0:E + 1, :].rearrange("e (t p) -> e t p", t=NT))\
                               .then_inc(copied_w.sem, 1)
                    add(b, NX - 1)
                    added.wait(dve, b, NX)
                    if gated:
                        biased.wait(dve, b)
                        dve.tensor_tensor(acc[:], acc[:], psR[:].rearrange("p (t d) -> p t d", t=NT), ALU.add)\
                           .then_inc(added.sem, 1)
                    else:
                        dve.sem_inc(added.sem, 1)
                    load.x_kept.wait(dve, b)
                    added.wait(dve, b, NX + 1)
                    x_ = batch(G.X, b)
                    dve.tensor_tensor(x_, acc[:], x_, ALU.add).then_inc(post.summed.sem, 1)
                    post.summed.wait(dve, b)
                    dve.sem_inc(added.sem, 1)
                    post.vector(dve, b, x_)



def restat(nc, G, tag):
    with ExitStack() as ctx:
        m = Stage(nc, ctx, tag)
        post = Post(m, G)
        finished = m.sem("finished")
        m.credit()
        with nc.Block() as block:
            @block.scalar
            def _(act):
                with turns(act, B) as b:
                    x = batch(G.X, b)
                    for t in range(NT):
                        last = act.activation(x[:, t, :], x[:, t, :], ACT.Identity,
                                              scale=G.rstd[:, bass.ds(b, 1), t], bias=G.shift[:, bass.ds(b, 1), t])
                    last.then_inc(post.summed.sem, 1)

            @block.vector
            def _(dve):
                with turns(dve, B) as b:
                    post.vector(dve, b, batch(G.X, b))

            @block.gpsimd
            def _(pool):
                post.finish(pool, finished)


def linear_attention_stage(nc, G, tag, a):
    restat(nc, G, tag + "s")
    DH, PAIRS, W_ = 64, 8, 65
    EPS_DEN = 1e-6
    with ExitStack() as ctx:
        m = Stage(nc, ctx, tag)
        gain, offset = m.sb("gain", [P, 1]), m.sb("offset", [P, 1])
        load, post = Load(m, G, G.X, affine=(gain, offset)), Post(m, G)
        Wq, Wk, Wv = (m.sb(n, [P, PAIRS * P]) for n in ("Wq", "Wk", "Wv"))
        Wo = m.sb("Wo", [P, PAIRS, P])
        causal = m.sb("causal", [P, P])
        VA = m.sb("VA", [P, NT, H, W_])
        ex = [m.sb(f"ex{i}", [P, T]) for i in range(2)]
        re = [m.sb(f"re{i}", [P, T]) for i in range(2)]
        Q = [[m.sb(f"Q{i}{h}", [P, T]) for h in range(2)] for i in range(2)]
        K = [m.sb(f"K{i}", [P, T]) for i in range(2)]
        Kt = [m.sb(f"Kt{i}", [P, NT, P]) for i in range(2)]
        AT = [[m.sb(f"AT{i}{h}", [P, NT, P]) for h in range(2)] for i in range(2)]
        S = [m.sb(f"S{i}", [P, 3, 2 * W_]) for i in range(2)]
        den = [m.sb(f"den{i}", [P, 4, 1]) for i in range(2)]
        o = m.sb("o", [P, NT, PAIRS * P])
        oT = m.sb("oT", [P, PAIRS, T])
        psQ, psK = m.ps("psQ", [P, T]), m.ps("psK", [P, T])
        psA = [m.ps(f"psA{i}", [P, T]) for i in range(2)]
        psN = [m.ps(f"psN{i}", [P, T]) for i in range(2)]
        psM = m.ps("psM", [P, T])
        v_made = m.flag("v_made", 8)
        v_copied = m.flag("v_copied", 8)
        qk_made = m.flag("qk_made", 16)
        qk_exped = m.flag("qk_exped", 32)
        phi = m.flag("phi", 24)
        inner = m.flag("inner", 16)
        masked = m.flag("masked", 16)
        k_turned = m.flag("k_turned", 8)
        k_copied = m.flag("k_copied", 8)
        state = m.flag("state", 24)
        state_copied = m.flag("state_copied", 24)
        numbered = m.flag("numbered", 16)
        divided = m.flag("divided", 48)
        o_turned = m.flag("o_turned", 8)
        o_copied = m.flag("o_copied", 8)
        projected = m.flag("projected", 1)
        loaded, cleared, finished = m.sem("loaded"), m.sem("cleared"), m.sem("finished")
        m.credit()
        with nc.Block() as block:
            @block.sync
            def _(sp):
                col = lambda v: v.rearrange("(p a) -> p a", a=1)
                sp.dma_start(gain[:], col(a["L1_attn_ln1_g"])).then_inc(loaded, 16)
                sp.dma_start(offset[:], col(a["L1_attn_ln1_b"])).then_inc(loaded, 16)
                sp.dma_start(Wv[:], a["L1_attn_Wv"]).then_inc(loaded, 16)
                sp.dma_start(Wq[:], a["L1_attn_Wq"]).then_inc(loaded, 16)
                sp.dma_start(Wk[:], a["L1_attn_Wk"]).then_inc(loaded, 16)
                sp.dma_start(causal[:], a["c_causal"]).then_inc(loaded, 16)
                sp.dma_start(Wo[:], a["L1_attn_Wo"].rearrange("(c p) d -> p c d", p=P)).then_inc(loaded, 16)
                sp.wait_ge(loaded, 112)

            @block.gpsimd
            def _(pool):
                for pair in Q:
                    for tile in pair:
                        pool.memset(tile[:], 0.0)
                pool.memset(VA[:, :, :, DH:W_], 1.0).then_inc(cleared, 1)
                with turns(pool, B) as b:
                    load.xs_ready.wait(pool, b)
                    pool.sem_inc(load.x_kept.sem, 1)
                post.finish(pool, finished)

            @block.tensor
            def _(pe):
                pe.wait_ge(loaded, 112)
                pe.wait_ge(cleared, 1)

                def project_pair(b, r):
                    qk_exped.wait(pe, b, 4 * r)
                    pe.matmul(psQ[:], Wq[:, r * P:(r + 1) * P], load.xT[:], start=True, stop=True)\
                      .then_inc(qk_made.sem, 1)
                    pe.matmul(psK[:], Wk[:, r * P:(r + 1) * P], load.xT[:], start=True, stop=True)\
                      .then_inc(qk_made.sem, 1)

                def inner_products(b, r):
                    phi.wait(pe, b, 3 * r + 3)
                    for h in range(2):
                        masked.wait(pe, b, 2 * r + h - 1)
                        for c in range(NT):
                            tok = slice(c * P, (c + 1) * P)
                            mm = pe.matmul(psA[h][:, tok], K[r % 2][:, tok], Q[r % 2][h][:, tok],
                                           start=True, stop=True)
                        mm.then_inc(inner.sem, 1)

                def turn_keys(b, r):
                    load.xT_ready.wait(pe, b)
                    k_copied.wait(pe, b, r)
                    for c in range(NT):
                        tok = slice(c * P, (c + 1) * P)
                        mm = pe.transpose(load.psX[:, tok], K[r % 2][:, tok], G.ident[:])
                    mm.then_inc(k_turned.sem, 1)

                def states(b, r, c):
                    if c == 0:
                        k_copied.wait(pe, b, r + 1)
                    state_copied.wait(pe, b, 3 * r + c)
                    rhs = VA[:, c, 2 * r:2 * r + 2, :].rearrange("p h w -> p (h w)")
                    pe.matmul(psM[:, 0:2 * W_], Kt[r % 2][:, c, :], rhs, start=(c == 0), stop=(c == 2),
                              skip_group_check=True).then_inc(state.sem, 1)

                def numerators(b, r, half):
                    if half == 0:
                        masked.wait(pe, b, 2 * r + 2)
                    state_copied.wait(pe, b, 3 * r + (1 if half == 0 else 3))
                    n = 2 * r + half
                    divided.wait(pe, b, 3 * (n - 1))
                    for i in range(2):
                        c = 2 * half + i
                        for h in range(2):
                            out = psN[half][:, (2 * i + h) * W_:(2 * i + h + 1) * W_]
                            mm = pe.matmul(out, AT[r % 2][h][:, c, :], VA[:, c, 2 * r + h, :], start=True,
                                           stop=(c == 0))
                            if c:
                                mm = pe.matmul(out, Q[r % 2][h][:, c * P:(c + 1) * P],
                                               S[r % 2][:, c - 1, h * W_:(h + 1) * W_], start=False, stop=True)
                    mm.then_inc(numbered.sem, 1)

                with turns(pe, B) as b:
                    load.tensor(pe, b)
                    load.xT_ready.wait(pe, b)
                    for n in range(8):
                        v_copied.wait(pe, b, n - 1)
                        if n < 2:
                            masked.wait(pe, b - 1)
                        pe.matmul(psA[n % 2][:], load.xT[:, (n // 2) * P:(n // 2 + 1) * P],
                                  Wv[:, (n % 2) * T:(n % 2 + 1) * T], start=True, stop=True).then_inc(v_made.sem, 1)
                    v_copied.wait(pe, b)
                    project_pair(b, 0)
                    for r in range(PAIRS + 1):
                        if r < PAIRS:
                            inner_products(b, r)
                            turn_keys(b, r)
                        if r + 1 < PAIRS:
                            project_pair(b, r + 1)
                        if r:
                            numerators(b, r - 1, 0)
                        if r < PAIRS:
                            states(b, r, 0)
                        if r:
                            numerators(b, r - 1, 1)
                        if r < PAIRS:
                            states(b, r, 1)
                            states(b, r, 2)
                    for r in range(PAIRS):
                        if r == 0:
                            divided.wait(pe, b)
                            masked.wait(pe, b)
                        o_copied.wait(pe, b, r - 1)
                        for c in range(NT):
                            tok = slice(c * P, (c + 1) * P)
                            mm = pe.transpose(psA[r % 2][:, tok], o[:, c, r * P:(r + 1) * P], G.ident[:])
                        mm.then_inc(o_turned.sem, 1)
                    o_copied.wait(pe, b)
                    for t in range(NT):
                        for r in range(PAIRS):
                            mm = pe.matmul(psN[0][:, t * P:(t + 1) * P], oT[:, r, t:T:NT], Wo[:, r, :],
                                           start=(r == 0), stop=(r == PAIRS - 1))
                    mm.then_inc(projected.sem, 1)
                    post.summed.wait(pe, b)

            @block.scalar
            def _(act):
                act.wait_ge(cleared, 1)
                with turns(act, B) as b:
                    load.scalar(act, b)
                    for n in range(0, 8, 2):
                        v_made.wait(act, b, n + 1)
                        if n == 0:
                            numbered.wait(act, b - 1)
                            state.wait(act, b - 1)
                        act.activation(VA[:, n // 2, 0:8, 0:DH], psA[0][:].rearrange("p (h d) -> p h d", d=DH),
                                       ACT.Copy).then_inc(v_copied.sem, 1)
                        v_made.wait(act, b, n + 2)
                        act.activation(VA[:, n // 2, 8:16, 0:DH], psA[1][:].rearrange("p (h d) -> p h d", d=DH),
                                       ACT.Copy).then_inc(v_copied.sem, 1)

                    def features(r):
                        for i, ps in enumerate((psQ, psK)):
                            qk_made.wait(act, b, 2 * r + i + 1)
                            phi.wait(act, b, 3 * r - (1 if i == 0 else 0))
                            act.activation(ex[i][:], ps[:], ACT.Exp).then_inc(qk_exped.sem, 1)
                            act.activation(re[i][:], ps[:], ACT.Relu).then_inc(qk_exped.sem, 1)

                    def state_copy(r, c):
                        state.wait(act, b, 3 * r + c + 1)
                        numbered.wait(act, b, 2 * r - 2)
                        act.activation(S[r % 2][:, c, :], psM[:, 0:2 * W_], ACT.Copy).then_inc(state_copied.sem, 1)

                    features(0)
                    for r in range(PAIRS):
                        k_turned.wait(act, b, r + 1)
                        state.wait(act, b, 3 * r - 3)
                        act.activation(Kt[r % 2][:], load.psX[:].rearrange("p (c d) -> p c d", c=NT), ACT.Copy)\
                           .then_inc(k_copied.sem, 1)
                        if r + 1 < PAIRS:
                            features(r + 1)
                        for c in range(3):
                            state_copy(r, c)
                    for r in range(0, PAIRS, 2):
                        o_turned.wait(act, b, r + 1)
                        if r == 0:
                            projected.wait(act, b - 1)
                        act.activation(oT[:, r, :], psA[0][:], ACT.Copy).then_inc(o_copied.sem, 1)
                        o_turned.wait(act, b, r + 2)
                        act.activation(oT[:, r + 1, :], psA[1][:], ACT.Copy).then_inc(o_copied.sem, 1)

            @block.vector
            def _(dve):
                dve.wait_ge(loaded, 112)
                dve.wait_ge(cleared, 1)
                with turns(dve, B) as b:
                    load.vector(dve, b, [v_made, qk_made, k_copied])

                    def features(r):
                        qk_exped.wait(dve, b, 4 * r + 2)
                        inner.wait(dve, b, 2 * r - 2)
                        numbered.wait(dve, b, 2 * r - 2)
                        for h in range(2):
                            rows = slice(DH * h, DH * (h + 1))
                            dve.scalar_tensor_tensor(out=Q[r % 2][h][rows, :], in0=ex[0][rows, :], scalar=1.0,
                                                     in1=re[0][rows, :], op0=ALU.min, op1=ALU.add)\
                               .then_inc(phi.sem, 1)
                        qk_exped.wait(dve, b, 4 * r + 4)
                        k_turned.wait(dve, b, r - 1)
                        dve.scalar_tensor_tensor(out=K[r % 2][:], in0=ex[1][:], scalar=1.0, in1=re[1][:],
                                                 op0=ALU.min, op1=ALU.add).then_inc(phi.sem, 1)

                    def mask(r):
                        for h in range(2):
                            inner.wait(dve, b, 2 * r + h + 1)
                            numbered.wait(dve, b, 2 * r - 2)
                            dve.tensor_tensor(AT[r % 2][h][:], psA[h][:].rearrange("p (c i) -> p c i", c=NT),
                                              causal[:].unsqueeze(1).broadcast_to([P, NT, P]), ALU.mult)\
                               .then_inc(masked.sem, 1)

                    def divide(r, half):
                        n = 2 * r + half
                        numbered.wait(dve, b, n + 1)
                        if n == 0:
                            o_turned.wait(dve, b - 1)
                        ps = psN[half][:, 0:4 * W_].rearrange("p (q w) -> p q w", w=W_)
                        dve.tensor_scalar(den[half][:], ps[:, :, DH:W_], EPS_DEN, None, ALU.max)\
                           .then_inc(divided.sem, 1)
                        divided.wait(dve, b, 3 * n + 1)
                        dve.reciprocal(den[half][:], den[half][:]).then_inc(divided.sem, 1)
                        divided.wait(dve, b, 3 * n + 2)
                        dst = o[:, 2 * half:2 * half + 2, r * P:(r + 1) * P].rearrange("p c (h d) -> p c h d", h=2)
                        num = psN[half][:, 0:4 * W_].rearrange("p (c h w) -> p c h w", c=2, h=2)
                        d4 = den[half][:].rearrange("p (c h) a -> p c h a", c=2)
                        dve.tensor_tensor(dst, num[:, :, :, 0:DH], d4.broadcast_to([P, 2, 2, DH]), ALU.mult)\
                           .then_inc(divided.sem, 1)

                    features(0)
                    for r in range(PAIRS + 1):
                        if r < PAIRS:
                            mask(r)
                        if r + 1 < PAIRS:
                            features(r + 1)
                        if r:
                            divide(r - 1, 0)
                            divide(r - 1, 1)
                    projected.wait(dve, b)
                    x1 = batch(G.X1, b)
                    dve.tensor_tensor(x1, psN[0][:].rearrange("p (t d) -> p t d", t=NT), batch(G.X, b), ALU.add)\
                       .then_inc(post.summed.sem, 1)
                    post.vector(dve, b, x1)



def gelu_stage(nc, G, tag, a):
    C = 4
    with ExitStack() as ctx:
        m = Stage(nc, ctx, tag)
        gain, offset = m.sb("gain", [P, 1]), m.sb("offset", [P, 1])
        load, post = Load(m, G, G.X1, affine=(gain, offset)), Post(m, G)
        W1, W2 = m.sb("W1", [P, C * P]), m.sb("W2", [P, C, P])
        act_ = [m.sb(f"act{i}", [P, C, T]) for i in range(1)]
        base = m.sb("base", [P, NT, P])
        psH = [m.ps(f"psH{i}", [P, T]) for i in range(2)]
        psY = m.ps("psY", [P, NT, P])
        hidden = m.flag("hidden", C)
        activated = m.flag("activated", C)
        projected = m.flag("projected", 1)
        base_ready = m.flag("base_ready", 1)
        loaded, finished = m.sem("loaded"), m.sem("finished")
        m.credit()
        with nc.Block() as block:
            @block.sync
            def _(sp):
                col = lambda v: v.rearrange("(p a) -> p a", a=1)
                sp.dma_start(gain[:], col(a["L1_attn_ln2_g"])).then_inc(loaded, 16)
                sp.dma_start(offset[:], col(a["L1_attn_ln2_b"])).then_inc(loaded, 16)
                sp.dma_start(W1[:], a["L1_attn_Wf1"]).then_inc(loaded, 16)
                sp.dma_start(W2[:], a["L1_attn_Wf2"].rearrange("(c p) d -> p c d", p=P)).then_inc(loaded, 16)
                sp.wait_ge(loaded, 64)

            @block.scalar
            def _(act):
                with turns(act, B) as b:
                    load.scalar(act, b)
                    for c in range(C):
                        hidden.wait(act, b, c + 1)
                        projected.wait(act, b - 1)
                        act.activation(act_[0][:, c, :], psH[c % 2][:], ACT.Gelu).then_inc(activated.sem, 1)

            @block.gpsimd
            def _(pool):
                with turns(pool, B) as b:
                    load.xs_ready.wait(pool, b)
                    pool.sem_inc(load.x_kept.sem, 1)
                    post.summed.wait(pool, b - 1)
                    pool.tensor_tensor(base[:], batch(G.X, b), batch(G.X1, b), ALU.add).then_inc(base_ready.sem, 1)
                post.finish(pool, finished)

            @block.tensor
            def _(pe):
                pe.wait_ge(loaded, 64)
                with turns(pe, B) as b:
                    load.tensor(pe, b)
                    load.xT_ready.wait(pe, b)
                    for c in range(C):
                        activated.wait(pe, b, c - 1)
                        pe.matmul(psH[c % 2][:], W1[:, c * P:(c + 1) * P], load.xT[:], start=True, stop=True)\
                          .then_inc(hidden.sem, 1)
                    activated.wait(pe, b)
                    post.summed.wait(pe, b - 1)
                    for t in range(NT):
                        for c in range(C):
                            mm = pe.matmul(psY[:, t, :], act_[0][:, c, t:T:NT], W2[:, c, :],
                                           start=(c == 0), stop=(c == C - 1))
                    mm.then_inc(projected.sem, 1)

            @block.vector
            def _(dve):
                dve.wait_ge(loaded, 64)
                with turns(dve, B) as b:
                    load.vector(dve, b, [hidden])
                    projected.wait(dve, b)
                    base_ready.wait(dve, b)
                    x = batch(G.X, b)
                    dve.tensor_tensor(x, psY[:], base[:], ALU.add).then_inc(post.summed.sem, 1)
                    post.vector(dve, b, x)


def ternary_stage(nc, G, tag, a):
    C, F = 4, 512
    with ExitStack() as ctx:
        m = Stage(nc, ctx, tag)
        load, post = Load(m, G, G.X), Post(m, G)
        Wfc, Wp = m.sb("Wfc", [P, F]), m.sb("Wp", [P, F])
        above, below = m.sb("above", [P, F]), m.sb("below", [P, F])
        size, half = m.sb("size", [P, 2]), m.sb("half", [P, 2, 2])
        ones = m.sb("ones", [P, P])
        gain, offset = m.sb("gain", [P, C]), m.sb("offset", [P, C])
        h = m.sb("h", [P, NT, F])
        hT = m.sb("hT", [P, C, T])
        st, mv = m.sb("st", [P, NT, 6]), m.sb("mvh", [P, NT, 2])
        rs, sh = m.sb("rs", [P, NT]), m.sb("sh", [P, NT])
        psH = [m.ps(f"psH{i}", [P, F]) for i in range(2)]
        psT = [m.ps(f"psT{i}", [P, T]) for i in range(2)]
        psY = m.ps("psY", [P, NT, P])
        hidden = m.flag("hidden", NT)
        geluted = m.flag("geluted", NT)
        stat = m.flag("statted", NT)
        aggregated = m.flag("aggr", 1)
        scaled = m.flag("scaled", 4)
        pool_passed = m.sem("pool_passed")
        normed = m.flag("normed", NT)
        turned_h = m.flag("turned_h", C)
        copied = m.flag("copied", C)
        projected = m.flag("projected", 1)
        loaded, finished, prep, filled, summed = (m.sem(n) for n in ("loaded", "finished", "prep", "filled", "sizes"))
        m.credit()
        with nc.Block() as block:
            @block.sync
            def _(sp):
                sp.dma_start(Wfc[:], a["L1_ffn_W_fc"]).then_inc(loaded, 16)
                sp.dma_start(Wp[:].rearrange("p (c d) -> p c d", c=C),
                             a["L1_ffn_W_proj"].rearrange("(c p) d -> p c d", p=P)).then_inc(loaded, 16)
                sp.dma_start(gain[:], a["L1_ln_w"]).then_inc(loaded, 16)
                sp.dma_start(offset[:], a["L1_ln_b"]).then_inc(loaded, 16)
                sp.wait_ge(loaded, 64)

            @block.vector
            def _(dve):
                dve.memset(ones[:], 1.0).then_inc(filled, 1)
                dve.wait_ge(loaded, 64)
                for i, w in enumerate((Wfc, Wp)):
                    dve.tensor_reduce(size[:, i:i + 1], w[:], AX.X, ALU.add, apply_absolute_value=True)\
                       .then_inc(filled, 1)
                dve.wait_ge(summed, 1)
                dve.tensor_scalar(half[:, 0, :], psY[:, 0, 0:2], 1.0 / (P * F), 1e-6, ALU.mult, ALU.add)\
                   .then_inc(prep, 1)
                dve.wait_ge(prep, 1)
                dve.tensor_scalar(half[:, 1, :], half[:, 0, :], -0.5, None, ALU.mult).then_inc(prep, 1)
                dve.wait_ge(prep, 2)
                dve.tensor_scalar(half[:, 0, :], half[:, 0, :], 0.5, None, ALU.mult).then_inc(prep, 1)
                dve.wait_ge(prep, 3)
                for i, w in enumerate((Wfc, Wp)):
                    dve.wait_ge(prep, 3 + 3 * i)
                    dve.tensor_scalar(above[:], w[:], half[:, 0, i:i + 1], None, ALU.is_gt).then_inc(prep, 1)
                    dve.tensor_scalar(below[:], w[:], half[:, 1, i:i + 1], None, ALU.is_lt).then_inc(prep, 1)
                    dve.wait_ge(prep, 5 + 3 * i)
                    dve.tensor_tensor(w[:], above[:], below[:], ALU.subtract).then_inc(prep, 1)

            @block.tensor
            def _(pe):
                pe.wait_ge(filled, 3)
                pe.matmul(psY[:, 0, 0:2], ones[:], size[:], start=True, stop=True).then_inc(summed, 1)

        with nc.Block() as block:
            @block.scalar
            def _(act):
                with turns(act, B) as b:
                    load.scalar(act, b)
                    for t in range(NT):
                        hidden.wait(act, b, t + 1)
                        turned_h.wait(act, b - 1)
                        act.activation(h[:, t, :], psH[t % 2][:], ACT.Gelu).then_inc(geluted.sem, 1)
                    scaled.wait(act, b)
                    for t in range(NT):
                        act.activation(h[:, t, :], h[:, t, :], ACT.Identity, scale=rs[:, t:t + 1],
                                       bias=sh[:, t:t + 1]).then_inc(normed.sem, 1)

            @block.gpsimd
            def _(pool):
                with turns(pool, B) as b:
                    load.pool(pool, b)
                    c = Chain(scaled, pool, b)
                    aggregated.wait(pool, b)
                    normed.wait(pool, b - 1)
                    stand(pool, pool_passed)
                    c.step(pool.tensor_scalar(rs[:], mv[:, :, 1], LN_EPS, None, ALU.add))
                    c.wait()
                    c.step(pool.tensor_tensor(rs[:], rs[:], G.minus_half[:, 0, :], ALU.pow))
                    c.wait()
                    c.step(pool.tensor_tensor(sh[:], mv[:, :, 0], rs[:], ALU.mult))
                    c.wait()
                    stand(pool, pool_passed)
                    c.step(pool.tensor_scalar(sh[:], sh[:], -1.0, None, ALU.mult))
                    c.end()
                post.finish(pool, finished)

            @block.tensor
            def _(pe):
                with turns(pe, B) as b:
                    load.tensor(pe, b)
                    load.xT_ready.wait(pe, b)
                    for t in range(NT):
                        geluted.wait(pe, b, t - 1)
                        pe.matmul(psH[t % 2][:], load.xT[:, t:T:NT], Wfc[:], start=True, stop=True)\
                          .then_inc(hidden.sem, 1)
                    normed.wait(pe, b)
                    for c in range(C):
                        copied.wait(pe, b, c - 1)
                        for t in range(NT):
                            mm = pe.transpose(psT[c % 2][:, t * P:(t + 1) * P], h[:, t, c * P:(c + 1) * P],
                                              G.ident[:])
                        mm.then_inc(turned_h.sem, 1)
                    copied.wait(pe, b)
                    post.summed.wait(pe, b - 1)
                    for t in range(NT):
                        for c in range(C):
                            mm = pe.matmul(psY[:, t, :], hT[:, c, t * P:(t + 1) * P], Wp[:, c * P:(c + 1) * P],
                                           start=(c == 0), stop=(c == C - 1))
                    mm.then_inc(projected.sem, 1)

            @block.vector
            def _(dve):
                with turns(dve, B) as b:
                    load.vector(dve, b, [hidden])
                    for t in range(NT):
                        geluted.wait(dve, b, t + 1)
                        stand(dve, post.passed)
                        dve.bn_stats(st[:, t, :], h[:, t, :]).then_inc(stat.sem, 1)
                    stat.wait(dve, b)
                    scaled.wait(dve, b - 1)
                    stand(dve, post.passed)
                    for t in range(NT):
                        last = dve.bn_aggr(mv[:, t, :], st[:, t, :])
                    last.then_inc(aggregated.sem, 1)
                    for c in range(C):
                        turned_h.wait(dve, b, c + 1)
                        projected.wait(dve, b - 1)
                        dve.tensor_scalar(hT[:, c, :], psT[c % 2][:], gain[:, c:c + 1], offset[:, c:c + 1],
                                          ALU.mult, ALU.add).then_inc(copied.sem, 1)
                    projected.wait(dve, b)
                    load.x_kept.wait(dve, b)
                    x = batch(G.X, b)
                    dve.tensor_tensor(x, psY[:], x, ALU.add).then_inc(post.summed.sem, 1)
                    post.vector(dve, b, x)


def fourier_stage(nc, G, tag, a):
    with ExitStack() as ctx:
        m = Stage(nc, ctx, tag)
        load, post = Load(m, G, G.X), Post(m, G)
        Wr, Wi, Cc, Ss = (m.sb(n, [P, P]) for n in ("Wr", "Wi", "cos", "sin"))
        nS = m.sb("nsin", [P, P])
        Ur, nUi, M = (m.sb(n, [P, P]) for n in ("Ur", "nUi", "M"))
        bias = m.sb("bias", [P, P])
        base = m.sb("base", [P, NT, P])
        psM = m.ps("psM", [P, 3, P])
        psY = m.ps("psY", [P, NT, P])
        base_ready = m.flag("base_ready", 1)
        projected = m.flag("projected", 1)
        loaded, finished, made, kept = (m.sem(n) for n in ("loaded", "finished", "made", "kept"))
        m.credit()
        with nc.Block() as block:
            @block.sync
            def _(sp):
                for dst, n in ((Wr, "L3_ffn_w_freq_real"), (Wi, "L3_ffn_w_freq_imag"), (Cc, "c_cos"), (Ss, "c_sin")):
                    sp.dma_start(dst[:], a[n]).then_inc(loaded, 16)
                sp.dma_start(bias[:], a["L3_ffn_bias"].rearrange("(a n) -> a n", a=1).broadcast_to([P, P]))\
                  .then_inc(loaded, 16)
                sp.wait_ge(loaded, 80)

            @block.tensor
            def _(pe):
                pe.wait_ge(loaded, 80)
                pe.wait_ge(kept, 1)
                pe.matmul(psM[:, 0, :], Wr[:], Cc[:], start=True, stop=False)
                pe.matmul(psM[:, 0, :], Wi[:], Ss[:], start=False, stop=True).then_inc(made, 1)
                pe.wait_ge(kept, 2)
                pe.matmul(psM[:, 1, :], Wr[:], Ss[:], start=True, stop=False)
                pe.matmul(psM[:, 1, :], Wi[:], nS[:], start=False, stop=True).then_inc(made, 1)
                pe.wait_ge(kept, 3)
                pe.matmul(psM[:, 2, :], Ur[:], Cc[:], start=True, stop=False)
                pe.matmul(psM[:, 2, :], nUi[:], Ss[:], start=False, stop=True).then_inc(made, 1)

            @block.vector
            def _(dve):
                dve.wait_ge(loaded, 80)
                dve.tensor_scalar(nS[:], Cc[:], -1.0, None, ALU.mult).then_inc(kept, 1)
                dve.wait_ge(made, 1)
                dve.tensor_copy(Ur[:], psM[:, 0, :]).then_inc(kept, 1)
                dve.wait_ge(made, 2)
                dve.tensor_copy(nUi[:], psM[:, 1, :]).then_inc(kept, 1)
                dve.wait_ge(made, 3)
                dve.tensor_scalar(M[:], psM[:, 2, :], 1.0 / P, None, ALU.mult).then_inc(kept, 1)

        with nc.Block() as block:
            @block.scalar
            def _(act):
                with turns(act, B) as b:
                    load.scalar(act, b)

            @block.gpsimd
            def _(pool):
                with turns(pool, B) as b:
                    load.xs_ready.wait(pool, b)
                    post.summed.wait(pool, b - 1)
                    pool.tensor_tensor(base[:], load.xs[:], bias[:].unsqueeze(1).broadcast_to([P, NT, P]), ALU.add)\
                        .then_inc(base_ready.sem, 1)
                    base_ready.wait(pool, b)
                    pool.sem_inc(load.x_kept.sem, 1)
                post.finish(pool, finished)

            @block.tensor
            def _(pe):
                with turns(pe, B) as b:
                    load.tensor(pe, b)
                    load.xT_ready.wait(pe, b)
                    post.summed.wait(pe, b - 1)
                    for t in range(NT):
                        mm = pe.matmul(psY[:, t, :], load.xT[:, t:T:NT], M[:], start=True, stop=True)
                    mm.then_inc(projected.sem, 1)

            @block.vector
            def _(dve):
                with turns(dve, B) as b:
                    load.vector(dve, b, [projected])
                    projected.wait(dve, b)
                    base_ready.wait(dve, b)
                    x = batch(G.X, b)
                    dve.tensor_tensor(x, psY[:], base[:], ALU.add).then_inc(post.summed.sem, 1)
                    post.vector(dve, b, x)



def constants():
    i = np.arange(P)
    t = np.arange(T)
    bf = np.dtype("bfloat16") if False else mybir.dt.np(BF16)
    ones = np.ones(T)
    high, low = (t // 256) * 256, t % 256
    kdecay = np.stack([high, low, ones, ones])
    qdecay = np.stack([ones, ones, -high, -low])
    rep = lambda x: np.ascontiguousarray(np.broadcast_to(x[:, None, :], (4, H, T))).astype(bf)
    future = np.where(i[None, :] > i[:, None], MASKED, 0.0)
    masks = np.stack([future, future.T], axis=1).astype(bf)
    angle = 2 * np.pi * ((i[:, None] * i[None, :]) % P) / P
    return {
        "c_ident": np.eye(P, dtype=np.float32),
        "c_qdecay": rep(qdecay),
        "c_kdecay": rep(kdecay),
        "c_masks": masks,
        "c_blocks": (i[:, None] // HD == i[None, :] // HD).astype(np.float32),
        "c_causal": (i[None, :] >= i[:, None]).astype(np.float32),
        "c_cos": np.cos(angle).astype(np.float32),
        "c_sin": np.sin(angle).astype(np.float32),
        "c_iota": np.ascontiguousarray(np.broadcast_to(np.arange(12, dtype=np.float32), (P, 12))),
    }


def layouts(x):
    out = dict(x)
    T_ = lambda w: np.ascontiguousarray(np.swapaxes(w, -1, -2))
    for name in ("L0_attn_Wq", "L0_attn_Wk", "L0_attn_Wv", "L0_attn_Wo", "L2_attn_Wq_w", "L2_attn_Wk_w",
                 "L2_attn_Wv_w", "L1_ffn_W_fc", "L1_ffn_W_proj", "L2_ffn_gate_w", "L2_ffn_w1", "L2_ffn_w2"):
        out[name] = T_(x[name])
    w, b = out.pop("L3_attn_w_qkv"), out.pop("L3_attn_b_qkv")
    for n, side in enumerate("qkv"):
        out[f"L3_w{side}"] = np.ascontiguousarray(w[:, n * P:(n + 1) * P])
        out[f"L3_b{side}"] = np.ascontiguousarray(b[n * P:(n + 1) * P])
    for side in "qv":
        out[f"L3_a{side}T"] = T_(out.pop(f"L3_attn_a_{side}"))
    out["L0_be1"] = np.ascontiguousarray(out.pop("L0_ffn_be1").reshape(12, 6, P).transpose(2, 0, 1))
    out["L0_bs1"] = T_(out.pop("L0_ffn_bs1").reshape(4, P))
    out["L0_b2"] = np.concatenate([out.pop("L0_ffn_be2"), out.pop("L0_ffn_bs2")[None]])
    out["L1_ln_w"], out["L1_ln_b"] = (T_(out.pop(f"L1_ffn_ln_{n}").reshape(4, P)) for n in "wb")
    return out


STAGES = ("A0", "M0", "L1", "F1", "T1", "A2", "M2", "A3", "F3")


def program(nc, a, out, stages=STAGES):
    with ExitStack() as ctx:
        G = setup(nc, ctx, a)
        for s in stages:
            if s == "A0":
                attention_stage(nc, G, s, a, "decay")
            elif s == "A2":
                attention_stage(nc, G, s, a, "cross")
            elif s == "A3":
                attention_stage(nc, G, s, a, "lora")
            elif s == "M0":
                expert_stage(nc, G, s, a, True)
            elif s == "M2":
                expert_stage(nc, G, s, a, False)
            elif s == "L1":
                linear_attention_stage(nc, G, s, a)
            elif s == "F1":
                gelu_stage(nc, G, s, a)
            elif s == "T1":
                ternary_stage(nc, G, s, a)
            elif s == "F3":
                fourier_stage(nc, G, s, a)
        store(nc, G, out)


def store(nc, G, out):
    with ExitStack() as ctx:
        m = Stage(nc, ctx, "st")
        y = m.sb("y", [P, B, NT, P])
        ready, stored = m.sem("ready"), m.sem("stored")
        with nc.Block() as block:
            @block.scalar
            def _(act):
                with turns(act, B) as b:
                    for t in range(NT):
                        last = act.activation(batch(y, b)[:, t, :], batch(G.X, b)[:, t, :], ACT.Identity,
                                              scale=G.rstd[:, bass.ds(b, 1), t], bias=G.shift[:, bass.ds(b, 1), t])
                    last.then_inc(ready, 1)

            @block.sync
            def _(sp):
                dst = out.rearrange("b (p t) d -> b p t d", t=NT)
                with turns(sp, B) as b:
                    sp.wait_ge(ready, b + 1)
                    sp.dma_start(dst[bass.ds(b, 1), :, :, :].rearrange("a p t d -> p (a t) d"), batch(y, b))\
                      .then_inc(stored, 16)
                sp.wait_ge(stored, 16 * B)


def kernel(**inputs):
    import concourse.bacc as bacc
    from concourse.bass_utils import run_bass_kernel_spmd

    arrays = {**layouts({k: np.asarray(v) for k, v in inputs.items()}), **constants()}
    nc = bacc.Bacc("TRN2", target_bir_lowering=False, num_devices=1)
    a = {n: nc.dram_tensor(n, v.shape, mybir.dt.from_np(v.dtype), kind="ExternalInput").ap()
         for n, v in arrays.items()}
    out = nc.dram_tensor("out", (B, T, P), F32, kind="ExternalOutput").ap()
    program(nc, a, out)
    return run_bass_kernel_spmd(nc, [arrays], core_ids=[0]).results[0]["out"]
```

```python
from contextlib import ExitStack

import concourse.bass as bass
import numpy as np
from concourse import mybir

F32 = mybir.dt.float32
BF16 = mybir.dt.bfloat16
U32 = mybir.dt.uint32
ALU = mybir.AluOpType
ACT = mybir.ActivationFunctionType
AX = mybir.AxisListType

P = 128
B = 8
T = 512
NT = T // P
H = 16
HD = P // H
GH = 4
NG = H // GH
LN_EPS = 1e-5
MASKED = -1e30

DECAY_ROWS = 4
PARTS = 3
MAX_ROW = 96


class Flag:

    def __init__(self, sem, per, lead=1, first=0):
        self.sem, self.per, self.lead, self.first = sem, per, lead, first

    def upto(self, turn, k):
        return turn * self.per + (self.lead * self.per + k)

    def wait(self, engine, turn, k=None):
        engine.wait_ge(self.sem, self.upto(turn, self.per if k is None else k))


class Chain:

    def __init__(self, signal, engine, turn):
        self.flag, self.engine, self.turn, self.n = signal, engine, turn, 0

    def step(self, instruction):
        self.n += 1
        assert self.n <= self.flag.per, (self.n, self.flag.per)
        instruction.then_inc(self.flag.sem, 1)

    def wait(self):
        self.flag.wait(self.engine, self.turn, self.n)

    def end(self):
        assert self.n == self.flag.per, (self.n, self.flag.per)


class Stage:

    def __init__(self, nc, ctx, tag):
        self.nc, self.ctx, self.tag, self.flags, self.sems = nc, ctx, tag, [], []

    def sb(self, name, shape, dt=F32):
        return self.ctx.enter_context(self.nc.sbuf_tensor(f"{self.tag}_{name}", shape, dt))

    def ps(self, name, shape):
        return self.ctx.enter_context(self.nc.psum_tensor(f"{self.tag}_{name}", shape, F32))

    def sem(self, name):
        self.sems.append(self.ctx.enter_context(self.nc.semaphore(f"{self.tag}_{name}")))
        return self.sems[-1]

    def flag(self, name, per, lead=1, first=0):
        s = Flag(self.sem(name), per, lead, first)
        self.flags.append(s)
        return s

    def credit(self):
        with self.nc.Block() as block:
            @block.sync
            def _(sp):
                for s in self.flags:
                    if s.lead + s.first:
                        sp.sem_inc(s.sem, (s.lead + s.first) * s.per)
        self.ctx.callback(self.retire)

    def retire(self):
        with self.nc.Block() as block:
            @block.sync
            def _(sp):
                for s in self.sems:
                    sp.sem_clear(s)


def stand(engine, passed):
    engine.sem_inc(passed, 1)


def turns(engine, n):
    return engine.Fori(0, n)


def batch(array, b):
    return array[:, bass.ds(b, 1), :, :].rearrange("p a t d -> p (a t) d")



class Load:

    def __init__(self, m, G, src, normalised=True, affine=None):
        self.m, self.G, self.src, self.normalised, self.affine = m, G, src, normalised, affine
        self.xs = m.sb("xs", [P, NT, P])
        self.xT = m.sb("xT", [P, T])
        self.psX = m.ps("psX", [P, T])
        self.xs_ready = m.flag("xs_ready", 1)
        self.x_kept = m.flag("x_kept", 1)
        self.turned = m.flag("turned", 1)
        self.xT_ready = m.flag("xT_ready", 1)

    def scalar(self, e, b):
        self.turned.wait(e, b - 1)
        self.x_kept.wait(e, b - 1)
        x = batch(self.src, b)
        if not self.normalised:
            e.activation(self.xs[:], x, ACT.Copy).then_inc(self.xs_ready.sem, 1)
            return
        for t in range(NT):
            last = e.activation(self.xs[:, t, :], x[:, t, :], ACT.Identity,
                                scale=self.G.rstd[:, bass.ds(b, 1), t], bias=self.G.shift[:, bass.ds(b, 1), t])
        last.then_inc(self.xs_ready.sem, 1)

    def pool(self, e, b):
        self.xs_ready.wait(e, b)
        e.tensor_copy(batch(self.src, b), self.xs[:]).then_inc(self.x_kept.sem, 1)

    def tensor(self, e, b):
        self.xs_ready.wait(e, b)
        self.xT_ready.wait(e, b - 1)
        for t in range(NT):
            last = e.transpose(self.psX[:, t * P:(t + 1) * P], self.xs[:, t, :], self.G.ident[:])
        last.then_inc(self.turned.sem, 1)

    def vector(self, e, b, users):
        self.turned.wait(e, b)
        for s in users:
            s.wait(e, b - 1)
        out, turned = self.xT[:].rearrange("d (p t) -> d t p", t=NT), self.psX[:].rearrange("d (t p) -> d t p", t=NT)
        if self.affine is None:
            e.tensor_copy(out, turned).then_inc(self.xT_ready.sem, 1)
        else:
            gain, offset = self.affine
            e.tensor_scalar(out, turned, gain[:, 0:1], offset[:, 0:1], ALU.mult, ALU.add)\
             .then_inc(self.xT_ready.sem, 1)


class Post:

    def __init__(self, m, G):
        self.G = G
        self.stats = m.sb("stats", [P, NT, 6])
        self.mv = m.sb("mv", [P, NT, 2])
        self.summed = m.flag("summed", 1)
        self.stat = m.flag("stat", 1)
        self.passed = m.sem("passed")
        self.aggregated = m.flag("aggregated", 1)
        self.mv_kept = m.flag("mv_kept", 1)

    def vector(self, e, b, row):
        self.summed.wait(e, b)
        stand(e, self.passed)
        for t in range(NT):
            last = e.bn_stats(self.stats[:, t, :], row[:, t, :])
        last.then_inc(self.stat.sem, 1)
        self.stat.wait(e, b)
        stand(e, self.passed)
        for t in range(NT):
            last = e.bn_aggr(self.mv[:, t, :], self.stats[:, t, :])
        last.then_inc(self.aggregated.sem, 1)
        self.aggregated.wait(e, b)
        e.tensor_copy(batch(self.G.mv, b), self.mv[:]).then_inc(self.mv_kept.sem, 1)

    def finish(self, e, sem):
        G = self.G
        self.mv_kept.wait(e, B - 1)
        rstd, shift = G.rstd[:, 0:B, :], G.shift[:, 0:B, :]
        e.tensor_scalar(rstd, G.mv[:, 0:B, :, 1], LN_EPS, None, ALU.add).then_inc(sem, 1)
        e.wait_ge(sem, 1)
        e.tensor_tensor(rstd, rstd, G.minus_half[:, 0:B, :], ALU.pow).then_inc(sem, 1)
        e.wait_ge(sem, 2)
        e.tensor_tensor(shift, G.mv[:, 0:B, :, 0], rstd, ALU.mult).then_inc(sem, 1)
        e.wait_ge(sem, 3)
        e.tensor_scalar(shift, shift, -1.0, None, ALU.mult).then_inc(sem, 1)
        e.wait_ge(sem, 4)


class Globals:
    pass


def setup(nc, ctx, a):
    G = Globals()
    m = Stage(nc, ctx, "g")
    G.X = m.sb("X", [P, B + 1, NT, P])
    G.X1 = m.sb("X1", [P, B + 1, NT, P])
    G.mv = m.sb("mv", [P, B + 1, NT, 2])
    G.rstd = m.sb("rstd", [P, B + 1, NT])
    G.shift = m.sb("shift", [P, B + 1, NT])
    G.minus_half = m.sb("minus_half", [P, B + 1, NT])
    G.ident = m.sb("ident", [P, P])
    G.identb = m.sb("identb", [P, P], BF16)
    loaded, filled = m.sem("loaded"), m.sem("filled")
    with nc.Block() as block:
        @block.sync
        def _(sp):
            sp.dma_start(G.ident[:], a["c_ident"]).then_inc(loaded, 16)
            sp.dma_start(G.X[:, 0:B, :, :], a["L0_attn_x"].rearrange("b (p t) d -> p b t d", t=NT)).then_inc(loaded, 16)
            sp.wait_ge(loaded, 32)

        @block.gpsimd
        def _(pool):
            pool.memset(G.rstd[:], 1.0)
            pool.memset(G.X[:, B, :, :], 0.0)
            pool.memset(G.X1[:, B, :, :], 0.0)
            pool.memset(G.mv[:, B, :, :], 0.0)
            pool.memset(G.shift[:], 0.0)
            pool.memset(G.minus_half[:], -0.5).then_inc(filled, 1)

        @block.vector
        def _(dve):
            dve.wait_ge(loaded, 32)
            dve.tensor_copy(G.identb[:], G.ident[:]).then_inc(filled, 1)
    return G



def project(nc, G, tag, src, n, q=None, k=None, v=None, normalised=True):
    with ExitStack() as ctx:
        m = Stage(nc, ctx, tag)
        load = Load(m, G, src, normalised)
        sides = [s for s in (q, k) if s]
        loaded, prepared = m.sem("loaded"), m.sem("prepared")
        nload = 0
        for i, s in enumerate(sides):
            s["W"] = m.sb(f"W{i}", [P, P])
            s["bias"] = m.sb(f"bias{i}", [P, 1])
            s["sbias"] = m.sb(f"sbias{i}", [P, 1])
            s["full"] = m.sb(f"full{i}", [P, T])
            s["raw"] = m.sb(f"raw{i}", [P, T]) if s["mix"] else None
            s["rest"] = m.sb(f"rest{i}", [P, T])
            s["bf"] = [m.sb(f"bf{i}{c}", [P, PARTS, T], BF16) for c in range(2)]
            s["ps"] = m.ps(f"ps{i}", [P, T])
            s["projected"] = m.flag(f"projected{i}", 1)
            s["raw_ready"] = m.flag(f"raw_ready{i}", 1)
            s["mixed"] = m.flag(f"mixed{i}", 1)
            s["full_ready"] = m.flag(f"full_ready{i}", 1)
            s["high_ready"] = m.flag(f"high_ready{i}", 1)
            s["rest_ready"] = m.flag(f"rest_ready{i}", 1)
            s["mid_ready"] = m.flag(f"mid_ready{i}", 1)
            s["low_ready"] = m.flag(f"low_ready{i}", 1, lead=2)
            s["stored"] = [m.flag(f"stored{i}{c}", 16) for c in range(2)]
        if v:
            Wv = m.sb("Wv", [P, P])
            bv = m.sb("bv", [P, P])
            bvc = m.sb("bvc", [P, 1])
            psV = m.ps("psV", [P, NT, P])
            vraw = m.sb("vraw", [P, T]) if v["mix"] else None
            v_projected = m.flag("v_projected", 1)
            v_raw_ready = m.flag("v_raw_ready", 1)
            v_mixed = m.flag("v_mixed", 1)
            v_added = m.flag("v_added", 1)
            v_ready = m.flag("v_ready", 1)
        m.credit()
        xT, xT_users = load.xT, [s["projected"] for s in sides] + ([v_projected] if v else [])
        nload = 32 * len(sides) + (48 if v else 0)

        def batches(engine, body):
            if n == 1:
                body(engine, 0, 0, 0)
                return
            with engine.Fori(0, n // 2) as half:
                for i in range(2):
                    body(engine, 2 * half + i, i, half)

        with nc.Block() as block:
            @block.sync
            def _(sp):
                for s in sides:
                    sp.dma_start(s["W"][:], s["w"]).then_inc(loaded, 16)
                    sp.dma_start(s["bias"][:], s["b"].rearrange("(p a) -> p a", a=1)).then_inc(loaded, 16)
                if v:
                    sp.dma_start(Wv[:], v["w"]).then_inc(loaded, 16)
                    row = v["b"].rearrange("(a n) -> a n", a=1)
                    sp.dma_start(bv[:], row.broadcast_to([P, P])).then_inc(loaded, 16)
                    sp.dma_start(bvc[:], v["b"].rearrange("(p a) -> p a", a=1)).then_inc(loaded, 16)
                def body(sp, b, i, half):
                    for s in sides:
                        s["low_ready"].wait(sp, b)
                        dst = s["parts"][bass.ds(b, 1), :, :, :, :].rearrange("a h d j n -> (a h d) j n")
                        sp.dma_start(dst, s["bf"][i][:]).then_inc(s["stored"][i].sem, 16)
                batches(sp, body)
                for s in sides:
                    for i in range(min(n, 2)):
                        s["stored"][i].wait(sp, (n - 1) // 2)

            @block.scalar
            def _(act):
                act.preload_act_table(ACT.Identity)
                act.wait_ge(loaded, nload)
                act.wait_ge(prepared, max(len(sides), 1))
                load.scalar(act, 0)

                def body(act, b, i, half):
                    load.scalar(act, b + 1)
                    if v and v["mix"] is not None:
                        v_projected.wait(act, b)
                        v_mixed.wait(act, b - 1)
                        act.activation(vraw[:], psV[:].rearrange("p t d -> p (t d)"), ACT.Identity,
                                       bias=bvc[:, 0:1]).then_inc(v_raw_ready.sem, 1)
                    for s in sides:
                        if s["mix"] is not None:
                            s["projected"].wait(act, b)
                            s["mixed"].wait(act, b - 1)
                            act.activation(s["raw"][:], s["ps"][:], ACT.Identity,
                                           bias=s["bias"][:, 0:1]).then_inc(s["raw_ready"].sem, 1)
                            s["mixed"].wait(act, b)
                            kw = dict(scale=s["scale"])
                        else:
                            s["projected"].wait(act, b)
                            kw = dict(scale=s["scale"], bias=s["sbias"][:, 0:1])
                        s["rest_ready"].wait(act, b - 1)
                        act.activation(s["full"][:], s["ps"][:], s["func"], **kw).then_inc(s["full_ready"].sem, 1)
                        s["stored"][i].wait(act, half - 1)
                        act.activation(s["bf"][i][:, 0, :], s["ps"][:], s["func"], **kw)\
                           .then_inc(s["high_ready"].sem, 1)
                batches(act, body)

            @block.gpsimd
            def _(pool):
                load.pool(pool, 0)

                def body(pool, b, i, half):
                    load.pool(pool, b + 1)
                    for s in sides:
                        s["mid_ready"].wait(pool, b)
                        s["stored"][i].wait(pool, half - 1)
                        pool.tensor_tensor(s["bf"][i][:, 2, :], s["rest"][:], s["bf"][i][:, 1, :],
                                           ALU.subtract).then_inc(s["low_ready"].sem, 1)
                batches(pool, body)

            @block.tensor
            def _(pe):
                pe.wait_ge(loaded, nload)
                load.tensor(pe, 0)

                def body(pe, b, i, half):
                    load.xT_ready.wait(pe, b)
                    for s in sides:
                        s["high_ready"].wait(pe, b - 1)
                        pe.matmul(s["ps"][:], s["W"][:], xT[:], start=True, stop=True)\
                          .then_inc(s["projected"].sem, 1)
                    if v:
                        v_added.wait(pe, b - 1)
                        if v["mix"] is None:
                            for t in range(NT):
                                last = pe.matmul(psV[:, t, :], xT[:, t * P:(t + 1) * P], Wv[:],
                                                 start=True, stop=True)
                            last.then_inc(v_projected.sem, 1)
                        else:
                            pe.matmul(psV[:].rearrange("p t d -> p (t d)"), Wv[:], xT[:], start=True, stop=True)\
                              .then_inc(v_projected.sem, 1)
                            v_raw_ready.wait(pe, b)
                            for t in range(NT):
                                last = pe.matmul(psV[:, t, :], vraw[:, t * P:(t + 1) * P], v["mix"][:],
                                                 start=True, stop=True)
                            last.then_inc(v_mixed.sem, 1)
                    for s in sides:
                        if s["mix"] is not None:
                            s["raw_ready"].wait(pe, b)
                            pe.matmul(s["ps"][:], s["mix"][:], s["raw"][:], start=True, stop=True)\
                              .then_inc(s["mixed"].sem, 1)
                    load.tensor(pe, b + 1)
                batches(pe, body)

            @block.vector
            def _(dve):
                dve.wait_ge(loaded, nload)
                for s in sides:
                    dve.tensor_scalar(s["sbias"][:], s["bias"][:], s["scale"], None, ALU.mult)\
                       .then_inc(prepared, 1)
                if not sides:
                    dve.sem_inc(prepared, 1)
                load.vector(dve, 0, xT_users)

                def body(dve, b, i, half):
                    if v:
                        (v_projected if v["mix"] is None else v_mixed).wait(dve, b)
                        out = batch(v["out"], b)
                        if v["mix"] is None:
                            dve.tensor_tensor(out, psV[:], bv[:].unsqueeze(1).broadcast_to([P, NT, P]), ALU.add)\
                               .then_inc(v_added.sem, 1)
                        else:
                            dve.tensor_copy(out, psV[:]).then_inc(v_added.sem, 1)
                        if v["relu"]:
                            v_added.wait(dve, b)
                            dve.tensor_scalar(out, out, 0.0, None, ALU.max).then_inc(v_ready.sem, 1)
                    load.vector(dve, b + 1, xT_users)
                    for s in sides:
                        s["full_ready"].wait(dve, b)
                        s["high_ready"].wait(dve, b)
                        s["low_ready"].wait(dve, b - 1)
                        dve.tensor_tensor(s["rest"][:], s["full"][:], s["bf"][i][:, 0, :], ALU.subtract)\
                           .then_inc(s["rest_ready"].sem, 1)
                        s["rest_ready"].wait(dve, b)
                        s["stored"][i].wait(dve, half - 1)
                        dve.tensor_copy(s["bf"][i][:, 1, :], s["rest"][:]).then_inc(s["mid_ready"].sem, 1)
                batches(dve, body)


class Stacked:

    def __init__(self, m, name, copies):
        self.tiles = [m.sb(f"{name}{i}", [P, H, T], BF16) for i in range(copies)]


def stack_rows(parts, b, query, j):
    if query:
        return [(DECAY_ROWS + 24 * j + HD * i, parts[b, :, :, j, :].rearrange("h d n -> d h n")) for i in range(PARTS)]
    return [(DECAY_ROWS + 24 * j + HD * i, parts[b, :, :, i, :].rearrange("h d n -> d h n")) for i in range(PARTS)]


def attend(nc, G, tag, a, qparts, kparts, Vc, O, causal, shared_keys):
    units = NT
    with ExitStack() as ctx:
        m = Stage(nc, ctx, tag)
        KC = 1 if shared_keys else 2
        QS = Stacked(m, "QS", 2).tiles
        KS = Stacked(m, "KS", KC).tiles
        VA = [m.sb(f"VA{i}", [P, NT, H, 32]) for i in range(KC)]
        PT = [m.sb(f"PT{i}", [P, GH, T]) for i in range(2)]
        negmax = [m.sb(f"negmax{i}", [P, GH, NT]) for i in range(2)]
        mrest = m.sb("mrest", [NT * GH, P])
        mparts = m.sb("mparts", [NT * GH, PARTS, P], BF16)
        Osb = m.sb("Osb", [P, T])
        rden = m.sb("rden", [P, NT, GH, 1])
        masks = m.sb("masks", [P, 2, P], BF16)
        psA = [m.ps(f"psA{i}", [P, T]) for i in range(3)]
        psB = [m.ps(f"psB{i}", [P, T]) for i in range(3)]
        psO = m.ps("psO", [P, T])
        psT = m.ps("psT", [P, T])

        queries_in = m.flag("queries_in", 16 * PARTS * PARTS)
        keys_in = m.flag("keys_in", 16 * PARTS * PARTS)
        values_in = m.flag("values_in", 1)
        row_scores = m.flag("row_scores", 16)
        maxed = m.flag("maxed", 16)
        max_turned = m.flag("max_turned", 1)
        max_split = m.flag("max_split", 4)
        max_in = m.flag("max_in", 16 * PARTS)
        col_scores = m.flag("col_scores", 16)
        exped = m.flag("exped", 16)
        weighted = m.flag("weighted", 4, lead=5)
        out_copied = m.flag("out_copied", 1, first=-1)
        out_turned = m.flag("out_turned", 1, lead=2, first=-1)
        out_scaled = m.flag("out_scaled", 2, lead=3, first=-1)
        constant = m.sem("constant")
        cleared = m.sem("cleared")
        m.credit()

        def tokens(t):
            return slice(t * P, (t + 1) * P)

        BANK = [0, 1, 2] * 4 + [0, 1, 0, 2]

        def before(n):
            return max(k for k in range(n - 16, n) if BANK[k % 16] == BANK[n])

        with nc.Block() as block:
            @block.gpsimd
            def _(pool):
                for tile in QS + KS:
                    pool.memset(tile[:], 0.0)
                pool.memset(O[:, B + 1, :, :], 0.0)
                for tile in VA:
                    last = pool.memset(tile[:], 0.0)
                last.then_inc(cleared, 1)

            @block.sync
            def _(sp):
                sp.wait_ge(cleared, 1)
                if causal:
                    for tile in QS:
                        sp.dma_start(tile[0:DECAY_ROWS, :, :], a["c_qdecay"]).then_inc(constant, 16)
                    for tile in KS:
                        sp.dma_start(tile[0:DECAY_ROWS, :, :], a["c_kdecay"]).then_inc(constant, 16)
                    sp.dma_start(masks[:], a["c_masks"]).then_inc(constant, 16)
                    sp.wait_ge(constant, 16 * (2 + KC + 1))

            @block.vector
            def _(dve):
                dve.wait_ge(cleared, 1)
                for tile in KS:
                    dve.memset(tile[MAX_ROW:MAX_ROW + PARTS, :, :], 1.0)
                for tile in VA:
                    dve.memset(tile[:, :, :, HD:HD + 1], 1.0)
                dve.memset(psO[:], 1.0)

        def slots(body):
            def walk(engine):
                with engine.Fori(0, B - 2, 2) as b:
                    for i in range(2):
                        body(engine, b + i, i, False, False)
                for i in range(2):
                    body(engine, B - 2 + i, i, i == 1, i == 1)
            return walk

        with nc.Block() as block:
            @block.sync
            def _(sp):
                def load(b, i, first=False):
                    if not first:
                        col_scores.wait(sp, 4 * (b - 2) + 3)
                    for j in range(PARTS):
                        for row, src in stack_rows(qparts, b, True, j):
                            sp.dma_start(QS[i][row:row + HD, :, :], src).then_inc(queries_in.sem, 16)
                        if not shared_keys:
                            for row, src in stack_rows(kparts, b, False, j):
                                sp.dma_start(KS[i][row:row + HD, :, :], src).then_inc(keys_in.sem, 16)

                if shared_keys:
                    for j in range(PARTS):
                        for row, src in stack_rows(kparts, 0, False, j):
                            sp.dma_start(KS[0][row:row + HD, :, :], src).then_inc(keys_in.sem, 16)
                load(0, 0, True)

                def max_rows(b, i, g):
                    for j, steps in enumerate((1, 3, 4)):
                        max_split.wait(sp, 4 * b + g, steps)
                        dst = QS[i][MAX_ROW + j:MAX_ROW + j + 1, GH * g:GH * g + GH, :]
                        sp.dma_start(dst, mparts[:, j, :]).then_inc(max_in.sem, 16)

                def body(sp, b, i, last, _):
                    max_rows(b, i, 0)
                    if not last:
                        load(b + 1, (i + 1) % 2)
                    for g in range(1, NG):
                        max_rows(b, i, g)
                slots(body)(sp)

            @block.gpsimd
            def _(pool):
                if shared_keys:
                    src = Vc[:, 0, :, :].rearrange("p t (h d) -> p t h d", d=HD)
                    pool.tensor_copy(VA[0][:, :, :, 0:HD], src).then_inc(values_in.sem, 1)
                else:
                    def body(pool, b, i, last, _):
                        weighted.wait(pool, 4 * (b - 2) + 3)
                        src = Vc[:, bass.ds(b, 1), :, :].rearrange("p a t (h d) -> p (a t) h d", d=HD)
                        pool.tensor_copy(VA[i][:, :, :, 0:HD], src).then_inc(values_in.sem, 1)
                    slots(body)(pool)

            @block.tensor
            def _(pe):
                def rows(G4, i, g, it, hh):
                    N = (it + 1) * P if causal else T
                    n, h = it * GH + hh, GH * g + hh
                    maxed.wait(pe, G4, before(n) + 1)
                    out = psA[BANK[n]]
                    mm = pe.matmul(out[:, 0:N], QS[i][0:MAX_ROW, h, tokens(it)],
                                   KS[i % KC][0:MAX_ROW, h, 0:N], start=True, stop=not causal,
                                   skip_group_check=causal)
                    if causal:
                        mm = pe.matmul(out[:, tokens(it)], G.identb[:], masks[:, 0, :], start=False,
                                       stop=True, skip_group_check=True)
                    mm.then_inc(row_scores.sem, 1)

                def turn_max(G4, i):
                    maxed.wait(pe, G4)
                    out_scaled.wait(pe, G4 - 3)
                    pe.transpose(psT[0:NT * GH, 0:P], negmax[i][:].rearrange("p h t -> p (h t)"), G.ident[:])\
                      .then_inc(max_turned.sem, 1)

                def columns(G4, i, g, jt, hh):
                    lo = jt * P if causal else 0
                    N = T - lo
                    n, h = jt * GH + hh, GH * g + hh
                    exped.wait(pe, G4, before(n) + 1)
                    out = psB[BANK[n]]
                    mm = pe.matmul(out[:, 0:N], KS[i % KC][:, h, tokens(jt)], QS[i][:, h, lo:T],
                                   start=True, stop=not causal, skip_group_check=causal)
                    if causal:
                        mm = pe.matmul(out[:, 0:P], G.identb[:], masks[:, 1, :], start=False,
                                       stop=True, skip_group_check=True)
                    mm.then_inc(col_scores.sem, 1)

                def weigh(G4, i, g, jt):
                    lo = jt * P if causal else 0
                    N = T - lo
                    if jt == 0:
                        out_copied.wait(pe, G4 - 1)
                    exped.wait(pe, G4, GH * (jt + 1))
                    for hh in range(GH):
                        mm = pe.matmul(psO[32 * hh:32 * hh + 32, lo:T], VA[i % KC][:, jt, GH * g + hh, :],
                                       PT[jt % 2][:, hh, 0:N], start=(jt == 0), stop=(jt == NT - 1),
                                       tile_position=(0, 32 * hh), skip_group_check=True)
                    mm.then_inc(weighted.sem, 1)

                def turn_out(G4, alone):
                    out_copied.wait(pe, G4)
                    if alone:
                        out_scaled.wait(pe, G4 - 1)
                    else:
                        max_split.wait(pe, G4 + 2, 2)
                    for t in range(NT):
                        mm = pe.transpose(psT[:, tokens(t)], Osb[:, tokens(t)], G.ident[:])
                    mm.then_inc(out_turned.sem, 1)

                def operands(b):
                    queries_in.wait(pe, b)
                    if not shared_keys:
                        keys_in.wait(pe, b)

                if shared_keys:
                    keys_in.wait(pe, 0)
                    values_in.wait(pe, 0)
                operands(0)
                for g in range(2):
                    for it in range(units):
                        for hh in range(GH):
                            rows(g, 0, g, it, hh)
                    if g == 0:
                        turn_max(0, 0)
                max_in.wait(pe, 0)
                for hh in range(GH):
                    columns(0, 0, 0, 0, hh)

                def body(pe, b, i, last, _):
                    for g in range(NG):
                        G4 = 4 * b + g
                        ahead = not (last and g >= 2)
                        end = last and g == NG - 1
                        ai, ag = (i, g + 2) if g < 2 else ((i + 1) % 2, g - 2)
                        if g == 2 and ahead:
                            operands(b + 1)
                        if g == 0 and not shared_keys:
                            values_in.wait(pe, b)
                        for u in range(units):
                            if u == 2:
                                turn_out(G4 - 1, end)
                            if u < units - 1:
                                following = (G4, i, g, u + 1)
                            elif not end:
                                following = (G4 + 1, i if g < NG - 1 else (i + 1) % 2, (g + 1) % NG, 0)
                                max_in.wait(pe, G4 + 1)
                            else:
                                following = None
                            for hh in range(GH):
                                if following:
                                    columns(*following, hh)
                                if ahead:
                                    rows(G4 + 2, ai, ag, u, hh)
                                if u == 0 and hh == 1 and not end:
                                    turn_max(G4 + 1, (g + 1) % 2)
                                if hh == 1:
                                    weigh(G4, i, g, u)
                    if last:
                        turn_out(4 * b + 3, True)

                slots(body)(pe)

            @block.scalar
            def _(act):
                def copy_out(act, G4):
                    weighted.wait(act, G4)
                    out_turned.wait(act, G4 - 1)
                    act.activation(Osb[:], psO[:], ACT.Copy).then_inc(out_copied.sem, 1)

                def body(act, b, i, last, _):
                    for g in range(NG):
                        G4 = 4 * b + g
                        for u in range(units):
                            N = T - u * P if causal else T
                            weighted.wait(act, G4, u - 1)
                            for hh in range(GH):
                                n = GH * u + hh
                                col_scores.wait(act, G4, n + 1)
                                act.activation(PT[u % 2][:, hh, 0:N], psB[BANK[n]][:, 0:N], ACT.Exp)\
                                   .then_inc(exped.sem, 1)
                                if n == 2:
                                    copy_out(act, G4 - 1)
                    if last:
                        copy_out(act, 4 * b + 3)
                slots(body)(act)

            @block.vector
            def _(dve):
                def maximum(G4, i, n):
                    it, hh = divmod(n, GH)
                    N = (it + 1) * P if causal else T
                    row_scores.wait(dve, G4, n + 1)
                    if n == 0 and not (isinstance(G4, int) and G4 < 2):
                        max_turned.wait(dve, G4 - 2)
                    dve.tensor_reduce(negmax[i][:, hh, it:it + 1], psA[BANK[n]][:, 0:N], AX.X, ALU.max,
                                      negate=True).then_inc(maxed.sem, 1)

                def split_max(G4, step):
                    rows16 = psT[0:NT * GH, 0:P]
                    if step == 0:
                        max_turned.wait(dve, G4)
                        max_in.wait(dve, G4 - 1)
                        made = dve.tensor_copy(mparts[:, 0, :], rows16)
                    else:
                        max_split.wait(dve, G4, step)
                        if step == 1:
                            made = dve.tensor_tensor(mrest[:], rows16, mparts[:, 0, :], ALU.subtract)
                        elif step == 2:
                            made = dve.tensor_copy(mparts[:, 1, :], mrest[:])
                        else:
                            made = dve.tensor_tensor(mparts[:, 2, :], mrest[:], mparts[:, 1, :], ALU.subtract)
                    made.then_inc(max_split.sem, 1)

                def scale_out(b, g, G4, step):
                    turned = psT[:].rearrange("p (t h c) -> p t h c", t=NT, h=GH)
                    if step == 0:
                        out_turned.wait(dve, G4)
                        dve.reciprocal(rden[:], turned[:, :, :, HD:HD + 1]).then_inc(out_scaled.sem, 1)
                    else:
                        out_scaled.wait(dve, G4, 1)
                        dst = O[:, bass.ds(b + 1, 1), :, GH * HD * g:GH * HD * (g + 1)]\
                            .rearrange("p a t (h d) -> p (a t) h d", d=HD)
                        dve.tensor_tensor(dst, turned[:, :, :, 0:HD], rden[:].broadcast_to([P, NT, GH, HD]),
                                          ALU.mult).then_inc(out_scaled.sem, 1)

                for g in range(2):
                    for n in range(units * GH):
                        maximum(g, g, n)
                for step in range(4):
                    split_max(0, step)

                def body(dve, b, i, last, _):
                    for g in range(NG):
                        G4 = 4 * b + g
                        for n in range(units * GH):
                            if not (last and g >= 2):
                                maximum(G4 + 2, g % 2, n)
                            if 2 <= n < 6 and not (last and g == NG - 1):
                                split_max(G4 + 1, n - 2)
                            if n in (10, 12):
                                scale_out(b if g else b - 1, (g - 1) % NG, G4 - 1, (n - 10) // 2)
                    if last:
                        for step in range(2):
                            scale_out(b, 3, 4 * b + 3, step)
                slots(body)(dve)


def attention_output(nc, G, tag, a, O, w, bias):
    with ExitStack() as ctx:
        m = Stage(nc, ctx, tag)
        post = Post(m, G)
        os_ = m.sb("os", [P, NT, P])
        oT = m.sb("oT", [P, T])
        base = m.sb("base", [P, NT, P])
        psT = m.ps("psT", [P, T])
        psY = m.ps("psY", [P, NT, P])
        copied = m.flag("copied", 1)
        turned = m.flag("turned", 1)
        oT_ready = m.flag("oT_ready", 1)
        projected = m.flag("projected", 1)
        base_ready = m.flag("base_ready", 1)
        loaded, finished = m.sem("loaded"), m.sem("finished")
        m.credit()
        if w is not None:
            W = m.sb("W", [P, P])
            bo = m.sb("bo", [P, P])
        with nc.Block() as block:
            if w is not None:
                @block.sync
                def _(sp):
                    sp.dma_start(W[:], w).then_inc(loaded, 16)
                    sp.dma_start(bo[:], bias.rearrange("(a n) -> a n", a=1).broadcast_to([P, P])).then_inc(loaded, 16)
                    sp.wait_ge(loaded, 32)

            @block.gpsimd
            def _(pool):
                if w is not None:
                    pool.wait_ge(loaded, 32)
                with turns(pool, B) as b:
                    post.summed.wait(pool, b - 1)
                    x = batch(G.X, b)
                    if w is not None:
                        pool.tensor_tensor(base[:], x, bo[:].unsqueeze(1).broadcast_to([P, NT, P]), ALU.add)\
                            .then_inc(base_ready.sem, 1)
                    else:
                        pool.tensor_tensor(base[:], x, x, ALU.add).then_inc(base_ready.sem, 1)
                post.finish(pool, finished)

            @block.scalar
            def _(act):
                def fetch(b):
                    turned.wait(act, b - 1)
                    act.activation(os_[:], batch(O, b + 1), ACT.Copy).then_inc(copied.sem, 1)

                fetch(0)
                with turns(act, B) as b:
                    fetch(b + 1)
                    if w is not None:
                        projected.wait(act, b - 1)
                        act.activation(oT[:], psT[:], ACT.Copy).then_inc(oT_ready.sem, 1)

            @block.tensor
            def _(pe):
                if w is not None:
                    pe.wait_ge(loaded, 32)
                def turn(b):
                    copied.wait(pe, b)
                    if w is not None:
                        oT_ready.wait(pe, b - 1)
                    else:
                        post.summed.wait(pe, b - 1)
                    for t in range(NT):
                        last = pe.transpose(psT[:, t * P:(t + 1) * P], os_[:, t, :], G.ident[:])
                    last.then_inc(turned.sem, 1)

                turn(0)
                with turns(pe, B) as b:
                    turn(b + 1)
                    if w is not None:
                        post.summed.wait(pe, b - 1)
                        for t in range(NT):
                            last = pe.matmul(psY[:, t, :], oT[:, t:T:NT], W[:], start=True, stop=True)
                        last.then_inc(projected.sem, 1)

            @block.vector
            def _(dve):
                with turns(dve, B) as b:
                    base_ready.wait(dve, b)
                    x = batch(G.X, b)
                    if w is not None:
                        projected.wait(dve, b)
                        dve.tensor_tensor(x, psY[:], base[:], ALU.add).then_inc(post.summed.sem, 1)
                    else:
                        turned.wait(dve, b)
                        dve.tensor_tensor(x, psT[:].rearrange("p (t c) -> p t c", t=NT), base[:], ALU.add)\
                           .then_inc(post.summed.sem, 1)
                    post.vector(dve, b, x)


def attention_stage(nc, G, tag, a, kind):
    scale = float(np.float32(1.0) / np.sqrt(np.float32(HD)))
    with ExitStack() as ctx:
        m = Stage(nc, ctx, tag)
        one = kind == "cross"
        O = m.sb("O", [P, B + 2, NT, P])
        Vc = m.sb("Vc", [P, 1 if one else B, NT, P])
        qparts = nc.dram_tensor(f"{tag}_qparts", [B, H, HD, PARTS, T], BF16, kind="Internal").ap()
        kparts = nc.dram_tensor(f"{tag}_kparts", [1 if one else B, H, HD, PARTS, T], BF16, kind="Internal").ap()
        if kind == "decay":
            q = dict(w=a["L0_attn_Wq"], b=a["L0_attn_bq"], scale=scale, func=ACT.Identity, mix=None, parts=qparts)
            k = dict(w=a["L0_attn_Wk"], b=a["L0_attn_bk"], scale=1.0, func=ACT.Identity, mix=None, parts=kparts)
            v = dict(w=a["L0_attn_Wv"], b=a["L0_attn_bv"], relu=False, mix=None, out=Vc)
            project(nc, G, tag + "p", G.X, B, q, k, v)
            attend(nc, G, tag + "a", a, qparts, kparts, Vc, O, True, False)
            attention_output(nc, G, tag + "o", a, O, a["L0_attn_Wo"], a["L0_attn_bo"])
        elif kind == "cross":
            q = dict(w=a["L2_attn_Wq_w"], b=a["L2_attn_Wq_b"], scale=scale, func=ACT.Relu, mix=None, parts=qparts)
            k = dict(w=a["L2_attn_Wk_w"], b=a["L2_attn_Wk_b"], scale=1.0, func=ACT.Relu, mix=None, parts=kparts)
            v = dict(w=a["L2_attn_Wv_w"], b=a["L2_attn_Wv_b"], relu=True, mix=None, out=Vc)
            KV = m.sb("KV", [P, 3, NT, P])
            spare = m.sem("spare")
            kv_in = m.sem("kv_in")
            ctx.callback(m.retire)
            with nc.Block() as block:
                @block.sync
                def _(sp):
                    for i, name in enumerate(("L2_attn_keys", "L2_attn_values")):
                        sp.dma_start(KV[:, i, :, :], a[name].rearrange("a (p t) d -> p (a t) d", t=NT))\
                          .then_inc(kv_in, 16)
                    sp.wait_ge(kv_in, 32)

                @block.gpsimd
                def _(pool):
                    pool.memset(KV[:, 2, :, :], 0.0).then_inc(spare, 1)
            project(nc, G, tag + "k", KV[:, 0:2, :, :], 1, k=k, normalised=False)
            project(nc, G, tag + "v", KV[:, 1:3, :, :], 1, v=v, normalised=False)
            project(nc, G, tag + "p", G.X, B, q=q)
            attend(nc, G, tag + "a", a, qparts, kparts, Vc, O, False, True)
            attention_output(nc, G, tag + "o", a, O, None, None)
        else:
            mixes = lora(nc, G, m, a)
            ctx.callback(m.retire)
            q = dict(w=a["L3_wq"], b=a["L3_bq"], scale=scale, func=ACT.Identity, mix=mixes[0], parts=qparts)
            k = dict(w=a["L3_wk"], b=a["L3_bk"], scale=1.0, func=ACT.Identity, mix=None, parts=kparts)
            v = dict(w=a["L3_wv"], b=a["L3_bv"], relu=False, mix=mixes[1], out=Vc)
            project(nc, G, tag + "p", G.X, B, q, k, v)
            attend(nc, G, tag + "a", a, qparts, kparts, Vc, O, False, False)
            attention_output(nc, G, tag + "o", a, O, a["L3_attn_w_proj"], a["L3_attn_b_proj"])


def lora(nc, G, m, a):
    LORA_SCALE = 2.0
    R = 16
    A = [m.sb(f"A{i}", [R, P]) for i in range(2)]
    Bm = [m.sb(f"B{i}", [R, P]) for i in range(2)]
    blocks = m.sb("blocks", [P, P])
    out = [m.sb(f"mix{i}", [P, P]) for i in range(2)]
    loaded, made, masked, added = m.sem("l_in"), m.sem("l_mm"), m.sem("l_mask"), m.sem("l_add")
    with ExitStack() as ctx:
        ps = [ctx.enter_context(nc.psum_tensor(f"{m.tag}_psL{i}", [P, T], F32)) for i in range(2)]
        with nc.Block() as block:
            @block.sync
            def _(sp):
                sp.dma_start(blocks[:], a["c_blocks"]).then_inc(loaded, 16)
                for i, side in enumerate("qv"):
                    sp.dma_start(A[i][:].rearrange("r (h d) -> r h d", h=H),
                                 a[f"L3_a{side}T"].unsqueeze(1).broadcast_to([R, H, HD])).then_inc(loaded, 16)
                    sp.dma_start(Bm[i][:].rearrange("r (h d) -> r h d", h=H),
                                 a[f"L3_attn_b_{side}"].unsqueeze(1).broadcast_to([R, H, HD])).then_inc(loaded, 16)
                sp.wait_ge(loaded, 80)

            @block.tensor
            def _(pe):
                pe.wait_ge(loaded, 80)
                for i in range(2):
                    pe.matmul(ps[i][:, 0:P], A[i][:], Bm[i][:], start=True, stop=True).then_inc(made, 1)

            @block.vector
            def _(dve):
                dve.wait_ge(loaded, 80)
                for i in range(2):
                    dve.wait_ge(made, i + 1)
                    dve.scalar_tensor_tensor(out=out[i][:], in0=ps[i][:, 0:P], scalar=LORA_SCALE, in1=blocks[:],
                                             op0=ALU.mult, op1=ALU.mult).then_inc(masked, 1)
                    dve.wait_ge(masked, i + 1)
                    dve.tensor_tensor(out[i][:], out[i][:], G.ident[:], ALU.add).then_inc(added, 1)
    return out



def expert_stage(nc, G, tag, a, gated):
    E = 12
    if gated:
        C, FF, temperature = 3, 3 * P, 1.5
        order = [(E, 2)] + [(e, C) for e in range(E)]
    else:
        C, FF, temperature = 2, 2 * P, 1.0
        order = [(e, C) for e in range(8)]
    chunks = [(x, c) for x, (_, n) in enumerate(order) for c in range(n)]
    NCH, NX = len(chunks), len(order)
    first_chunk = [sum(n for _, n in order[:x]) for x in range(NX + 1)]
    with ExitStack() as ctx:
        m = Stage(nc, ctx, tag)
        load, post = Load(m, G, G.X), Post(m, G)
        NE = 12 if gated else 8
        W1 = m.sb("W1", [P, NE, (2 if gated else 1) * FF])
        W2 = m.sb("W2", [P, NE, C, P])
        Wr = m.sb("Wr", [P, E])
        br = m.sb("br", [P, E])
        iota = m.sb("iota", [P, E])
        if gated:
            Ws1, Ws2 = m.sb("Ws1", [P, 4 * P]), m.sb("Ws2", [P, 2, P])
            b1, bs1 = m.sb("b1", [P, NE, 2 * C]), m.sb("bs1", [P, 4])
            b2 = m.sb("b2", [E + 1, P])
            gate = [m.sb(f"gate{i}", [P, T]) for i in range(2)]
            wT = m.sb("wT", [E + 1, NT, P])
        act_ = [m.sb(f"act{i}", [P, C, T]) for i in range(2)]
        acc = m.sb("acc", [P, NT, P])
        logits = m.sb("logits", [P, NT, E])
        top = m.sb("top", [P, NT, 8])
        index = m.sb("index", [P, NT, 8], U32)
        indexf = m.sb("indexf", [P, NT, 2])
        margin = m.sb("margin", [P, NT])
        th = m.sb("th", [P, NT, 1])
        share = m.sb("share", [P, 2, NT])
        hit = m.sb("hit", [P, 2, NT, E])
        w = m.sb("w", [P, NT, E + 1])
        through = m.sb("through", [P, NT])
        psa = [m.ps(f"psa{i}", [P, T]) for i in range(2)]
        psg = [m.ps(f"psg{i}", [P, T]) for i in range(2)]
        psY = [m.ps(f"psY{i}", [P, NT, P]) for i in range(2)]
        psR = m.ps("psR", [P, T])
        hidden = m.flag("hidden", NCH)
        gelued = m.flag("gelued", NCH)
        activated = m.flag("activated", NCH)
        yielded = m.flag("yielded", NX)
        added = m.flag("added", NX + 2)
        scored = m.flag("scored", 1)
        ranked = m.flag("ranked", 5)
        tanhed = m.flag("tanhed", 1)
        routed = m.flag("routed", 4 if gated else 6)
        turned_w = m.flag("turned_w", 1)
        copied_w = m.flag("copied_w", 1)
        biased = m.flag("biased", 1)
        small_in, ones, finished = m.sem("small_in"), m.sem("ones"), m.sem("finished")
        expert_in = [m.sem(f"expert_in{x}") for x in range(NX)]
        m.credit()
        nsmall = 16 * (6 if gated else 3)
        prefix = "L0_ffn" if gated else "L2_ffn"
        with nc.Block() as block:
            @block.sync
            def _(sp):
                rows = lambda v: v.rearrange("(a n) -> a n", a=1).broadcast_to([P, E])
                if gated:
                    sp.dma_start(Wr[:], a["L0_ffn_Wr"]).then_inc(small_in, 16)
                    sp.dma_start(br[:], rows(a["L0_ffn_br"])).then_inc(small_in, 16)
                    sp.dma_start(b1[:], a["L0_be1"]).then_inc(small_in, 16)
                    sp.dma_start(bs1[:], a["L0_bs1"]).then_inc(small_in, 16)
                    sp.dma_start(b2[:], a["L0_b2"]).then_inc(small_in, 16)
                else:
                    sp.dma_start(Wr[:], a["L2_ffn_gate_w"]).then_inc(small_in, 16)
                    sp.dma_start(br[:], rows(a["L2_ffn_expert_bias"])).then_inc(small_in, 16)
                sp.dma_start(iota[:], a["c_iota"]).then_inc(small_in, 16)
                for x, (e, n) in enumerate(order):
                    if e == E:
                        sp.dma_start(Ws1[:], a["L0_ffn_Ws1"]).then_inc(expert_in[x], 16)
                        sp.dma_start(Ws2[:], a["L0_ffn_Ws2"].rearrange("(c f) d -> f c d", f=P))\
                          .then_inc(expert_in[x], 16)
                    else:
                        w1, w2 = (a["L0_ffn_We1"], a["L0_ffn_We2"]) if gated else (a["L2_ffn_w1"], a["L2_ffn_w2"])
                        sp.dma_start(W1[:, e, :], w1[e, :, :]).then_inc(expert_in[x], 16)
                        sp.dma_start(W2[:, e, :, :], w2[e, :, :].rearrange("(c f) d -> f c d", f=P))\
                          .then_inc(expert_in[x], 16)
                for s in expert_in:
                    sp.wait_ge(s, 32)

            @block.scalar
            def _(act):
                act.preload_act_table(ACT.Gelu if gated else ACT.Silu)
                act.wait_ge(small_in, nsmall)
                load.scalar(act, 0)
                with turns(act, B) as b:
                    for n, (x, c) in enumerate(chunks):
                        e, C_ = order[x]
                        hidden.wait(act, b, n + 1)
                        if gated:
                            activated.wait(act, b, n - 1)
                            bias = bs1[:, 2 + c:3 + c] if e == E else b1[:, e, C + c:C + c + 1]
                            act.activation(gate[n % 2][:], psg[n % 2][:], ACT.Gelu, bias=bias)\
                               .then_inc(gelued.sem, 1)
                        else:
                            yielded.wait(act, b, max(x - 1, 0))
                            ps = (psa + psg)[n % 4]
                            act.activation(act_[x % 2][:, c, :], ps[:], ACT.Silu).then_inc(activated.sem, 1)
                        if n == NCH - 4:
                            load.scalar(act, b + 1)
                        if n == 3:
                            ranked.wait(act, b)
                            act.activation(th[:, :, 0], margin[:], ACT.Tanh, scale=0.5 / temperature)\
                               .then_inc(tanhed.sem, 1)

            @block.gpsimd
            def _(pool):
                pool.memset(w[:], 1.0).then_inc(ones, 1)
                load.pool(pool, 0)
                with turns(pool, B) as b:
                    load.pool(pool, b + 1)
                post.finish(pool, finished)

            @block.tensor
            def _(pe):
                pe.wait_ge(small_in, nsmall)

                def hidden_of(b, x):
                    e, C_ = order[x]
                    pe.wait_ge(expert_in[x], 32)
                    for c in range(C_):
                        n = first_chunk[x] + c
                        w1 = Ws1[:, :] if e == E else W1[:, e, :]
                        if gated:
                            activated.wait(pe, b, n - 1)
                            pe.matmul(psa[n % 2][:], w1[:, c * P:(c + 1) * P], load.xT[:], start=True, stop=True)
                            pe.matmul(psg[n % 2][:], w1[:, (C_ + c) * P:(C_ + c + 1) * P], load.xT[:],
                                      start=True, stop=True).then_inc(hidden.sem, 1)
                        else:
                            activated.wait(pe, b, n - 3)
                            pe.matmul((psa + psg)[n % 4][:], w1[:, c * P:(c + 1) * P], load.xT[:],
                                      start=True, stop=True).then_inc(hidden.sem, 1)

                def output_of(b, x):
                    e, C_ = order[x]
                    activated.wait(pe, b, first_chunk[x + 1])
                    added.wait(pe, b, max(x - 1, 0))
                    for t in range(NT):
                        for c in range(C_):
                            w2 = Ws2[:, c, :] if e == E else W2[:, e, c, :]
                            mm = pe.matmul(psY[x % 2][:, t, :], act_[x % 2][:, c, t:T:NT], w2,
                                           start=(c == 0), stop=(c == C_ - 1))
                    mm.then_inc(yielded.sem, 1)

                load.tensor(pe, 0)
                with turns(pe, B) as b:
                    load.xT_ready.wait(pe, b)
                    added.wait(pe, b - 1)
                    for t in range(NT):
                        mm = pe.matmul(psR[:, t * E:(t + 1) * E], load.xT[:, t:T:NT], Wr[:], start=True, stop=True)
                    mm.then_inc(scored.sem, 1)
                    for x in range(NX):
                        hidden_of(b, x)
                        if x:
                            output_of(b, x - 1)
                        if x == 3 and gated:
                            routed.wait(pe, b)
                            for t in range(NT):
                                mm = pe.transpose(psR[0:E + 1, t * P:(t + 1) * P], w[:, t, :], G.ident[:])
                            mm.then_inc(turned_w.sem, 1)
                        if x == 5 and gated:
                            copied_w.wait(pe, b)
                            for t in range(NT):
                                mm = pe.matmul(psR[:, t * P:(t + 1) * P], wT[:, t, :], b2[:], start=True, stop=True)
                            mm.then_inc(biased.sem, 1)
                    load.tensor(pe, b + 1)
                    output_of(b, NX - 1)

            @block.vector
            def _(dve):
                dve.wait_ge(small_in, nsmall)
                dve.wait_ge(ones, 1)

                def rank(b):
                    c = Chain(ranked, dve, b)
                    scored.wait(dve, b)
                    c.step(dve.tensor_tensor(logits[:], psR[:, 0:NT * E].rearrange("p (t e) -> p t e", t=NT),
                                             br[:].unsqueeze(1).broadcast_to([P, NT, E]), ALU.add))
                    c.wait()
                    stand(dve, post.passed)
                    for t in range(NT):
                        last = dve.max(top[:, t, :], logits[:, t, :])
                    c.step(last)
                    c.wait()
                    stand(dve, post.passed)
                    for t in range(NT):
                        last = dve.max_index(index[:, t, :], top[:, t, :], logits[:, t, :])
                    c.step(last)
                    tanhed.wait(dve, b - 1)
                    c.step(dve.tensor_tensor(margin[:], top[:, :, 0], top[:, :, 1], ALU.subtract))
                    c.wait()
                    c.step(dve.tensor_copy(indexf[:], index[:, :, 0:2]))
                    c.end()

                def route(b):
                    c = Chain(routed, dve, b)
                    tanhed.wait(dve, b)
                    ranked.wait(dve, b)
                    if gated:
                        turned_w.wait(dve, b - 1)
                    for i, half in enumerate((0.5, -0.5)):
                        dve.tensor_scalar(share[:, i, :], th[:, :, 0], half, 0.5, ALU.mult, ALU.add)
                    for i in range(2):
                        last = dve.tensor_tensor(hit[:, i, :, :], iota[:].unsqueeze(1).broadcast_to([P, NT, E]),
                                                 indexf[:, :, i:i + 1].broadcast_to([P, NT, E]), ALU.is_equal)
                    c.step(last)
                    c.wait()
                    for i in range(2):
                        c.step(dve.tensor_tensor(hit[:, i, :, :], hit[:, i, :, :],
                                                 share[:, i, :].unsqueeze(2).broadcast_to([P, NT, E]), ALU.mult))
                    c.wait()
                    c.step(dve.tensor_tensor(w[:, :, 0:E], hit[:, 0, :, :], hit[:, 1, :, :], ALU.add))
                    c.wait()
                    if not gated:
                        c.step(dve.tensor_reduce(through[:], w[:, :, 8:E], AX.X, ALU.add))
                        c.wait()
                        load.x_kept.wait(dve, b)
                        c.step(dve.tensor_tensor(acc[:], batch(G.X, b),
                                                 through[:].unsqueeze(2).broadcast_to([P, NT, P]), ALU.mult))
                        c.wait()
                    c.end()

                def add(b, x):
                    e, _ = order[x]
                    yielded.wait(dve, b, x + 1)
                    if x:
                        added.wait(dve, b, x)
                    for t in range(NT):
                        if e == E:
                            last = dve.tensor_copy(acc[:, t, :], psY[x % 2][:, t, :])
                        else:
                            last = dve.scalar_tensor_tensor(out=acc[:, t, :], in0=psY[x % 2][:, t, :],
                                                            scalar=w[:, t, e:e + 1], in1=acc[:, t, :],
                                                            op0=ALU.mult, op1=ALU.add)
                    last.then_inc(added.sem, 1)

                load.vector(dve, 0, [hidden, scored])
                with turns(dve, B) as b:
                    for x in range(NX):
                        e, C_ = order[x]
                        if gated:
                            for c in range(C_):
                                n = first_chunk[x] + c
                                hidden.wait(dve, b, n + 1)
                                gelued.wait(dve, b, n + 1)
                                yielded.wait(dve, b, max(x - 1, 0))
                                bias = bs1[:, c:c + 1] if e == E else b1[:, e, c:c + 1]
                                dve.scalar_tensor_tensor(out=act_[x % 2][:, c, :], in0=psa[n % 2][:], scalar=bias,
                                                         in1=gate[n % 2][:], op0=ALU.add, op1=ALU.mult)\
                                   .then_inc(activated.sem, 1)
                        if x == 0:
                            rank(b)
                        if x == 1:
                            route(b)
                        if x:
                            add(b, x - 1)
                        if x == 4 and gated:
                            turned_w.wait(dve, b)
                            biased.wait(dve, b - 1)
                            dve.tensor_copy(wT[:], psR[0:E + 1, :].rearrange("e (t p) -> e t p", t=NT))\
                               .then_inc(copied_w.sem, 1)
                    load.vector(dve, b + 1, [hidden, scored])
                    add(b, NX - 1)
                    added.wait(dve, b, NX)
                    if gated:
                        biased.wait(dve, b)
                        dve.tensor_tensor(acc[:], acc[:], psR[:].rearrange("p (t d) -> p t d", t=NT), ALU.add)\
                           .then_inc(added.sem, 1)
                    else:
                        dve.sem_inc(added.sem, 1)
                    load.x_kept.wait(dve, b)
                    added.wait(dve, b, NX + 1)
                    x_ = batch(G.X, b)
                    dve.tensor_tensor(x_, acc[:], x_, ALU.add).then_inc(post.summed.sem, 1)
                    post.summed.wait(dve, b)
                    dve.sem_inc(added.sem, 1)
                    post.vector(dve, b, x_)



def restat(nc, G, tag):
    with ExitStack() as ctx:
        m = Stage(nc, ctx, tag)
        post = Post(m, G)
        finished = m.sem("finished")
        m.credit()
        with nc.Block() as block:
            @block.scalar
            def _(act):
                act.preload_act_table(ACT.Identity)
                with turns(act, B) as b:
                    x = batch(G.X, b)
                    for t in range(NT):
                        last = act.activation(x[:, t, :], x[:, t, :], ACT.Identity,
                                              scale=G.rstd[:, bass.ds(b, 1), t], bias=G.shift[:, bass.ds(b, 1), t])
                    last.then_inc(post.summed.sem, 1)

            @block.vector
            def _(dve):
                with turns(dve, B) as b:
                    post.vector(dve, b, batch(G.X, b))

            @block.gpsimd
            def _(pool):
                post.finish(pool, finished)


def linear_attention_stage(nc, G, tag, a):
    restat(nc, G, tag + "s")
    DH, PAIRS, W_ = 64, 8, 65
    RING = [0, 1, 2, 0, 1, 2, 0, 1]

    def before(r):
        return max(k for k in range(r - PAIRS, r) if RING[k % PAIRS] == RING[r])

    EPS_DEN = 1e-6
    with ExitStack() as ctx:
        m = Stage(nc, ctx, tag)
        gain, offset = m.sb("gain", [P, 1]), m.sb("offset", [P, 1])
        load, post = Load(m, G, G.X, affine=(gain, offset)), Post(m, G)
        Wq, Wk, Wv = (m.sb(n, [P, PAIRS * P]) for n in ("Wq", "Wk", "Wv"))
        Wo = m.sb("Wo", [P, PAIRS, P])
        causal = m.sb("causal", [P, P])
        VA = m.sb("VA", [P, NT, H, W_])
        ex = [m.sb(f"ex{i}", [P, T]) for i in range(2)]
        re = [m.sb(f"re{i}", [P, T]) for i in range(2)]
        Q = [[m.sb(f"Q{i}{h}", [P, T]) for h in range(2)] for i in range(3)]
        K = [m.sb(f"K{i}", [P, T]) for i in range(2)]
        Kt = [m.sb(f"Kt{i}", [P, NT, P]) for i in range(2)]
        AT = [[m.sb(f"AT{i}{h}", [P, NT, P]) for h in range(2)] for i in range(2)]
        S = [m.sb(f"S{i}", [P, 3, 2 * W_]) for i in range(2)]
        den = [m.sb(f"den{i}", [P, 4, 1]) for i in range(2)]
        o = m.sb("o", [P, NT, PAIRS * P])
        oT = m.sb("oT", [P, PAIRS, T])
        psQ, psK = m.ps("psQ", [P, T]), m.ps("psK", [P, T])
        psA = [m.ps(f"psA{i}", [P, T]) for i in range(2)]
        psN = [m.ps(f"psN{i}", [P, T]) for i in range(2)]
        psM = m.ps("psM", [P, T])
        v_made = m.flag("v_made", 8)
        v_copied = m.flag("v_copied", 8)
        qk_made = m.flag("qk_made", 16)
        qk_exped = m.flag("qk_exped", 32)
        phi = m.flag("phi", 24)
        inner = m.flag("inner", 16)
        masked = m.flag("masked", 16)
        k_turned = m.flag("k_turned", 8)
        k_copied = m.flag("k_copied", 8)
        state = m.flag("state", 24)
        state_copied = m.flag("state_copied", 24)
        numbered = m.flag("numbered", 16)
        divided = m.flag("divided", 48)
        o_turned = m.flag("o_turned", 8)
        o_copied = m.flag("o_copied", 8)
        projected = m.flag("projected", 1)
        loaded, cleared, finished = m.sem("loaded"), m.sem("cleared"), m.sem("finished")
        m.credit()
        with nc.Block() as block:
            @block.sync
            def _(sp):
                col = lambda v: v.rearrange("(p a) -> p a", a=1)
                sp.dma_start(gain[:], col(a["L1_attn_ln1_g"])).then_inc(loaded, 16)
                sp.dma_start(offset[:], col(a["L1_attn_ln1_b"])).then_inc(loaded, 16)
                sp.dma_start(Wv[:], a["L1_attn_Wv"]).then_inc(loaded, 16)
                sp.dma_start(Wq[:], a["L1_attn_Wq"]).then_inc(loaded, 16)
                sp.dma_start(Wk[:], a["L1_attn_Wk"]).then_inc(loaded, 16)
                sp.dma_start(causal[:], a["c_causal"]).then_inc(loaded, 16)
                sp.dma_start(Wo[:], a["L1_attn_Wo"].rearrange("(c p) d -> p c d", p=P)).then_inc(loaded, 16)
                sp.wait_ge(loaded, 112)

            @block.gpsimd
            def _(pool):
                for pair in Q:
                    for tile in pair:
                        pool.memset(tile[:], 0.0)
                pool.memset(VA[:, :, :, DH:W_], 1.0).then_inc(cleared, 1)
                load.xs_ready.wait(pool, 0)
                pool.sem_inc(load.x_kept.sem, 1)
                with turns(pool, B) as b:
                    load.xs_ready.wait(pool, b + 1)
                    pool.sem_inc(load.x_kept.sem, 1)
                post.finish(pool, finished)

            @block.tensor
            def _(pe):
                pe.wait_ge(loaded, 112)
                pe.wait_ge(cleared, 1)

                def project_pair(b, r):
                    qk_exped.wait(pe, b, 4 * r)
                    pe.matmul(psQ[:], Wq[:, r * P:(r + 1) * P], load.xT[:], start=True, stop=True)\
                      .then_inc(qk_made.sem, 1)
                    pe.matmul(psK[:], Wk[:, r * P:(r + 1) * P], load.xT[:], start=True, stop=True)\
                      .then_inc(qk_made.sem, 1)

                def inner_products(b, r, h):
                    phi.wait(pe, b, 3 * r + 3)
                    masked.wait(pe, b, 2 * r + h - 1)
                    for c in range(NT):
                        tok = slice(c * P, (c + 1) * P)
                        mm = pe.matmul(psA[h][:, tok], K[r % 2][:, tok], Q[RING[r]][h][:, tok],
                                       start=True, stop=True)
                    mm.then_inc(inner.sem, 1)

                def turn_keys(b, r):
                    load.xT_ready.wait(pe, b)
                    k_copied.wait(pe, b, r)
                    for c in range(NT):
                        tok = slice(c * P, (c + 1) * P)
                        mm = pe.transpose(load.psX[:, tok], K[r % 2][:, tok], G.ident[:])
                    mm.then_inc(k_turned.sem, 1)

                def states(b, r, c):
                    if c == 0:
                        k_copied.wait(pe, b, r + 1)
                    state_copied.wait(pe, b, 3 * r + c)
                    rhs = VA[:, c, 2 * r:2 * r + 2, :].rearrange("p h w -> p (h w)")
                    pe.matmul(psM[:, 0:2 * W_], Kt[r % 2][:, c, :], rhs, start=(c == 0), stop=(c == 2),
                              skip_group_check=True).then_inc(state.sem, 1)

                def numerators(b, r, half):
                    if half == 0:
                        masked.wait(pe, b, 2 * r + 2)
                    state_copied.wait(pe, b, 3 * r + (1 if half == 0 else 3))
                    n = 2 * r + half
                    divided.wait(pe, b, 3 * (n - 1))
                    if n == 0:
                        post.summed.wait(pe, b - 1)
                    for i in range(2):
                        c = 2 * half + i
                        for h in range(2):
                            out = psN[half][:, (2 * i + h) * W_:(2 * i + h + 1) * W_]
                            mm = pe.matmul(out, AT[r % 2][h][:, c, :], VA[:, c, 2 * r + h, :], start=True,
                                           stop=(c == 0))
                            if c:
                                mm = pe.matmul(out, Q[RING[r]][h][:, c * P:(c + 1) * P],
                                               S[r % 2][:, c - 1, h * W_:(h + 1) * W_], start=False, stop=True)
                    mm.then_inc(numbered.sem, 1)

                load.tensor(pe, 0)
                with turns(pe, B) as b:
                    load.xT_ready.wait(pe, b)
                    project_pair(b, 0)
                    for n in range(8):
                        v_copied.wait(pe, b, n - 1)
                        pe.matmul(psA[n % 2][:], load.xT[:, (n // 2) * P:(n // 2 + 1) * P],
                                  Wv[:, (n % 2) * T:(n % 2 + 1) * T], start=True, stop=True).then_inc(v_made.sem, 1)
                    v_copied.wait(pe, b)
                    for r in range(PAIRS + 1):
                        if r + 1 < PAIRS:
                            project_pair(b, r + 1)
                        if r:
                            states(b, r - 1, 0)
                        if r < PAIRS:
                            inner_products(b, r, 0)
                        if r:
                            if r == PAIRS:
                                k_copied.wait(pe, b)
                                load.tensor(pe, b + 1)
                            states(b, r - 1, 1)
                        if r < PAIRS:
                            inner_products(b, r, 1)
                        elif r:
                            numerators(b, r - 1, 0)
                        if r:
                            states(b, r - 1, 2)
                        if r < PAIRS:
                            turn_keys(b, r)
                        if r:
                            if r < PAIRS:
                                numerators(b, r - 1, 0)
                            numerators(b, r - 1, 1)
                    for r in range(PAIRS):
                        if r == 0:
                            divided.wait(pe, b)
                            masked.wait(pe, b)
                        o_copied.wait(pe, b, r - 1)
                        for c in range(NT):
                            tok = slice(c * P, (c + 1) * P)
                            mm = pe.transpose(psA[r % 2][:, tok], o[:, c, r * P:(r + 1) * P], G.ident[:])
                        mm.then_inc(o_turned.sem, 1)
                    o_copied.wait(pe, b)
                    for t in range(NT):
                        for r in range(PAIRS):
                            mm = pe.matmul(psN[0][:, t * P:(t + 1) * P], oT[:, r, t:T:NT], Wo[:, r, :],
                                           start=(r == 0), stop=(r == PAIRS - 1))
                    mm.then_inc(projected.sem, 1)

            @block.scalar
            def _(act):
                act.preload_act_table(ACT.Exp)
                act.wait_ge(cleared, 1)
                def features(b, r):
                    for i, ps in enumerate((psQ, psK)):
                        qk_made.wait(act, b, 2 * r + i + 1)
                        phi.wait(act, b, 3 * r - (1 if i == 0 else 0))
                        act.activation(ex[i][:], ps[:], ACT.Exp).then_inc(qk_exped.sem, 1)
                        act.activation(re[i][:], ps[:], ACT.Relu).then_inc(qk_exped.sem, 1)

                def state_copy(b, r, c):
                    state.wait(act, b, 3 * r + c + 1)
                    numbered.wait(act, b, 2 * r - 2)
                    act.activation(S[r % 2][:, c, :], psM[:, 0:2 * W_], ACT.Copy).then_inc(state_copied.sem, 1)

                load.scalar(act, 0)
                with turns(act, B) as b:
                    features(b, 0)
                    for n in range(8):
                        v_made.wait(act, b, n + 1)
                        if n == 0:
                            numbered.wait(act, b - 1)
                            state.wait(act, b - 1)
                        act.activation(VA[:, n // 2, 8 * (n % 2):8 * (n % 2) + 8, 0:DH],
                                       psA[n % 2][:].rearrange("p (h d) -> p h d", d=DH),
                                       ACT.Copy).then_inc(v_copied.sem, 1)
                    for r in range(PAIRS + 1):
                        if r + 1 < PAIRS:
                            features(b, r + 1)
                        if r:
                            for c in range(3):
                                state_copy(b, r - 1, c)
                        if r < PAIRS:
                            k_turned.wait(act, b, r + 1)
                            state.wait(act, b, 3 * r - 3)
                            act.activation(Kt[r % 2][:], load.psX[:].rearrange("p (c d) -> p c d", c=NT),
                                           ACT.Copy).then_inc(k_copied.sem, 1)
                        if r == 1:
                            load.scalar(act, b + 1)
                    for r in range(0, PAIRS, 2):
                        o_turned.wait(act, b, r + 1)
                        if r == 0:
                            projected.wait(act, b - 1)
                        act.activation(oT[:, r, :], psA[0][:], ACT.Copy).then_inc(o_copied.sem, 1)
                        o_turned.wait(act, b, r + 2)
                        act.activation(oT[:, r + 1, :], psA[1][:], ACT.Copy).then_inc(o_copied.sem, 1)

            @block.vector
            def _(dve):
                dve.wait_ge(loaded, 112)
                dve.wait_ge(cleared, 1)
                xT_users = [v_made, qk_made, k_copied]
                load.vector(dve, 0, xT_users)
                with turns(dve, B) as b:
                    def features(r):
                        qk_exped.wait(dve, b, 4 * r + 2)
                        numbered.wait(dve, b, 2 * before(r) + 2)
                        for h in range(2):
                            rows = slice(DH * h, DH * (h + 1))
                            dve.scalar_tensor_tensor(out=Q[RING[r]][h][rows, :], in0=ex[0][rows, :], scalar=1.0,
                                                     in1=re[0][rows, :], op0=ALU.min, op1=ALU.add)\
                               .then_inc(phi.sem, 1)
                        qk_exped.wait(dve, b, 4 * r + 4)
                        inner.wait(dve, b, 2 * r - 2)
                        k_turned.wait(dve, b, r - 1)
                        dve.scalar_tensor_tensor(out=K[r % 2][:], in0=ex[1][:], scalar=1.0, in1=re[1][:],
                                                 op0=ALU.min, op1=ALU.add).then_inc(phi.sem, 1)

                    def mask(r):
                        for h in range(2):
                            inner.wait(dve, b, 2 * r + h + 1)
                            numbered.wait(dve, b, 2 * r - 2)
                            dve.tensor_tensor(AT[r % 2][h][:], psA[h][:].rearrange("p (c i) -> p c i", c=NT),
                                              causal[:].unsqueeze(1).broadcast_to([P, NT, P]), ALU.mult)\
                               .then_inc(masked.sem, 1)

                    def divide(r, half):
                        n = 2 * r + half
                        numbered.wait(dve, b, n + 1)
                        if n == 0:
                            o_turned.wait(dve, b - 1)
                        ps = psN[half][:, 0:4 * W_].rearrange("p (q w) -> p q w", w=W_)
                        dve.tensor_scalar(den[half][:], ps[:, :, DH:W_], EPS_DEN, None, ALU.max)\
                           .then_inc(divided.sem, 1)
                        divided.wait(dve, b, 3 * n + 1)
                        dve.reciprocal(den[half][:], den[half][:]).then_inc(divided.sem, 1)
                        divided.wait(dve, b, 3 * n + 2)
                        dst = o[:, 2 * half:2 * half + 2, r * P:(r + 1) * P].rearrange("p c (h d) -> p c h d", h=2)
                        num = psN[half][:, 0:4 * W_].rearrange("p (c h w) -> p c h w", c=2, h=2)
                        d4 = den[half][:].rearrange("p (c h) a -> p c h a", c=2)
                        dve.tensor_tensor(dst, num[:, :, :, 0:DH], d4.broadcast_to([P, 2, 2, DH]), ALU.mult)\
                           .then_inc(divided.sem, 1)

                    features(0)
                    for r in range(PAIRS + 1):
                        if r + 1 < PAIRS:
                            features(r + 1)
                        if r < PAIRS:
                            mask(r)
                        else:
                            load.vector(dve, b + 1, xT_users)
                        if r:
                            divide(r - 1, 0)
                            divide(r - 1, 1)
                    projected.wait(dve, b)
                    x1 = batch(G.X1, b)
                    dve.tensor_tensor(x1, psN[0][:].rearrange("p (t d) -> p t d", t=NT), batch(G.X, b), ALU.add)\
                       .then_inc(post.summed.sem, 1)
                    post.vector(dve, b, x1)



def gelu_stage(nc, G, tag, a):
    C = 4
    with ExitStack() as ctx:
        m = Stage(nc, ctx, tag)
        gain, offset = m.sb("gain", [P, 1]), m.sb("offset", [P, 1])
        load, post = Load(m, G, G.X1, affine=(gain, offset)), Post(m, G)
        W1, W2 = m.sb("W1", [P, C * P]), m.sb("W2", [P, C, P])
        act_ = [m.sb(f"act{i}", [P, C, T]) for i in range(1)]
        base = m.sb("base", [P, NT, P])
        psH = [m.ps(f"psH{i}", [P, T]) for i in range(2)]
        psY = m.ps("psY", [P, NT, P])
        hidden = m.flag("hidden", C)
        activated = m.flag("activated", C)
        projected = m.flag("projected", 1)
        base_ready = m.flag("base_ready", 1)
        loaded, finished = m.sem("loaded"), m.sem("finished")
        m.credit()
        with nc.Block() as block:
            @block.sync
            def _(sp):
                col = lambda v: v.rearrange("(p a) -> p a", a=1)
                sp.dma_start(gain[:], col(a["L1_attn_ln2_g"])).then_inc(loaded, 16)
                sp.dma_start(offset[:], col(a["L1_attn_ln2_b"])).then_inc(loaded, 16)
                sp.dma_start(W1[:], a["L1_attn_Wf1"]).then_inc(loaded, 16)
                sp.dma_start(W2[:], a["L1_attn_Wf2"].rearrange("(c p) d -> p c d", p=P)).then_inc(loaded, 16)
                sp.wait_ge(loaded, 64)

            @block.scalar
            def _(act):
                act.preload_act_table(ACT.Gelu)
                load.scalar(act, 0)
                with turns(act, B) as b:
                    load.scalar(act, b + 1)
                    for c in range(C):
                        hidden.wait(act, b, c + 1)
                        projected.wait(act, b - 1)
                        act.activation(act_[0][:, c, :], psH[c % 2][:], ACT.Gelu).then_inc(activated.sem, 1)

            @block.gpsimd
            def _(pool):
                pool.sem_inc(load.x_kept.sem, 1)
                with turns(pool, B) as b:
                    load.xs_ready.wait(pool, b)
                    pool.sem_inc(load.x_kept.sem, 1)
                    post.summed.wait(pool, b - 1)
                    pool.tensor_tensor(base[:], batch(G.X, b), batch(G.X1, b), ALU.add).then_inc(base_ready.sem, 1)
                post.finish(pool, finished)

            @block.tensor
            def _(pe):
                pe.wait_ge(loaded, 64)
                load.tensor(pe, 0)
                with turns(pe, B) as b:
                    load.xT_ready.wait(pe, b)
                    for c in range(C):
                        activated.wait(pe, b, c - 1)
                        pe.matmul(psH[c % 2][:], W1[:, c * P:(c + 1) * P], load.xT[:], start=True, stop=True)\
                          .then_inc(hidden.sem, 1)
                    load.tensor(pe, b + 1)
                    activated.wait(pe, b)
                    post.summed.wait(pe, b - 1)
                    for t in range(NT):
                        for c in range(C):
                            mm = pe.matmul(psY[:, t, :], act_[0][:, c, t:T:NT], W2[:, c, :],
                                           start=(c == 0), stop=(c == C - 1))
                    mm.then_inc(projected.sem, 1)

            @block.vector
            def _(dve):
                dve.wait_ge(loaded, 64)
                load.vector(dve, 0, [hidden])
                with turns(dve, B) as b:
                    load.vector(dve, b + 1, [hidden])
                    projected.wait(dve, b)
                    base_ready.wait(dve, b)
                    x = batch(G.X, b)
                    dve.tensor_tensor(x, psY[:], base[:], ALU.add).then_inc(post.summed.sem, 1)
                    post.vector(dve, b, x)


def ternary_stage(nc, G, tag, a):
    C, F = 4, 512
    with ExitStack() as ctx:
        m = Stage(nc, ctx, tag)
        load, post = Load(m, G, G.X), Post(m, G)
        Wfc, Wp = m.sb("Wfc", [P, F]), m.sb("Wp", [P, F])
        above, below = m.sb("above", [P, F]), m.sb("below", [P, F])
        size, half = m.sb("size", [P, 2]), m.sb("half", [P, 2, 2])
        ones = m.sb("ones", [P, P])
        gain, offset = m.sb("gain", [P, C]), m.sb("offset", [P, C])
        h = m.sb("h", [P, NT, F])
        hT = m.sb("hT", [P, C, T])
        st, mv = m.sb("st", [P, NT, 6]), m.sb("mvh", [P, NT, 2])
        rs, sh = m.sb("rs", [P, NT]), m.sb("sh", [P, NT])
        psH = [m.ps(f"psH{i}", [P, F]) for i in range(2)]
        psT = [m.ps(f"psT{i}", [P, T]) for i in range(2)]
        psY = m.ps("psY", [P, NT, P])
        hidden = m.flag("hidden", NT)
        geluted = m.flag("geluted", NT)
        stat = m.flag("statted", NT)
        aggregated = m.flag("aggr", 1)
        scaled = m.flag("scaled", 4)
        pool_passed = m.sem("pool_passed")
        normed = m.flag("normed", NT)
        turned_h = m.flag("turned_h", C)
        copied = m.flag("copied", C)
        projected = m.flag("projected", 1)
        loaded, finished, prep, filled, summed = (m.sem(n) for n in ("loaded", "finished", "prep", "filled", "sizes"))
        m.credit()
        with nc.Block() as block:
            @block.sync
            def _(sp):
                sp.dma_start(Wfc[:], a["L1_ffn_W_fc"]).then_inc(loaded, 16)
                sp.dma_start(Wp[:].rearrange("p (c d) -> p c d", c=C),
                             a["L1_ffn_W_proj"].rearrange("(c p) d -> p c d", p=P)).then_inc(loaded, 16)
                sp.dma_start(gain[:], a["L1_ln_w"]).then_inc(loaded, 16)
                sp.dma_start(offset[:], a["L1_ln_b"]).then_inc(loaded, 16)
                sp.wait_ge(loaded, 64)

            @block.vector
            def _(dve):
                dve.memset(ones[:], 1.0).then_inc(filled, 1)
                dve.wait_ge(loaded, 64)
                for i, w in enumerate((Wfc, Wp)):
                    dve.tensor_reduce(size[:, i:i + 1], w[:], AX.X, ALU.add, apply_absolute_value=True)\
                       .then_inc(filled, 1)
                dve.wait_ge(summed, 1)
                dve.tensor_scalar(half[:, 0, :], psY[:, 0, 0:2], 1.0 / (P * F), 1e-6, ALU.mult, ALU.add)\
                   .then_inc(prep, 1)
                dve.wait_ge(prep, 1)
                dve.tensor_scalar(half[:, 1, :], half[:, 0, :], -0.5, None, ALU.mult).then_inc(prep, 1)
                dve.wait_ge(prep, 2)
                dve.tensor_scalar(half[:, 0, :], half[:, 0, :], 0.5, None, ALU.mult).then_inc(prep, 1)
                dve.wait_ge(prep, 3)
                for i, w in enumerate((Wfc, Wp)):
                    dve.wait_ge(prep, 3 + 3 * i)
                    dve.tensor_scalar(above[:], w[:], half[:, 0, i:i + 1], None, ALU.is_gt).then_inc(prep, 1)
                    dve.tensor_scalar(below[:], w[:], half[:, 1, i:i + 1], None, ALU.is_lt).then_inc(prep, 1)
                    dve.wait_ge(prep, 5 + 3 * i)
                    dve.tensor_tensor(w[:], above[:], below[:], ALU.subtract).then_inc(prep, 1)

            @block.tensor
            def _(pe):
                pe.wait_ge(filled, 3)
                pe.matmul(psY[:, 0, 0:2], ones[:], size[:], start=True, stop=True).then_inc(summed, 1)

        with nc.Block() as block:
            @block.scalar
            def _(act):
                act.preload_act_table(ACT.Gelu)
                load.scalar(act, 0)
                with turns(act, B) as b:
                    for t in range(NT):
                        hidden.wait(act, b, t + 1)
                        turned_h.wait(act, b - 1)
                        act.activation(h[:, t, :], psH[t % 2][:], ACT.Gelu).then_inc(geluted.sem, 1)
                    load.scalar(act, b + 1)
                    scaled.wait(act, b)
                    for t in range(NT):
                        act.activation(h[:, t, :], h[:, t, :], ACT.Identity, scale=rs[:, t:t + 1],
                                       bias=sh[:, t:t + 1]).then_inc(normed.sem, 1)

            @block.gpsimd
            def _(pool):
                load.pool(pool, 0)
                with turns(pool, B) as b:
                    c = Chain(scaled, pool, b)
                    aggregated.wait(pool, b)
                    normed.wait(pool, b - 1)
                    stand(pool, pool_passed)
                    c.step(pool.tensor_scalar(rs[:], mv[:, :, 1], LN_EPS, None, ALU.add))
                    c.wait()
                    c.step(pool.tensor_tensor(rs[:], rs[:], G.minus_half[:, 0, :], ALU.pow))
                    c.wait()
                    c.step(pool.tensor_tensor(sh[:], mv[:, :, 0], rs[:], ALU.mult))
                    c.wait()
                    stand(pool, pool_passed)
                    c.step(pool.tensor_scalar(sh[:], sh[:], -1.0, None, ALU.mult))
                    c.end()
                    load.pool(pool, b + 1)
                post.finish(pool, finished)

            @block.tensor
            def _(pe):
                load.tensor(pe, 0)
                with turns(pe, B) as b:
                    load.xT_ready.wait(pe, b)
                    for t in range(NT):
                        geluted.wait(pe, b, t - 1)
                        pe.matmul(psH[t % 2][:], load.xT[:, t:T:NT], Wfc[:], start=True, stop=True)\
                          .then_inc(hidden.sem, 1)
                    load.tensor(pe, b + 1)
                    normed.wait(pe, b)
                    for c in range(C):
                        copied.wait(pe, b, c - 1)
                        for t in range(NT):
                            mm = pe.transpose(psT[c % 2][:, t * P:(t + 1) * P], h[:, t, c * P:(c + 1) * P],
                                              G.ident[:])
                        mm.then_inc(turned_h.sem, 1)
                    copied.wait(pe, b)
                    post.summed.wait(pe, b - 1)
                    for t in range(NT):
                        for c in range(C):
                            mm = pe.matmul(psY[:, t, :], hT[:, c, t * P:(t + 1) * P], Wp[:, c * P:(c + 1) * P],
                                           start=(c == 0), stop=(c == C - 1))
                    mm.then_inc(projected.sem, 1)

            @block.vector
            def _(dve):
                load.vector(dve, 0, [hidden])
                with turns(dve, B) as b:
                    for t in range(NT):
                        geluted.wait(dve, b, t + 1)
                        stand(dve, post.passed)
                        dve.bn_stats(st[:, t, :], h[:, t, :]).then_inc(stat.sem, 1)
                    stat.wait(dve, b)
                    scaled.wait(dve, b - 1)
                    stand(dve, post.passed)
                    for t in range(NT):
                        last = dve.bn_aggr(mv[:, t, :], st[:, t, :])
                    last.then_inc(aggregated.sem, 1)
                    load.vector(dve, b + 1, [hidden])
                    for c in range(C):
                        turned_h.wait(dve, b, c + 1)
                        projected.wait(dve, b - 1)
                        dve.tensor_scalar(hT[:, c, :], psT[c % 2][:], gain[:, c:c + 1], offset[:, c:c + 1],
                                          ALU.mult, ALU.add).then_inc(copied.sem, 1)
                    projected.wait(dve, b)
                    load.x_kept.wait(dve, b)
                    x = batch(G.X, b)
                    dve.tensor_tensor(x, psY[:], x, ALU.add).then_inc(post.summed.sem, 1)
                    post.vector(dve, b, x)


def fourier_stage(nc, G, tag, a):
    with ExitStack() as ctx:
        m = Stage(nc, ctx, tag)
        load, post = Load(m, G, G.X), Post(m, G)
        Wr, Wi, Cc, Ss = (m.sb(n, [P, P]) for n in ("Wr", "Wi", "cos", "sin"))
        nS = m.sb("nsin", [P, P])
        Ur, nUi, M = (m.sb(n, [P, P]) for n in ("Ur", "nUi", "M"))
        bias = m.sb("bias", [P, P])
        base = m.sb("base", [P, NT, P])
        psM = m.ps("psM", [P, 3, P])
        psY = m.ps("psY", [P, NT, P])
        base_ready = m.flag("base_ready", 1)
        projected = m.flag("projected", 1)
        loaded, finished, made, kept = (m.sem(n) for n in ("loaded", "finished", "made", "kept"))
        m.credit()
        with nc.Block() as block:
            @block.sync
            def _(sp):
                for dst, n in ((Wr, "L3_ffn_w_freq_real"), (Wi, "L3_ffn_w_freq_imag"), (Cc, "c_cos"), (Ss, "c_sin")):
                    sp.dma_start(dst[:], a[n]).then_inc(loaded, 16)
                sp.dma_start(bias[:], a["L3_ffn_bias"].rearrange("(a n) -> a n", a=1).broadcast_to([P, P]))\
                  .then_inc(loaded, 16)
                sp.wait_ge(loaded, 80)

            @block.tensor
            def _(pe):
                pe.wait_ge(loaded, 80)
                pe.wait_ge(kept, 1)
                pe.matmul(psM[:, 0, :], Wr[:], Cc[:], start=True, stop=False)
                pe.matmul(psM[:, 0, :], Wi[:], Ss[:], start=False, stop=True).then_inc(made, 1)
                pe.wait_ge(kept, 2)
                pe.matmul(psM[:, 1, :], Wr[:], Ss[:], start=True, stop=False)
                pe.matmul(psM[:, 1, :], Wi[:], nS[:], start=False, stop=True).then_inc(made, 1)
                pe.wait_ge(kept, 3)
                pe.matmul(psM[:, 2, :], Ur[:], Cc[:], start=True, stop=False)
                pe.matmul(psM[:, 2, :], nUi[:], Ss[:], start=False, stop=True).then_inc(made, 1)

            @block.vector
            def _(dve):
                dve.wait_ge(loaded, 80)
                dve.tensor_scalar(nS[:], Cc[:], -1.0, None, ALU.mult).then_inc(kept, 1)
                dve.wait_ge(made, 1)
                dve.tensor_copy(Ur[:], psM[:, 0, :]).then_inc(kept, 1)
                dve.wait_ge(made, 2)
                dve.tensor_copy(nUi[:], psM[:, 1, :]).then_inc(kept, 1)
                dve.wait_ge(made, 3)
                dve.tensor_scalar(M[:], psM[:, 2, :], 1.0 / P, None, ALU.mult).then_inc(kept, 1)

        with nc.Block() as block:
            @block.scalar
            def _(act):
                act.preload_act_table(ACT.Identity)
                load.scalar(act, 0)
                with turns(act, B) as b:
                    load.scalar(act, b + 1)

            @block.gpsimd
            def _(pool):
                with turns(pool, B) as b:
                    load.xs_ready.wait(pool, b)
                    post.summed.wait(pool, b - 1)
                    pool.tensor_tensor(base[:], load.xs[:], bias[:].unsqueeze(1).broadcast_to([P, NT, P]), ALU.add)\
                        .then_inc(base_ready.sem, 1)
                    base_ready.wait(pool, b)
                    pool.sem_inc(load.x_kept.sem, 1)
                post.finish(pool, finished)

            @block.tensor
            def _(pe):
                load.tensor(pe, 0)
                with turns(pe, B) as b:
                    load.xT_ready.wait(pe, b)
                    post.summed.wait(pe, b - 1)
                    for t in range(NT):
                        mm = pe.matmul(psY[:, t, :], load.xT[:, t:T:NT], M[:], start=True, stop=True)
                    mm.then_inc(projected.sem, 1)
                    load.tensor(pe, b + 1)

            @block.vector
            def _(dve):
                load.vector(dve, 0, [projected])
                with turns(dve, B) as b:
                    load.vector(dve, b + 1, [projected])
                    projected.wait(dve, b)
                    base_ready.wait(dve, b)
                    x = batch(G.X, b)
                    dve.tensor_tensor(x, psY[:], base[:], ALU.add).then_inc(post.summed.sem, 1)
                    post.vector(dve, b, x)



def constants():
    i = np.arange(P)
    t = np.arange(T)
    bf = np.dtype("bfloat16") if False else mybir.dt.np(BF16)
    ones = np.ones(T)
    high, low = (t // 256) * 256, t % 256
    kdecay = np.stack([high, low, ones, ones])
    qdecay = np.stack([ones, ones, -high, -low])
    rep = lambda x: np.ascontiguousarray(np.broadcast_to(x[:, None, :], (4, H, T))).astype(bf)
    future = np.where(i[None, :] > i[:, None], MASKED, 0.0)
    masks = np.stack([future, future.T], axis=1).astype(bf)
    angle = 2 * np.pi * ((i[:, None] * i[None, :]) % P) / P
    return {
        "c_ident": np.eye(P, dtype=np.float32),
        "c_qdecay": rep(qdecay),
        "c_kdecay": rep(kdecay),
        "c_masks": masks,
        "c_blocks": (i[:, None] // HD == i[None, :] // HD).astype(np.float32),
        "c_causal": (i[None, :] >= i[:, None]).astype(np.float32),
        "c_cos": np.cos(angle).astype(np.float32),
        "c_sin": np.sin(angle).astype(np.float32),
        "c_iota": np.ascontiguousarray(np.broadcast_to(np.arange(12, dtype=np.float32), (P, 12))),
    }


def layouts(x):
    out = dict(x)
    T_ = lambda w: np.ascontiguousarray(np.swapaxes(w, -1, -2))
    for name in ("L0_attn_Wq", "L0_attn_Wk", "L0_attn_Wv", "L0_attn_Wo", "L2_attn_Wq_w", "L2_attn_Wk_w",
                 "L2_attn_Wv_w", "L1_ffn_W_fc", "L1_ffn_W_proj", "L2_ffn_gate_w", "L2_ffn_w1", "L2_ffn_w2"):
        out[name] = T_(x[name])
    w, b = out.pop("L3_attn_w_qkv"), out.pop("L3_attn_b_qkv")
    for n, side in enumerate("qkv"):
        out[f"L3_w{side}"] = np.ascontiguousarray(w[:, n * P:(n + 1) * P])
        out[f"L3_b{side}"] = np.ascontiguousarray(b[n * P:(n + 1) * P])
    for side in "qv":
        out[f"L3_a{side}T"] = T_(out.pop(f"L3_attn_a_{side}"))
    out["L0_be1"] = np.ascontiguousarray(out.pop("L0_ffn_be1").reshape(12, 6, P).transpose(2, 0, 1))
    out["L0_bs1"] = T_(out.pop("L0_ffn_bs1").reshape(4, P))
    out["L0_b2"] = np.concatenate([out.pop("L0_ffn_be2"), out.pop("L0_ffn_bs2")[None]])
    out["L1_ln_w"], out["L1_ln_b"] = (T_(out.pop(f"L1_ffn_ln_{n}").reshape(4, P)) for n in "wb")
    return out


STAGES = ("A0", "M0", "L1", "F1", "T1", "A2", "M2", "A3", "F3")


def program(nc, a, out, stages=STAGES):
    with ExitStack() as ctx:
        G = setup(nc, ctx, a)
        for s in stages:
            if s == "A0":
                attention_stage(nc, G, s, a, "decay")
            elif s == "A2":
                attention_stage(nc, G, s, a, "cross")
            elif s == "A3":
                attention_stage(nc, G, s, a, "lora")
            elif s == "M0":
                expert_stage(nc, G, s, a, True)
            elif s == "M2":
                expert_stage(nc, G, s, a, False)
            elif s == "L1":
                linear_attention_stage(nc, G, s, a)
            elif s == "F1":
                gelu_stage(nc, G, s, a)
            elif s == "T1":
                ternary_stage(nc, G, s, a)
            elif s == "F3":
                fourier_stage(nc, G, s, a)
        store(nc, G, out)


def store(nc, G, out):
    with ExitStack() as ctx:
        m = Stage(nc, ctx, "st")
        y = m.sb("y", [P, B, NT, P])
        ready, stored = m.sem("ready"), m.sem("stored")
        with nc.Block() as block:
            @block.scalar
            def _(act):
                act.preload_act_table(ACT.Identity)
                with turns(act, B) as b:
                    for t in range(NT):
                        last = act.activation(batch(y, b)[:, t, :], batch(G.X, b)[:, t, :], ACT.Identity,
                                              scale=G.rstd[:, bass.ds(b, 1), t], bias=G.shift[:, bass.ds(b, 1), t])
                    last.then_inc(ready, 1)

            @block.sync
            def _(sp):
                dst = out.rearrange("b (p t) d -> b p t d", t=NT)
                with turns(sp, B) as b:
                    sp.wait_ge(ready, b + 1)
                    sp.dma_start(dst[bass.ds(b, 1), :, :, :].rearrange("a p t d -> p (a t) d"), batch(y, b))\
                      .then_inc(stored, 16)
                sp.wait_ge(stored, 16 * B)


def kernel(**inputs):
    import concourse.bacc as bacc
    from concourse.bass_utils import run_bass_kernel_spmd

    arrays = {**layouts({k: np.asarray(v) for k, v in inputs.items()}), **constants()}
    nc = bacc.Bacc("TRN2", target_bir_lowering=False, num_devices=1)
    a = {n: nc.dram_tensor(n, v.shape, mybir.dt.from_np(v.dtype), kind="ExternalInput").ap()
         for n, v in arrays.items()}
    out = nc.dram_tensor("out", (B, T, P), F32, kind="ExternalOutput").ap()
    program(nc, a, out)
    return run_bass_kernel_spmd(nc, [arrays], core_ids=[0]).results[0]["out"]
```

```python
from contextlib import ExitStack

import concourse.bass as bass
import numpy as np
from concourse import mybir

F32 = mybir.dt.float32
F32R = mybir.dt.float32r
BF16 = mybir.dt.bfloat16
U32 = mybir.dt.uint32
ALU = mybir.AluOpType
ACT = mybir.ActivationFunctionType
AX = mybir.AxisListType

P = 128
B = 8
T = 512
NT = T // P
H = 16
HD = P // H
GH = 4
NG = H // GH
LN_EPS = 1e-5
MASKED = -1e30

DECAY_ROWS = 4
PARTS = 3
MAX_ROW = 96


class Flag:

    def __init__(self, sem, per, lead=1, first=0):
        self.sem, self.per, self.lead, self.first = sem, per, lead, first

    def upto(self, turn, k):
        return turn * self.per + (self.lead * self.per + k)

    def wait(self, engine, turn, k=None):
        engine.wait_ge(self.sem, self.upto(turn, self.per if k is None else k))


class Chain:

    def __init__(self, signal, engine, turn):
        self.flag, self.engine, self.turn, self.n = signal, engine, turn, 0

    def step(self, instruction):
        self.n += 1
        assert self.n <= self.flag.per, (self.n, self.flag.per)
        instruction.then_inc(self.flag.sem, 1)

    def wait(self):
        self.flag.wait(self.engine, self.turn, self.n)

    def after(self, n):
        self.n = n
        self.wait()

    def end(self):
        assert self.n == self.flag.per, (self.n, self.flag.per)


class Stage:

    left = []

    def __init__(self, nc, ctx, tag):
        self.nc, self.ctx, self.tag, self.flags, self.sems = nc, ctx, tag, [], []

    def sb(self, name, shape, dt=F32):
        return self.ctx.enter_context(self.nc.sbuf_tensor(f"{self.tag}_{name}", shape, dt))

    def ps(self, name, shape):
        return self.ctx.enter_context(self.nc.psum_tensor(f"{self.tag}_{name}", shape, F32))

    def sem(self, name):
        self.sems.append(self.ctx.enter_context(self.nc.semaphore(f"{self.tag}_{name}")))
        return self.sems[-1]

    def flag(self, name, per, lead=1, first=0):
        s = Flag(self.sem(name), per, lead, first)
        self.flags.append(s)
        return s

    def credit(self, function=None):
        left, Stage.left = Stage.left, []
        with self.nc.Block() as block:
            @block.sync
            def _(sp):
                for s in left:
                    sp.sem_clear(s)
                for s in self.flags:
                    if s.lead + s.first:
                        sp.sem_inc(s.sem, (s.lead + s.first) * s.per)

            if function is not None:
                @block.scalar
                def _(act):
                    act.preload_act_table(function)
        self.ctx.callback(self.retire)

    def retire(self):
        Stage.left += self.sems


def stand(engine, passed):
    engine.sem_inc(passed, 1)


def turns(engine, n):
    return engine.Fori(0, n)


def batch(array, b):
    return array[:, bass.ds(b, 1), :, :].rearrange("p a t d -> p (a t) d")



class Pair:

    def __init__(self, m, name, shape):
        self.high, self.low = m.sb(f"{name}_high", shape, F32R), m.sb(f"{name}_low", shape, F32R)

    def cut(self, index):
        return self.high[index], self.low[index]


def products(pe, out, left, right, start, stop):
    pe.matmul(out, left[0], right[1], start=start, stop=False, skip_group_check=True)
    pe.matmul(out, left[0], right[0], start=False, stop=False, skip_group_check=True)
    return pe.matmul(out, left[1], right[0], start=False, stop=stop, skip_group_check=True)



class Load:

    def __init__(self, m, G, src, normalised=True, affine=None, split=False, again=False):
        self.m, self.G, self.src, self.normalised, self.affine = m, G, src, normalised, affine
        self.xs = m.sb("xs", [P, NT, P])
        self.split = split
        if split:
            self.xT = Pair(m, "xT", [P, T])
            self.high_ready = m.flag("x_high_ready", 1)
        else:
            self.xT = m.sb("xT", [P, T])
        self.psX = m.ps("psX", [P, T])
        self.again = again
        if again:
            self.xs2, self.rstd2 = m.sb("xs2", [P, NT, P]), m.sb("rstd2", [P, NT])
            self.rstd2_made = m.flag("rstd2_made", 3)
            self.xs2_ready = m.flag("xs2_ready", 1)
            self.pool_passed = m.sem("load_pool_passed")
        if split and affine:
            self.whole = m.sb("xT_whole", [P, T])
            self.whole_ready = m.flag("x_whole_ready", 1)
        self.xs_ready = m.flag("xs_ready", 1)
        self.x_kept = m.flag("x_kept", 1)
        self.turned = m.flag("turned", 1)
        self.xT_ready = m.flag("xT_ready", 1)

    def scalar(self, e, b):
        self.turned.wait(e, b - 1)
        self.x_kept.wait(e, b - 1)
        x = batch(self.src, b)
        if not self.normalised:
            e.activation(self.xs[:], x, ACT.Copy).then_inc(self.xs_ready.sem, 1)
            return
        for t in range(NT):
            last = e.activation(self.xs[:, t, :], x[:, t, :], ACT.Identity,
                                scale=self.G.rstd[:, bass.ds(b, 1), t], bias=self.G.shift[:, bass.ds(b, 1), t])
        last.then_inc(self.xs_ready.sem, 1)
        if self.again:
            self.xs_ready.wait(e, b)
            self.rstd2_made.wait(e, b)
            for t in range(NT):
                last = e.activation(self.xs2[:, t, :], self.xs[:, t, :], ACT.Identity, scale=self.rstd2[:, t:t + 1])
            last.then_inc(self.xs2_ready.sem, 1)

    def pool(self, e, b):
        if self.again:
            c = Chain(self.rstd2_made, e, b)
            rstd = self.G.rstd[:, bass.ds(b, 1), :].rearrange("p a t -> p (a t)")
            self.xs2_ready.wait(e, b - 1)
            c.step(e.tensor_tensor(self.rstd2[:], rstd, rstd, ALU.mult))
            c.wait()
            stand(e, self.pool_passed)
            c.step(e.tensor_scalar(self.rstd2[:], self.rstd2[:], -LN_EPS, 1.0 + LN_EPS, ALU.mult, ALU.add))
            c.wait()
            c.step(e.tensor_tensor(self.rstd2[:], self.rstd2[:], self.G.minus_half[:], ALU.pow))
            c.end()
        self.xs_ready.wait(e, b)
        e.tensor_copy(batch(self.src, b), self.xs[:]).then_inc(self.x_kept.sem, 1)

    def tensor(self, e, b):
        (self.xs2_ready if self.again else self.xs_ready).wait(e, b)
        xs = self.xs2 if self.again else self.xs
        self.xT_ready.wait(e, b - 1)
        for t in range(NT):
            last = e.transpose(self.psX[:, t * P:(t + 1) * P], xs[:, t, :], self.G.ident[:])
        last.then_inc(self.turned.sem, 1)

    def vector(self, e, b, users):
        self.turned.wait(e, b)
        for s in users:
            s.wait(e, b - 1)
        turned = self.psX[:].rearrange("d (t p) -> d t p", t=NT)
        if self.split:
            high, low = (x[:].rearrange("d (p t) -> d t p", t=NT) for x in (self.xT.high, self.xT.low))
            if self.affine is not None:
                gain, offset = self.affine
                e.tensor_scalar(self.whole[:].rearrange("d (p t) -> d t p", t=NT), turned, gain[:, 0:1],
                                offset[:, 0:1], ALU.mult, ALU.add).then_inc(self.whole_ready.sem, 1)
                self.whole_ready.wait(e, b)
                high, low, turned = self.xT.high[:], self.xT.low[:], self.whole[:]
            e.tensor_copy(high, turned).then_inc(self.high_ready.sem, 1)
            self.high_ready.wait(e, b)
            e.tensor_tensor(low, turned, high.bitcast(F32), ALU.subtract).then_inc(self.xT_ready.sem, 1)
            return
        out = self.xT[:].rearrange("d (p t) -> d t p", t=NT)
        if self.affine is None:
            e.tensor_copy(out, turned).then_inc(self.xT_ready.sem, 1)
        else:
            gain, offset = self.affine
            e.tensor_scalar(out, turned, gain[:, 0:1], offset[:, 0:1], ALU.mult, ALU.add)\
             .then_inc(self.xT_ready.sem, 1)


class Post:

    def __init__(self, m, G):
        self.G = G
        self.stats = m.sb("stats", [P, NT, 6])
        self.mv = m.sb("mv", [P, NT, 2])
        self.spread, self.minus_mean = m.sb("spread", [P, NT]), m.sb("minus_mean", [P, NT])
        self.summed = m.flag("summed", 1, lead=2)
        self.stat = m.flag("stat", 1)
        self.passed = m.sem("passed")
        self.aggregated = m.flag("aggregated", 1)
        self.prepared = m.flag("variance_kept", 2)
        self.rooted = m.flag("rooted", 2)

    def vector(self, e, b, row):
        self.summed.wait(e, b)
        stand(e, self.passed)
        for t in range(NT):
            last = e.bn_stats(self.stats[:, t, :], row[:, t, :])
        last.then_inc(self.stat.sem, 1)
        self.stat.wait(e, b)
        self.rooted.wait(e, b - 1)
        stand(e, self.passed)
        for t in range(NT):
            last = e.bn_aggr(self.mv[:, t, :], self.stats[:, t, :])
        last.then_inc(self.aggregated.sem, 1)
        self.aggregated.wait(e, b)
        e.tensor_scalar(self.spread[:], self.mv[:, :, 1], LN_EPS, None, ALU.add).then_inc(self.prepared.sem, 1)
        e.tensor_scalar(self.minus_mean[:], self.mv[:, :, 0], -1.0, None, ALU.mult).then_inc(self.prepared.sem, 1)

    def pool(self, e, b):
        self.prepared.wait(e, b)
        rstd = self.G.rstd[:, bass.ds(b, 1), :].rearrange("p a t -> p (a t)")
        shift = self.G.shift[:, bass.ds(b, 1), :].rearrange("p a t -> p (a t)")
        e.tensor_tensor(rstd, self.spread[:], self.G.minus_half[:], ALU.pow).then_inc(self.rooted.sem, 1)
        self.rooted.wait(e, b, 1)
        e.tensor_tensor(shift, self.minus_mean[:], rstd, ALU.mult).then_inc(self.rooted.sem, 1)


class Globals:
    pass


def setup(nc, ctx, a):
    G = Globals()
    m = Stage(nc, ctx, "g")
    G.X = m.sb("X", [P, B + 2, NT, P])
    G.rstd = m.sb("rstd", [P, B + 2, NT])
    G.shift = m.sb("shift", [P, B + 2, NT])
    G.minus_half = m.sb("minus_half", [P, NT])
    G.ident = m.sb("ident", [P, P])
    G.identb = m.sb("identb", [P, P], BF16)
    loaded, filled, G.x_in = m.sem("loaded"), m.sem("filled"), m.sem("x_in")
    with nc.Block() as block:
        @block.sync
        def _(sp):
            sp.dma_start(G.ident[:], a["c_ident"]).then_inc(loaded, 16)
            x = a["L0_attn_x"].rearrange("b (p t) d -> p b t d", t=NT)
            sp.dma_start(G.X[:, 0:1, :, :], x[:, 0:1, :, :]).then_inc(loaded, 16)
            sp.dma_start(G.X[:, 1:B, :, :], x[:, 1:B, :, :]).then_inc(G.x_in, 16)
            sp.wait_ge(loaded, 32)

        @block.gpsimd
        def _(pool):
            pool.memset(G.rstd[:], 1.0)
            pool.memset(G.X[:, B:B + 2, :, :], 0.0)
            pool.memset(G.shift[:], 0.0)
            pool.memset(G.minus_half[:], -0.5).then_inc(filled, 1)

        @block.vector
        def _(dve):
            dve.wait_ge(loaded, 32)
            dve.tensor_copy(G.identb[:], G.ident[:]).then_inc(filled, 1)
    return G



def project(nc, G, tag, src, n, q=None, k=None, v=None, normalised=True, operands=None, arriving=None):
    with ExitStack() as ctx:
        m = Stage(nc, ctx, tag)
        load = Load(m, G, src, normalised)
        sides = [s for s in (q, k) if s]
        loaded, prepared = m.sem("loaded"), m.sem("prepared")
        nload = 0
        for i, s in enumerate(sides):
            s["W"] = m.sb(f"W{i}", [P, P])
            s["bias"] = m.sb(f"bias{i}", [P, 1])
            s["sbias"] = m.sb(f"sbias{i}", [P, 1])
            s["full"] = m.sb(f"full{i}", [P, T])
            s["raw"] = m.sb(f"raw{i}", [P, T]) if s["mix"] else None
            s["rest"] = m.sb(f"rest{i}", [P, T])
            s["bf"] = [m.sb(f"bf{i}{c}", [P, PARTS, T], BF16) for c in range(2)]
            s["ps"] = m.ps(f"ps{i}", [P, T])
            s["projected"] = m.flag(f"projected{i}", 1)
            s["raw_ready"] = m.flag(f"raw_ready{i}", 1)
            s["mixed"] = m.flag(f"mixed{i}", 1)
            s["full_ready"] = m.flag(f"full_ready{i}", 1)
            s["high_ready"] = m.flag(f"high_ready{i}", 1)
            s["rest_ready"] = m.flag(f"rest_ready{i}", 1)
            s["mid_ready"] = m.flag(f"mid_ready{i}", 1)
            s["low_ready"] = m.flag(f"low_ready{i}", 1, lead=2)
            s["stored"] = [m.flag(f"stored{i}{c}", 16 * PARTS) for c in range(2)]
        if v:
            Wv = m.sb("Wv", [P, P])
            bv = m.sb("bv", [P, P])
            bvc = m.sb("bvc", [P, 1])
            psV = m.ps("psV", [P, NT, P])
            vraw = m.sb("vraw", [P, T]) if v["mix"] else None
            v_projected = m.flag("v_projected", 1)
            v_raw_ready = m.flag("v_raw_ready", 1)
            v_mixed = m.flag("v_mixed", 1)
            v_added = m.flag("v_added", 1)
            v_ready = m.flag("v_ready", 1)
        m.credit(ACT.Identity)
        xT, xT_users = load.xT, [s["projected"] for s in sides] + ([v_projected] if v else [])
        nload = 32 * len(sides) + (48 if v else 0)

        def batches(engine, body, done=0):
            if n == 1:
                body(engine, 0, 0, 0)
                return
            with engine.Fori(done, n // 2) as half:
                for i in range(2):
                    body(engine, 2 * half + i, i, half)

        with nc.Block() as block:
            @block.sync
            def _(sp):
                for s in sides:
                    sp.dma_start(s["W"][:], s["w"]).then_inc(loaded, 16)
                    sp.dma_start(s["bias"][:], s["b"].rearrange("(p a) -> p a", a=1)).then_inc(loaded, 16)
                if v:
                    sp.dma_start(Wv[:], v["w"]).then_inc(loaded, 16)
                    row = v["b"].rearrange("(a n) -> a n", a=1)
                    sp.dma_start(bv[:], row.broadcast_to([P, P])).then_inc(loaded, 16)
                    sp.dma_start(bvc[:], v["b"].rearrange("(p a) -> p a", a=1)).then_inc(loaded, 16)
                if operands:
                    operands.sync(sp)

                def body(sp, b, i, half):
                    for s in sides:
                        for j, ready in enumerate(("high_ready", "mid_ready", "low_ready")):
                            s[ready].wait(sp, b)
                            dst = s["parts"][bass.ds(b, 1), j, :, :, :].rearrange("a d h n -> h (a d) n")
                            sp.dma_start(dst, s["bf"][i][:, j, :]).then_inc(s["stored"][i].sem, 16)
                if operands:
                    for i in range(2):
                        body(sp, i, i, 0)
                    for s in sides:
                        s["stored"][0].wait(sp, 0)
                    operands.first_batch(sp)
                batches(sp, body, 1 if operands else 0)
                for s in sides:
                    for i in range(min(n, 2)):
                        s["stored"][i].wait(sp, (n - 1) // 2)
                if operands:
                    operands.wait(sp)

            @block.scalar
            def _(act):
                load.scalar(act, 0)
                if arriving is not None:
                    act.wait_ge(arriving, 16)
                act.wait_ge(loaded, nload)
                act.wait_ge(prepared, len(sides))

                def body(act, b, i, half):
                    load.scalar(act, b + 1)
                    if v and v["mix"] is not None:
                        v_projected.wait(act, b)
                        v_mixed.wait(act, b - 1)
                        act.activation(vraw[:], psV[:].rearrange("p t d -> p (t d)"), ACT.Identity,
                                       bias=bvc[:, 0:1]).then_inc(v_raw_ready.sem, 1)
                    for s in sides:
                        if s["mix"] is not None:
                            s["projected"].wait(act, b)
                            s["mixed"].wait(act, b - 1)
                            act.activation(s["raw"][:], s["ps"][:], ACT.Identity,
                                           bias=s["bias"][:, 0:1]).then_inc(s["raw_ready"].sem, 1)
                            s["mixed"].wait(act, b)
                            kw = dict(scale=s["scale"])
                        else:
                            s["projected"].wait(act, b)
                            kw = dict(scale=s["scale"], bias=s["sbias"][:, 0:1])
                        s["rest_ready"].wait(act, b - 1)
                        act.activation(s["full"][:], s["ps"][:], s["func"], **kw).then_inc(s["full_ready"].sem, 1)
                        s["stored"][i].wait(act, half - 1)
                        act.activation(s["bf"][i][:, 0, :], s["ps"][:], s["func"], **kw)\
                           .then_inc(s["high_ready"].sem, 1)
                batches(act, body)

            @block.gpsimd
            def _(pool):
                load.pool(pool, 0)

                def body(pool, b, i, half):
                    load.pool(pool, b + 1)
                    for s in sides:
                        s["mid_ready"].wait(pool, b)
                        s["stored"][i].wait(pool, half - 1)
                        pool.tensor_tensor(s["bf"][i][:, 2, :], s["rest"][:], s["bf"][i][:, 1, :],
                                           ALU.subtract).then_inc(s["low_ready"].sem, 1)
                batches(pool, body)

            @block.tensor
            def _(pe):
                load.tensor(pe, 0)
                pe.wait_ge(loaded, nload)

                def body(pe, b, i, half):
                    load.xT_ready.wait(pe, b)
                    for s in sides:
                        s["high_ready"].wait(pe, b - 1)
                        pe.matmul(s["ps"][:], s["W"][:], xT[:], start=True, stop=True)\
                          .then_inc(s["projected"].sem, 1)
                    if v:
                        v_added.wait(pe, b - 1)
                        if v["mix"] is None:
                            for t in range(NT):
                                last = pe.matmul(psV[:, t, :], xT[:, t * P:(t + 1) * P], Wv[:],
                                                 start=True, stop=True)
                            last.then_inc(v_projected.sem, 1)
                        else:
                            pe.matmul(psV[:].rearrange("p t d -> p (t d)"), Wv[:], xT[:], start=True, stop=True)\
                              .then_inc(v_projected.sem, 1)
                            v_raw_ready.wait(pe, b)
                            for t in range(NT):
                                last = pe.matmul(psV[:, t, :], vraw[:, t * P:(t + 1) * P], v["mix"][:],
                                                 start=True, stop=True)
                            last.then_inc(v_mixed.sem, 1)
                    for s in sides:
                        if s["mix"] is not None:
                            s["raw_ready"].wait(pe, b)
                            pe.matmul(s["ps"][:], s["mix"][:], s["raw"][:], start=True, stop=True)\
                              .then_inc(s["mixed"].sem, 1)
                    load.tensor(pe, b + 1)
                batches(pe, body)

            @block.vector
            def _(dve):
                load.vector(dve, 0, xT_users)
                dve.wait_ge(loaded, nload)
                for s in sides:
                    dve.tensor_scalar(s["sbias"][:], s["bias"][:], s["scale"], None, ALU.mult)\
                       .then_inc(prepared, 1)
                if operands:
                    operands.vector(dve)

                def body(dve, b, i, half):
                    if v:
                        (v_projected if v["mix"] is None else v_mixed).wait(dve, b)
                        out = batch(v["out"], b)
                        if v["mix"] is None:
                            dve.tensor_tensor(out, psV[:], bv[:].unsqueeze(1).broadcast_to([P, NT, P]), ALU.add)\
                               .then_inc(v_added.sem, 1)
                        else:
                            dve.tensor_copy(out, psV[:]).then_inc(v_added.sem, 1)
                        if v["relu"]:
                            v_added.wait(dve, b)
                            dve.tensor_scalar(out, out, 0.0, None, ALU.max).then_inc(v_ready.sem, 1)
                    load.vector(dve, b + 1, xT_users)
                    for s in sides:
                        s["full_ready"].wait(dve, b)
                        s["high_ready"].wait(dve, b)
                        s["low_ready"].wait(dve, b - 1)
                        dve.tensor_tensor(s["rest"][:], s["full"][:], s["bf"][i][:, 0, :], ALU.subtract)\
                           .then_inc(s["rest_ready"].sem, 1)
                        s["rest_ready"].wait(dve, b)
                        s["stored"][i].wait(dve, half - 1)
                        dve.tensor_copy(s["bf"][i][:, 1, :], s["rest"][:]).then_inc(s["mid_ready"].sem, 1)
                batches(dve, body)


class Operands:

    def __init__(self, m, a, qparts, kparts, causal, shared_keys):
        self.a, self.causal, self.copies = a, causal, 1 if shared_keys else 2
        self.qparts, self.kparts = qparts, kparts
        self.QS = [m.sb(f"QS{i}", [P, H, T], BF16) for i in range(2)]
        self.KS = [m.sb(f"KS{i}", [P, H, T], BF16) for i in range(self.copies)]
        self.VA = [m.sb(f"VA{i}", [P, NT, H, 32]) for i in range(self.copies)]
        self.masks = m.sb("masks", [P, 2, P], BF16)
        self.constant, self.filled, self.first = m.sem("constant"), m.sem("filled"), m.sem("first")

    def sync(self, sp):
        a, wide = self.a, lambda x: x.unsqueeze(1).broadcast_to([x.shape[0], H, T])
        first = DECAY_ROWS + PARTS * PARTS * HD
        for tiles, decay, tail in ((self.QS, "c_qdecay", "c_qtail"), (self.KS, "c_kdecay", "c_ktail")):
            for tile in tiles:
                src = a[decay] if self.causal else wide(a["c_qtail"][0:DECAY_ROWS, :])
                sp.dma_start(tile[0:DECAY_ROWS, :, :], src).then_inc(self.constant, 16)
                sp.dma_start(tile[first:P, :, :], wide(a[tail])).then_inc(self.constant, 16)
        sp.dma_start(self.masks[:], a["c_masks"]).then_inc(self.constant, 16)

    def load_queries(self, sp, b, i, sem):
        rows = slice(DECAY_ROWS, DECAY_ROWS + PARTS * PARTS * HD)
        src = self.qparts[b, :, :, :, :].rearrange("j d h n -> (j d) (h n)")
        sp.dma_start(self.QS[i][rows, :, :], src.unsqueeze(0).broadcast_to([PARTS, PARTS * HD, H * T]))\
          .then_inc(sem, 16)

    def load_keys(self, sp, b, i, sem):
        for part in range(PARTS):
            row = DECAY_ROWS + PARTS * HD * part
            src = self.kparts[b, part, :, :, :].rearrange("d h n -> d (h n)")
            sp.dma_start(self.KS[i][row:row + PARTS * HD, :, :],
                         src.unsqueeze(0).broadcast_to([PARTS, HD, H * T])).then_inc(sem, 16)

    def first_batch(self, sp):
        self.load_keys(sp, 0, 0, self.first)
        self.load_queries(sp, 0, 0, self.first)

    def vector(self, dve):
        for tile in self.VA:
            dve.memset(tile[:, :, :, HD:HD + 1], 1.0)
            last = dve.memset(tile[:, :, :, HD + 1:32], 0.0)
        last.then_inc(self.filled, 1)

    def wait(self, sp):
        sp.wait_ge(self.constant, 16 * (4 + 2 * self.copies + 1))
        sp.wait_ge(self.filled, 1)
        sp.wait_ge(self.first, 16 * (PARTS + 1))


def attend(nc, G, tag, operands, Vc, O, causal, shared_keys):
    units = NT
    late = 2 if causal else 1
    with ExitStack() as ctx:
        m = Stage(nc, ctx, tag)
        QS, KS, VA, KC, masks = operands.QS, operands.KS, operands.VA, operands.copies, operands.masks
        PT = [m.sb(f"PT{i}", [P, GH, T]) for i in range(2)]
        negmax = [m.sb(f"negmax{i}", [P, GH, NT]) for i in range(2)]
        mrest = m.sb("mrest", [NT * GH, P])
        mparts = m.sb("mparts", [NT * GH, PARTS, P], BF16)
        Osb = m.sb("Osb", [P, T])
        rden = m.sb("rden", [P, NT, GH, 1])
        psA = [m.ps(f"psA{i}", [P, T]) for i in range(3)]
        psB = [m.ps(f"psB{i}", [P, T]) for i in range(3)]
        psO = m.ps("psO", [P, T])
        psT = m.ps("psT", [P, T])

        queries_in = m.flag("queries_in", 16, first=1)
        keys_in = m.flag("keys_in", 16 * PARTS, first=1)
        values_in = m.flag("values_in", 1)
        row_scores = m.flag("row_scores", 16)
        maxed = m.flag("maxed", 16)
        max_turned = m.flag("max_turned", 1)
        max_split = m.flag("max_split", 4)
        max_in = m.flag("max_in", 16 * PARTS)
        col_scores = m.flag("col_scores", 16)
        exped = m.flag("exped", 16)
        weighted = m.flag("weighted", 4, lead=5)
        out_copied = m.flag("out_copied", 1, first=-1)
        out_turned = m.flag("out_turned", 1, lead=2, first=-1)
        out_scaled = m.flag("out_scaled", 2, lead=3, first=-1)
        cleared = m.sem("cleared")
        m.credit(ACT.Exp)

        def tokens(t):
            return slice(t * P, (t + 1) * P)

        BANK = [0, 1, 2] * 4 + [0, 1, 0, 2]

        def before(n):
            return max(k for k in range(n - 16, n) if BANK[k % 16] == BANK[n])

        def slots(body):
            def walk(engine):
                with engine.Fori(0, B - 2, 2) as b:
                    for i in range(2):
                        body(engine, b + i, i, False, False)
                for i in range(2):
                    body(engine, B - 2 + i, i, i == 1, i == 1)
            return walk

        with nc.Block() as block:
            @block.sync
            def _(sp):
                def load(b, i):
                    col_scores.wait(sp, 4 * (b - 2) + 3)
                    operands.load_queries(sp, b, i, queries_in.sem)
                    if not shared_keys:
                        operands.load_keys(sp, b, i, keys_in.sem)

                def max_rows(b, i, g):
                    for j, steps in enumerate((1, 3, 4)):
                        max_split.wait(sp, 4 * b + g, steps)
                        dst = QS[i][MAX_ROW + j:MAX_ROW + j + 1, GH * g:GH * g + GH, :]
                        sp.dma_start(dst, mparts[:, j, :]).then_inc(max_in.sem, 16)

                def body(sp, b, i, last, _):
                    max_rows(b, i, 0)
                    if not last:
                        load(b + 1, (i + 1) % 2)
                    for g in range(1, NG):
                        max_rows(b, i, g)
                slots(body)(sp)

            @block.gpsimd
            def _(pool):
                pool.memset(O[:, B + 1, :, :], 0.0)
                if shared_keys:
                    src = Vc[:, 1, :, :].rearrange("p t (h d) -> p t h d", d=HD)
                    pool.tensor_copy(VA[0][:, :, :, 0:HD], src).then_inc(values_in.sem, 1)
                else:
                    def body(pool, b, i, last, _):
                        weighted.wait(pool, 4 * (b - 2) + 3)
                        src = Vc[:, bass.ds(b, 1), :, :].rearrange("p a t (h d) -> p (a t) h d", d=HD)
                        pool.tensor_copy(VA[i][:, :, :, 0:HD], src).then_inc(values_in.sem, 1)
                    slots(body)(pool)

            @block.tensor
            def _(pe):
                def rows(G4, i, g, it, hh):
                    N = (it + 1) * P if causal else T
                    n, h = it * GH + hh, GH * g + hh
                    maxed.wait(pe, G4, before(n) + 1)
                    out = psA[BANK[n]]
                    mm = pe.matmul(out[:, 0:N], QS[i][0:MAX_ROW, h, tokens(it)],
                                   KS[i % KC][0:MAX_ROW, h, 0:N], start=True, stop=not causal,
                                   skip_group_check=causal)
                    if causal:
                        mm = pe.matmul(out[:, tokens(it)], G.identb[:], masks[:, 0, :], start=False,
                                       stop=True, skip_group_check=True)
                    mm.then_inc(row_scores.sem, 1)

                def turn_max(G4, i):
                    maxed.wait(pe, G4)
                    out_scaled.wait(pe, G4 - 3)
                    pe.transpose(psT[0:NT * GH, 0:P], negmax[i][:].rearrange("p h t -> p (h t)"), G.ident[:])\
                      .then_inc(max_turned.sem, 1)

                def columns(G4, i, g, jt, hh):
                    lo = jt * P if causal else 0
                    N = T - lo
                    n, h = jt * GH + hh, GH * g + hh
                    exped.wait(pe, G4, before(n) + 1)
                    out = psB[BANK[n]]
                    mm = pe.matmul(out[:, 0:N], KS[i % KC][:, h, tokens(jt)], QS[i][:, h, lo:T],
                                   start=True, stop=not causal, skip_group_check=causal)
                    if causal:
                        mm = pe.matmul(out[:, 0:P], G.identb[:], masks[:, 1, :], start=False,
                                       stop=True, skip_group_check=True)
                    mm.then_inc(col_scores.sem, 1)

                def weigh(G4, i, g, jt):
                    lo = jt * P if causal else 0
                    N = T - lo
                    if jt == 0:
                        out_copied.wait(pe, G4 - 1)
                    exped.wait(pe, G4, GH * (jt + 1))
                    for hh in range(GH):
                        mm = pe.matmul(psO[32 * hh:32 * hh + 32, lo:T], VA[i % KC][:, jt, GH * g + hh, :],
                                       PT[jt % 2][:, hh, 0:N], start=(jt == 0), stop=(jt == NT - 1),
                                       tile_position=(0, 32 * hh), skip_group_check=True)
                    mm.then_inc(weighted.sem, 1)

                def turn_out(G4, alone):
                    out_copied.wait(pe, G4)
                    if alone:
                        out_scaled.wait(pe, G4 - 1)
                    else:
                        max_split.wait(pe, G4 + 2, 2)
                    for t in range(NT):
                        mm = pe.transpose(psT[:, tokens(t)], Osb[:, tokens(t)], G.ident[:])
                    mm.then_inc(out_turned.sem, 1)

                def operands_in(b):
                    queries_in.wait(pe, b)
                    if not shared_keys:
                        keys_in.wait(pe, b)

                if shared_keys:
                    values_in.wait(pe, 0)
                for g in range(2):
                    for it in range(units):
                        for hh in range(GH):
                            rows(g, 0, g, it, hh)
                            if g == 1 and it == 0 and hh == 1:
                                turn_max(0, 0)
                max_in.wait(pe, 0)
                for hh in range(GH):
                    columns(0, 0, 0, 0, hh)

                def body(pe, b, i, last, _):
                    for g in range(NG):
                        G4 = 4 * b + g
                        ahead = not (last and g >= 2)
                        end = last and g == NG - 1
                        ai, ag = (i, g + 2) if g < 2 else ((i + 1) % 2, g - 2)
                        if g == 2 and ahead:
                            operands_in(b + 1)
                        if g == 0 and not shared_keys:
                            values_in.wait(pe, b)
                        for u in range(units):
                            if u == 2:
                                turn_out(G4 - 1, end)
                            if u < units - 1:
                                following = (G4, i, g, u + 1)
                            elif not end:
                                following = (G4 + 1, i if g < NG - 1 else (i + 1) % 2, (g + 1) % NG, 0)
                                max_in.wait(pe, G4 + 1)
                            else:
                                following = None
                            for hh in range(GH):
                                if following:
                                    columns(*following, hh)
                                if ahead:
                                    rows(G4 + 2, ai, ag, u, hh)
                                if u == 0 and hh == late and not end:
                                    turn_max(G4 + 1, (g + 1) % 2)
                                if hh == late:
                                    weigh(G4, i, g, u)
                    if last:
                        turn_out(4 * b + 3, True)

                slots(body)(pe)

            @block.scalar
            def _(act):
                def copy_out(act, G4):
                    weighted.wait(act, G4)
                    out_turned.wait(act, G4 - 1)
                    act.activation(Osb[:], psO[:], ACT.Copy).then_inc(out_copied.sem, 1)

                def body(act, b, i, last, _):
                    for g in range(NG):
                        G4 = 4 * b + g
                        for u in range(units):
                            N = T - u * P if causal else T
                            weighted.wait(act, G4, u - 1)
                            for hh in range(GH):
                                n = GH * u + hh
                                col_scores.wait(act, G4, n + 1)
                                act.activation(PT[u % 2][:, hh, 0:N], psB[BANK[n]][:, 0:N], ACT.Exp)\
                                   .then_inc(exped.sem, 1)
                                if n == 2:
                                    copy_out(act, G4 - 1)
                    if last:
                        copy_out(act, 4 * b + 3)
                act.wait_ge(cleared, 1)
                slots(body)(act)

            @block.vector
            def _(dve):
                def maximum(G4, i, n):
                    it, hh = divmod(n, GH)
                    N = (it + 1) * P if causal else T
                    row_scores.wait(dve, G4, n + 1)
                    if n == 0 and not (isinstance(G4, int) and G4 < 2):
                        max_turned.wait(dve, G4 - 2)
                    dve.tensor_reduce(negmax[i][:, hh, it:it + 1], psA[BANK[n]][:, 0:N], AX.X, ALU.max,
                                      negate=True).then_inc(maxed.sem, 1)

                def split_max(G4, step):
                    rows16 = psT[0:NT * GH, 0:P]
                    if step == 0:
                        max_turned.wait(dve, G4)
                        max_in.wait(dve, G4 - 1)
                        made = dve.tensor_copy(mparts[:, 0, :], rows16)
                    else:
                        max_split.wait(dve, G4, step)
                        if step == 1:
                            made = dve.tensor_tensor(mrest[:], rows16, mparts[:, 0, :], ALU.subtract)
                        elif step == 2:
                            made = dve.tensor_copy(mparts[:, 1, :], mrest[:])
                        else:
                            made = dve.tensor_tensor(mparts[:, 2, :], mrest[:], mparts[:, 1, :], ALU.subtract)
                    made.then_inc(max_split.sem, 1)

                def scale_out(b, g, G4, step):
                    turned = psT[:].rearrange("p (t h c) -> p t h c", t=NT, h=GH)
                    if step == 0:
                        out_turned.wait(dve, G4)
                        dve.reciprocal(rden[:], turned[:, :, :, HD:HD + 1]).then_inc(out_scaled.sem, 1)
                    else:
                        out_scaled.wait(dve, G4, 1)
                        dst = O[:, bass.ds(b + 1, 1), :, GH * HD * g:GH * HD * (g + 1)]\
                            .rearrange("p a t (h d) -> p (a t) h d", d=HD)
                        dve.tensor_tensor(dst, turned[:, :, :, 0:HD], rden[:].broadcast_to([P, NT, GH, HD]),
                                          ALU.mult).then_inc(out_scaled.sem, 1)

                dve.memset(psO[:], 1.0).then_inc(cleared, 1)
                for g in range(2):
                    for n in range(units * GH):
                        maximum(g, g, n)
                        if g == 1 and 2 <= n < 6:
                            split_max(0, n - 2)

                def body(dve, b, i, last, _):
                    for g in range(NG):
                        G4 = 4 * b + g
                        for n in range(units * GH):
                            if not (last and g >= 2):
                                maximum(G4 + 2, g % 2, n)
                            if 2 <= n < 6 and not (last and g == NG - 1):
                                split_max(G4 + 1, n - 2)
                            if n in (10, 12):
                                scale_out(b if g else b - 1, (g - 1) % NG, G4 - 1, (n - 10) // 2)
                    if last:
                        for step in range(2):
                            scale_out(b, 3, 4 * b + 3, step)
                slots(body)(dve)


def attention_output(nc, G, tag, a, O, w, bias):
    with ExitStack() as ctx:
        m = Stage(nc, ctx, tag)
        post = Post(m, G)
        os_ = [m.sb(f"os{i}", [P, NT, P]) for i in range(2)]
        oT = [m.sb(f"oT{i}", [P, T]) for i in range(2)]
        psT = [m.ps(f"psT{i}", [P, T]) for i in range(2)]
        psY = [m.ps(f"psY{i}", [P, NT, P]) for i in range(2)]
        copied = m.flag("copied", 1)
        turned = m.flag("turned", 1, lead=2)
        oT_ready = m.flag("oT_ready", 1, lead=2)
        projected = m.flag("projected", 1, lead=2)
        base_ready = m.flag("base_ready", 1)
        loaded = m.sem("loaded")
        m.credit()
        if w is not None:
            W = m.sb("W", [P, P])
            bo = m.sb("bo", [P, P])

        def pairs(engine, body):
            with engine.Fori(0, B // 2) as half:
                for i in range(2):
                    body(2 * half + i, i)

        with nc.Block() as block:
            if w is not None:
                @block.sync
                def _(sp):
                    sp.dma_start(W[:], w).then_inc(loaded, 16)
                    sp.dma_start(bo[:], bias.rearrange("(a n) -> a n", a=1).broadcast_to([P, P])).then_inc(loaded, 16)
                    sp.wait_ge(loaded, 32)

            @block.gpsimd
            def _(pool):
                if w is not None:
                    pool.wait_ge(loaded, 32)
                def prepare(b):
                    x = batch(G.X, b)
                    other = bo[:].unsqueeze(1).broadcast_to([P, NT, P]) if w is not None else x
                    pool.tensor_tensor(x, x, other, ALU.add).then_inc(base_ready.sem, 1)

                prepare(0)
                with turns(pool, B) as b:
                    prepare(b + 1)
                    post.pool(pool, b)

            @block.scalar
            def _(act):
                def fetch(b, i):
                    turned.wait(act, b - 2)
                    act.activation(os_[i][:], batch(O, b + 1), ACT.Copy).then_inc(copied.sem, 1)

                def body(b, i):
                    fetch(b + 1, 1 - i)
                    if w is not None:
                        turned.wait(act, b)
                        projected.wait(act, b - 2)
                        act.activation(oT[i][:], psT[i][:], ACT.Copy).then_inc(oT_ready.sem, 1)

                fetch(0, 0)
                pairs(act, body)

            @block.tensor
            def _(pe):
                def turn(b, i):
                    copied.wait(pe, b)
                    (oT_ready if w is not None else post.summed).wait(pe, b - 2)
                    for t in range(NT):
                        last = pe.transpose(psT[i][:, t * P:(t + 1) * P], os_[i][:, t, :], G.ident[:])
                    last.then_inc(turned.sem, 1)

                def body(b, i):
                    turn(b + 1, 1 - i)
                    if w is not None:
                        oT_ready.wait(pe, b)
                        post.summed.wait(pe, b - 2)
                        for t in range(NT):
                            last = pe.matmul(psY[i][:, t, :], oT[i][:, t:T:NT], W[:], start=True, stop=True)
                        last.then_inc(projected.sem, 1)

                turn(0, 0)
                if w is not None:
                    pe.wait_ge(loaded, 32)
                pairs(pe, body)

            @block.vector
            def _(dve):
                def body(b, i):
                    base_ready.wait(dve, b)
                    x = batch(G.X, b)
                    if w is not None:
                        projected.wait(dve, b)
                        dve.tensor_tensor(x, psY[i][:], x, ALU.add).then_inc(post.summed.sem, 1)
                    else:
                        turned.wait(dve, b)
                        dve.tensor_tensor(x, psT[i][:].rearrange("p (t c) -> p t c", t=NT), x, ALU.add)\
                           .then_inc(post.summed.sem, 1)
                    post.vector(dve, b, x)
                pairs(dve, body)


def attention_stage(nc, G, tag, a, kind):
    scale = float(np.float32(1.0) / np.sqrt(np.float32(HD)))
    with ExitStack() as ctx:
        m = Stage(nc, ctx, tag)
        one = kind == "cross"
        O = m.sb("O", [P, B + 2, NT, P])
        Vc = m.sb("Vc", [P, 2 if one else B, NT, P])
        qparts = nc.dram_tensor(f"{tag}_qparts", [B, PARTS, HD, H, T], BF16, kind="Internal").ap()
        kparts = nc.dram_tensor(f"{tag}_kparts", [2 if one else B, PARTS, HD, H, T], BF16, kind="Internal").ap()
        operands = Operands(m, a, qparts, kparts, kind == "decay", one)
        if kind == "decay":
            ctx.callback(m.retire)
            q = dict(w=a["L0_attn_Wq"], b=a["L0_attn_bq"], scale=scale, func=ACT.Identity, mix=None, parts=qparts)
            k = dict(w=a["L0_attn_Wk"], b=a["L0_attn_bk"], scale=1.0, func=ACT.Identity, mix=None, parts=kparts)
            v = dict(w=a["L0_attn_Wv"], b=a["L0_attn_bv"], relu=False, mix=None, out=Vc)
            project(nc, G, tag + "p", G.X, B, q, k, v, operands=operands, arriving=G.x_in)
            attend(nc, G, tag + "a", operands, Vc, O, True, False)
            attention_output(nc, G, tag + "o", a, O, a["L0_attn_Wo"], a["L0_attn_bo"])
        elif kind == "cross":
            q = dict(w=a["L2_attn_Wq_w"], b=a["L2_attn_Wq_b"], scale=scale, func=ACT.Relu, mix=None, parts=qparts)
            k = dict(w=a["L2_attn_Wk_w"], b=a["L2_attn_Wk_b"], scale=1.0, func=ACT.Relu, mix=None, parts=kparts)
            v = dict(w=a["L2_attn_Wv_w"], b=a["L2_attn_Wv_b"], relu=True, mix=None, out=Vc)
            KV = m.sb("KV", [P, 3, NT, P])
            spare = m.sem("spare")
            kv_in = m.sem("kv_in")
            m.credit()
            with nc.Block() as block:
                @block.sync
                def _(sp):
                    for i, name in enumerate(("L2_attn_keys", "L2_attn_values")):
                        sp.dma_start(KV[:, i, :, :], a[name].rearrange("a (p t) d -> p (a t) d", t=NT))\
                          .then_inc(kv_in, 16)
                    sp.wait_ge(kv_in, 32)

                @block.gpsimd
                def _(pool):
                    pool.memset(KV[:, 2, :, :], 0.0).then_inc(spare, 1)
            project(nc, G, tag + "k", KV, 2, k=k, v=v, normalised=False)
            project(nc, G, tag + "p", G.X, B, q=q, operands=operands)
            attend(nc, G, tag + "a", operands, Vc, O, False, True)
            attention_output(nc, G, tag + "o", a, O, None, None)
        else:
            mixes = lora(nc, G, m, a)
            q = dict(w=a["L3_wq"], b=a["L3_bq"], scale=scale, func=ACT.Identity, mix=mixes[0], parts=qparts)
            k = dict(w=a["L3_wk"], b=a["L3_bk"], scale=1.0, func=ACT.Identity, mix=None, parts=kparts)
            v = dict(w=a["L3_wv"], b=a["L3_bv"], relu=False, mix=mixes[1], out=Vc)
            project(nc, G, tag + "p", G.X, B, q, k, v, operands=operands)
            attend(nc, G, tag + "a", operands, Vc, O, False, False)
            attention_output(nc, G, tag + "o", a, O, a["L3_attn_w_proj"], a["L3_attn_b_proj"])


def lora(nc, G, m, a):
    LORA_SCALE = 2.0
    R = 16
    A = [m.sb(f"A{i}", [R, P]) for i in range(2)]
    Bm = [m.sb(f"B{i}", [R, P]) for i in range(2)]
    blocks = m.sb("blocks", [P, P])
    out = [m.sb(f"mix{i}", [P, P]) for i in range(2)]
    loaded, made, masked, added = m.sem("l_in"), m.sem("l_mm"), m.sem("l_mask"), m.sem("l_add")
    m.credit()
    with ExitStack() as ctx:
        ps = [ctx.enter_context(nc.psum_tensor(f"{m.tag}_psL{i}", [P, T], F32)) for i in range(2)]
        with nc.Block() as block:
            @block.sync
            def _(sp):
                sp.dma_start(blocks[:], a["c_blocks"]).then_inc(loaded, 16)
                for i, side in enumerate("qv"):
                    sp.dma_start(A[i][:].rearrange("r (h d) -> r h d", h=H),
                                 a[f"L3_a{side}T"].unsqueeze(1).broadcast_to([R, H, HD])).then_inc(loaded, 16)
                    sp.dma_start(Bm[i][:].rearrange("r (h d) -> r h d", h=H),
                                 a[f"L3_attn_b_{side}"].unsqueeze(1).broadcast_to([R, H, HD])).then_inc(loaded, 16)
                sp.wait_ge(loaded, 80)

            @block.tensor
            def _(pe):
                pe.wait_ge(loaded, 80)
                for i in range(2):
                    pe.matmul(ps[i][:, 0:P], A[i][:], Bm[i][:], start=True, stop=True).then_inc(made, 1)

            @block.vector
            def _(dve):
                dve.wait_ge(loaded, 80)
                for i in range(2):
                    dve.wait_ge(made, i + 1)
                    dve.scalar_tensor_tensor(out=out[i][:], in0=ps[i][:, 0:P], scalar=LORA_SCALE, in1=blocks[:],
                                             op0=ALU.mult, op1=ALU.mult).then_inc(masked, 1)
                    dve.wait_ge(masked, i + 1)
                    dve.tensor_tensor(out[i][:], out[i][:], G.ident[:], ALU.add).then_inc(added, 1)
    return out



def expert_stage(nc, G, tag, a, gated):
    E = 12
    if gated:
        C, FF, temperature = 3, 3 * P, 1.5
        order = [(E, 2)] + [(e, C) for e in range(E)]
    else:
        C, FF, temperature = 2, 2 * P, 1.0
        order = [(e, C) for e in range(8)]
    chunks = [(x, c) for x, (_, n) in enumerate(order) for c in range(n)]
    NCH, NX = len(chunks), len(order)
    first_chunk = [sum(n for _, n in order[:x]) for x in range(NX + 1)]
    LAG, RING = (3, 4) if gated else (4, 6)
    WITH_BIAS = 8
    SLOT = [n % RING for n in range(NCH)]

    def before(n):
        return max(k for k in range(n - NCH, n) if SLOT[k % NCH] == SLOT[n])

    with ExitStack() as ctx:
        m = Stage(nc, ctx, tag)
        load, post = Load(m, G, G.X, split=True), Post(m, G)
        NE = 12 if gated else 8
        HW_ = (2 if gated else 1) * FF
        W1 = Pair(m, "W1", [P, NE, HW_])
        W2 = m.sb("W2", [P, NE, C, P])
        raw1 = [m.sb(f"raw1{i}", [P, HW_]) for i in range(2)]
        Wr, rawr = Pair(m, "Wr", [P, E]), m.sb("rawr", [P, E])
        br = m.sb("br", [P, E])
        iota = m.sb("iota", [P, E])
        if gated:
            Ws1, Ws2 = Pair(m, "Ws1", [P, 4 * P]), m.sb("Ws2", [P, 2, P])
            b1, bs1 = m.sb("b1", [P, NE, 2 * C]), m.sb("bs1", [P, 4])
            b2 = m.sb("b2", [E + 1, P])
            gate = [m.sb(f"gate{i}", [P, T]) for i in range(2)]
            wT = m.sb("wT", [E + 1, NT, P])
        act_ = [m.sb(f"act{i}", [P, T]) for i in range(RING)]
        acc = m.sb("acc", [P, NT, P])
        logits = m.sb("logits", [P, NT, E])
        top = m.sb("top", [P, NT, 8])
        index = m.sb("index", [P, NT, 8], U32)
        indexf = m.sb("indexf", [P, NT, 2])
        margin = m.sb("margin", [P, NT])
        th = m.sb("th", [P, NT, 1])
        share = m.sb("share", [P, 2, NT])
        hit = m.sb("hit", [P, 2, NT, E])
        w = m.sb("w", [P, NT, E + 1])
        through = m.sb("through", [P, NT])
        psa = [m.ps(f"psa{i}", [P, T]) for i in range(2)]
        psg = [m.ps(f"psg{i}", [P, T]) for i in range(2)]
        psY = [m.ps(f"psY{i}", [P, NT, P]) for i in range(2)]
        psR = m.ps("psR", [P, T])
        hidden = m.flag("hidden", NCH)
        gelued = m.flag("gelued", NCH)
        activated = m.flag("activated", NCH)
        consumed = m.flag("consumed", NCH)
        added = m.flag("added", NX)
        bias_added = m.flag("bias_added", 1)
        scored = m.flag("scored", 1)
        ranked = m.flag("ranked", 5)
        tanhed = m.flag("tanhed", 1)
        routed = m.flag("routed", 4 if gated else 6)
        turned_w = m.flag("turned_w", 1)
        copied_w = m.flag("copied_w", 1)
        biased = m.flag("biased", 1)
        router_in, small_in, ones = (m.sem(n) for n in ("router_in", "small_in", "ones"))
        raw_in = [m.sem(f"raw_in{i}") for i in range(2)]
        second_in = [m.sem(f"second_in{x}") for x in range(NX)]
        cut_high, cut_low = m.sem("cut_high"), m.sem("cut_low")
        m.credit(ACT.Gelu if gated else ACT.Silu)
        nsmall = 16 * (5 if gated else 2)

        def first_weights(x, part):
            e, _ = order[x]
            return (Ws1.high, Ws1.low)[part][:, :] if e == E else (W1.high, W1.low)[part][:, e, :]

        def second_weights(x):
            e, _ = order[x]
            return Ws2[:, :, :] if e == E else W2[:, e, :, :]

        with nc.Block() as block:
            @block.sync
            def _(sp):
                rows = lambda v: v.rearrange("(a n) -> a n", a=1).broadcast_to([P, E])
                if gated:
                    sp.dma_start(rawr[:], a["L0_ffn_Wr"]).then_inc(router_in, 16)
                    sp.dma_start(br[:], rows(a["L0_ffn_br"])).then_inc(small_in, 16)
                else:
                    sp.dma_start(rawr[:], a["L2_ffn_gate_w"]).then_inc(router_in, 16)
                    sp.dma_start(br[:], rows(a["L2_ffn_expert_bias"])).then_inc(small_in, 16)
                for x, (e, n) in enumerate(order):
                    if e == E:
                        w1, w2 = a["L0_ffn_Ws1"], a["L0_ffn_Ws2"]
                    else:
                        w1, w2 = (a["L0_ffn_We1"], a["L0_ffn_We2"]) if gated else (a["L2_ffn_w1"], a["L2_ffn_w2"])
                        w1, w2 = w1[e, :, :], w2[e, :, :]
                    sp.dma_start(second_weights(x), w2.rearrange("(c f) d -> f c d", f=P)).then_inc(second_in[x], 16)
                    if x >= 2:
                        sp.wait_ge(cut_low, x - 1)
                    sp.dma_start(raw1[x % 2][:, 0:w1.shape[1]], w1).then_inc(raw_in[x % 2], 16)
                    if x == 0:
                        sp.dma_start(iota[:], a["c_iota"]).then_inc(small_in, 16)
                        if gated:
                            sp.dma_start(b1[:], a["L0_be1"]).then_inc(small_in, 16)
                            sp.dma_start(bs1[:], a["L0_bs1"]).then_inc(small_in, 16)
                            sp.dma_start(b2[:], a["L0_b2"]).then_inc(small_in, 16)
                sp.wait_ge(small_in, nsmall)
                for s in second_in:
                    sp.wait_ge(s, 16)

            @block.gpsimd
            def _(pool):
                pool.memset(w[:], 1.0).then_inc(ones, 1)
                pool.wait_ge(router_in, 16)
                pool.tensor_copy(Wr.high[:], rawr[:]).then_inc(ones, 1)
                pool.wait_ge(ones, 2)
                pool.tensor_tensor(Wr.low[:], rawr[:], Wr.high[:].bitcast(F32), ALU.subtract).then_inc(ones, 1)
                for x, (e, n) in enumerate(order):
                    if x == 2:
                        load.pool(pool, 0)
                    pool.wait_ge(raw_in[x % 2], 16 * (x // 2 + 1))
                    high, low = (first_weights(x, part) for part in range(2))
                    raw = raw1[x % 2][:, 0:high.shape[1]]
                    pool.tensor_copy(high, raw).then_inc(cut_high, 1)
                    pool.wait_ge(cut_high, x + 1)
                    pool.tensor_tensor(low, raw, high.bitcast(F32), ALU.subtract).then_inc(cut_low, 1)
                with turns(pool, B) as b:
                    load.pool(pool, b + 1)
                    post.pool(pool, b)

            @block.scalar
            def _(act):

                load.scalar(act, 0)
                act.wait_ge(small_in, nsmall)
                with turns(act, B) as b:
                    for n, (x, c) in enumerate(chunks):
                        e, C_ = order[x]
                        hidden.wait(act, b, n + 1)
                        if gated:
                            activated.wait(act, b, n - 1)
                            bias = bs1[:, 2 + c:3 + c] if e == E else b1[:, e, C + c:C + c + 1]
                            act.activation(gate[n % 2][:], psg[n % 2][:], ACT.Gelu, bias=bias)\
                               .then_inc(gelued.sem, 1)
                        else:
                            ps = (psa + psg)[n % 4]
                            consumed.wait(act, b, before(n) + 1)
                            act.activation(act_[SLOT[n]][:], ps[:], ACT.Silu).then_inc(activated.sem, 1)
                        if n == NCH - 4:
                            load.scalar(act, b + 1)
                        if n == 4:
                            ranked.wait(act, b)
                            act.activation(th[:, :, 0], margin[:], ACT.Tanh, scale=0.5 / temperature)\
                               .then_inc(tanhed.sem, 1)

            @block.tensor
            def _(pe):

                def hidden_of(b, n):
                    x, c = chunks[n]
                    e, C_ = order[x]
                    pe.wait_ge(cut_low, x + 1)
                    halves = [first_weights(x, part) for part in range(2)]
                    xT = load.xT.cut((slice(None), slice(None)))
                    if gated:
                        activated.wait(pe, b, n - 1)
                        products(pe, psa[n % 2][:], [h[:, c * P:(c + 1) * P] for h in halves], xT, True, True)
                        products(pe, psg[n % 2][:], [h[:, (C_ + c) * P:(C_ + c + 1) * P] for h in halves], xT,
                                 True, True).then_inc(hidden.sem, 1)
                    else:
                        activated.wait(pe, b, n - 3)
                        products(pe, (psa + psg)[n % 4][:], [h[:, c * P:(c + 1) * P] for h in halves], xT,
                                 True, True).then_inc(hidden.sem, 1)

                def output_of(b, n):
                    x, c = chunks[n]
                    e, C_ = order[x]
                    activated.wait(pe, b, n + 1)
                    if c == 0:
                        pe.wait_ge(second_in[x], 16)
                        added.wait(pe, b, max(x - 1, 0))
                    for t in range(NT):
                        mm = pe.matmul(psY[x % 2][:, t, :], act_[SLOT[n]][:, t:T:NT], second_weights(x)[:, c, :],
                                       start=(c == 0 and t == 0), stop=(c == C_ - 1 and t == NT - 1),
                                       skip_group_check=True)
                    mm.then_inc(consumed.sem, 1)

                load.tensor(pe, 0)
                pe.wait_ge(ones, 3)
                with turns(pe, B) as b:
                    load.xT_ready.wait(pe, b)
                    bias_added.wait(pe, b - 1) if gated else ranked.wait(pe, b - 1, 1)
                    for t in range(NT):
                        mm = products(pe, psR[:, t * E:(t + 1) * E], load.xT.cut((slice(None), slice(t, T, NT))),
                                      Wr.cut((slice(None), slice(None))), True, True)
                    mm.then_inc(scored.sem, 1)
                    for n in range(NCH + LAG):
                        if n < NCH:
                            hidden_of(b, n)
                        if n == NCH - 1:
                            load.tensor(pe, b + 1)
                        if n >= LAG:
                            output_of(b, n - LAG)
                        if gated and n == first_chunk[4] - 1:
                            routed.wait(pe, b)
                            for t in range(NT):
                                mm = pe.transpose(psR[0:E + 1, t * P:(t + 1) * P], w[:, t, :], G.ident[:])
                            mm.then_inc(turned_w.sem, 1)
                        if gated and n == first_chunk[6] - 1:
                            copied_w.wait(pe, b)
                            for t in range(NT):
                                mm = pe.matmul(psR[:, t * P:(t + 1) * P], wT[:, t, :], b2[:], start=True, stop=True)
                            mm.then_inc(biased.sem, 1)

            @block.vector
            def _(dve):

                def rank(b, part):
                    c = Chain(ranked, dve, b)
                    if part == 0:
                        scored.wait(dve, b)
                        c.step(dve.tensor_tensor(logits[:], psR[:, 0:NT * E].rearrange("p (t e) -> p t e", t=NT),
                                                 br[:].unsqueeze(1).broadcast_to([P, NT, E]), ALU.add))
                    elif part == 1:
                        c.after(1)
                        stand(dve, post.passed)
                        for t in range(NT):
                            last = dve.max(top[:, t, :], logits[:, t, :])
                        c.step(last)
                    else:
                        c.after(2)
                        stand(dve, post.passed)
                        for t in range(NT):
                            last = dve.max_index(index[:, t, :], top[:, t, :], logits[:, t, :])
                        c.step(last)
                        tanhed.wait(dve, b - 1)
                        c.step(dve.tensor_tensor(margin[:], top[:, :, 0], top[:, :, 1], ALU.subtract))
                        c.wait()
                        c.step(dve.tensor_copy(indexf[:], index[:, :, 0:2]))
                        c.end()

                def route(b, part):
                    c = Chain(routed, dve, b)
                    if part == 0:
                        tanhed.wait(dve, b)
                        ranked.wait(dve, b)
                        for i, half in enumerate((0.5, -0.5)):
                            dve.tensor_scalar(share[:, i, :], th[:, :, 0], half, 0.5, ALU.mult, ALU.add)
                        for i in range(2):
                            last = dve.tensor_tensor(hit[:, i, :, :], iota[:].unsqueeze(1).broadcast_to([P, NT, E]),
                                                     indexf[:, :, i:i + 1].broadcast_to([P, NT, E]), ALU.is_equal)
                        c.step(last)
                        return
                    c.after(1)
                    for i in range(2):
                        c.step(dve.tensor_tensor(hit[:, i, :, :], hit[:, i, :, :],
                                                 share[:, i, :].unsqueeze(2).broadcast_to([P, NT, E]), ALU.mult))
                    c.wait()
                    if gated:
                        turned_w.wait(dve, b - 1)
                    c.step(dve.tensor_tensor(w[:, :, 0:E], hit[:, 0, :, :], hit[:, 1, :, :], ALU.add))
                    c.wait()
                    if not gated:
                        c.step(dve.tensor_reduce(through[:], w[:, :, 8:E], AX.X, ALU.add))
                        c.wait()
                        load.x_kept.wait(dve, b)
                        c.step(dve.tensor_tensor(acc[:], batch(G.X, b),
                                                 through[:].unsqueeze(2).broadcast_to([P, NT, P]), ALU.mult))
                        c.wait()
                    c.end()

                def add(b, x):
                    e, _ = order[x]
                    consumed.wait(dve, b, first_chunk[x + 1])
                    if x:
                        added.wait(dve, b, x)
                    if gated and x == WITH_BIAS + 1:
                        bias_added.wait(dve, b)
                    for t in range(NT):
                        if e == E:
                            last = dve.tensor_copy(acc[:, t, :], psY[x % 2][:, t, :])
                        else:
                            last = dve.scalar_tensor_tensor(out=acc[:, t, :], in0=psY[x % 2][:, t, :],
                                                            scalar=w[:, t, e:e + 1], in1=acc[:, t, :],
                                                            op0=ALU.mult, op1=ALU.add)
                    last.then_inc(added.sem, 1)
                    if gated and x == WITH_BIAS:
                        biased.wait(dve, b)
                        added.wait(dve, b, x + 1)
                        dve.tensor_tensor(acc[:], acc[:], psR[:].rearrange("p (t d) -> p t d", t=NT), ALU.add)\
                           .then_inc(bias_added.sem, 1)

                xT_users = [hidden, scored]
                load.vector(dve, 0, xT_users)
                dve.wait_ge(small_in, nsmall)
                dve.wait_ge(ones, 1)
                with turns(dve, B) as b:
                    for n in range(NCH + LAG + 1):
                        if gated and n < NCH:
                            x, c = chunks[n]
                            e, _ = order[x]
                            hidden.wait(dve, b, n + 1)
                            gelued.wait(dve, b, n + 1)
                            consumed.wait(dve, b, before(n) + 1)
                            bias = bs1[:, c:c + 1] if e == E else b1[:, e, c:c + 1]
                            dve.scalar_tensor_tensor(out=act_[SLOT[n]][:], in0=psa[n % 2][:], scalar=bias,
                                                     in1=gate[n % 2][:], op0=ALU.add, op1=ALU.mult)\
                               .then_inc(activated.sem, 1)
                        if n == NCH - 1:
                            load.vector(dve, b + 1, xT_users)
                        if n in (1, 2, 3):
                            rank(b, n - 1)
                        if n in (5, 6):
                            route(b, n - 5)
                        if gated and n == first_chunk[5] - 1:
                            turned_w.wait(dve, b)
                            biased.wait(dve, b - 1)
                            dve.tensor_copy(wT[:], psR[0:E + 1, :].rearrange("e (t p) -> e t p", t=NT))\
                               .then_inc(copied_w.sem, 1)
                        if n - LAG in first_chunk[1:]:
                            add(b, first_chunk.index(n - LAG) - 1)
                    load.x_kept.wait(dve, b)
                    added.wait(dve, b, NX)
                    x_ = batch(G.X, b)
                    dve.tensor_tensor(x_, acc[:], x_, ALU.add).then_inc(post.summed.sem, 1)
                    post.vector(dve, b, x_)



def linear_attention_stage(nc, G, tag, a):
    DH, PAIRS, W_ = 64, 8, 65
    RING = [0, 1, 2, 0, 1, 2, 0, 1]

    def before(r):
        return max(k for k in range(r - PAIRS, r) if RING[k % PAIRS] == RING[r])

    EPS_DEN = 1e-6
    with ExitStack() as ctx:
        m = Stage(nc, ctx, tag)
        gain, offset = m.sb("gain", [P, 1]), m.sb("offset", [P, 1])
        load, post = Load(m, G, G.X, affine=(gain, offset), split=True, again=True), Post(m, G)
        raw = [m.sb(f"raw{i}", [P, PAIRS * P]) for i in range(3)]
        Wq, Wk, Wv = (Pair(m, n, [P, PAIRS * P]) for n in ("Wq", "Wk", "Wv"))
        Wo = m.sb("Wo", [P, PAIRS, P])
        causal = m.sb("causal", [P, P])
        VA = m.sb("VA", [P, NT, H, W_])
        ex = [m.sb(f"ex{i}", [P, T]) for i in range(2)]
        re = [m.sb(f"re{i}", [P, T]) for i in range(2)]
        Q = [[m.sb(f"Q{i}{h}", [P, T]) for h in range(2)] for i in range(3)]
        QQ = [m.sb(f"QQ{i}", [P, T]) for i in range(3)]
        K = [m.sb(f"K{i}", [P, T]) for i in range(2)]
        Kt = [m.sb(f"Kt{i}", [P, NT, P]) for i in range(2)]
        AT = [[m.sb(f"AT{i}{h}", [P, NT, P]) for h in range(2)] for i in range(2)]
        S = [m.sb(f"S{i}", [P, 3, 2 * W_]) for i in range(2)]
        den = [m.sb(f"den{i}", [P, 4, 1]) for i in range(2)]
        o = m.sb("o", [P, NT, PAIRS * P])
        oT = m.sb("oT", [P, PAIRS, T])
        psQ, psK = m.ps("psQ", [P, T]), m.ps("psK", [P, T])
        psA = [m.ps(f"psA{i}", [P, T]) for i in range(2)]
        psN = [m.ps(f"psN{i}", [P, T]) for i in range(2)]
        psM = m.ps("psM", [P, T])
        psV = [*psA, load.psX]
        psO = [*psA, psQ, psK]
        v_made = m.flag("v_made", 8)
        v_copied = m.flag("v_copied", 8)
        qk_made = m.flag("qk_made", 16)
        qk_exped = m.flag("qk_exped", 32)
        phi = m.flag("phi", 32)
        inner = m.flag("inner", 16)
        masked = m.flag("masked", 16)
        k_turned = m.flag("k_turned", 8)
        k_copied = m.flag("k_copied", 8)
        state = m.flag("state", 24)
        state_copied = m.flag("state_copied", 24)
        numbered = m.flag("numbered", 16)
        divided = m.flag("divided", 48)
        o_turned = m.flag("o_turned", 8)
        o_copied = m.flag("o_copied", 8)
        projected = m.flag("projected", 1)
        loaded, cleared = m.sem("loaded"), m.sem("cleared")
        cut_high, cut_low = m.sem("cut_high"), m.sem("cut_low")
        m.credit(ACT.Exp)
        with nc.Block() as block:
            @block.sync
            def _(sp):
                col = lambda v: v.rearrange("(p a) -> p a", a=1)
                sp.dma_start(gain[:], col(a["L1_attn_ln1_g"])).then_inc(loaded, 16)
                sp.dma_start(offset[:], col(a["L1_attn_ln1_b"])).then_inc(loaded, 16)
                for i, name in enumerate("qkv"):
                    sp.dma_start(raw[i][:], a[f"L1_attn_W{name}"]).then_inc(loaded, 16)
                sp.dma_start(causal[:], a["c_causal"]).then_inc(loaded, 16)
                sp.dma_start(Wo[:], a["L1_attn_Wo"].rearrange("(c p) d -> p c d", p=P)).then_inc(loaded, 16)
                sp.wait_ge(loaded, 112)

            @block.gpsimd
            def _(pool):
                for pair in Q:
                    for tile in pair:
                        pool.memset(tile[:], 0.0)
                for tile in S:
                    pool.memset(tile[:], 0.0)
                pool.memset(G.X1[:, B, :, :], 0.0)
                pool.memset(VA[:, :, :, DH:W_], 1.0).then_inc(cleared, 1)
                load.pool(pool, 0)
                with turns(pool, B) as b:
                    load.pool(pool, b + 1)
                    post.pool(pool, b)

            @block.tensor
            def _(pe):
                every = (slice(None), slice(None))

                def project_pair(b, r):
                    qk_exped.wait(pe, b, 4 * r)
                    pair = (slice(None), slice(r * P, (r + 1) * P))
                    products(pe, psQ[:], Wq.cut(pair), load.xT.cut(every), True, True).then_inc(qk_made.sem, 1)
                    products(pe, psK[:], Wk.cut(pair), load.xT.cut(every), True, True).then_inc(qk_made.sem, 1)

                def inner_products(b, r, h):
                    phi.wait(pe, b, 4 * r + 4)
                    masked.wait(pe, b, 2 * r + h - 1)
                    for c in range(NT):
                        tok = slice(c * P, (c + 1) * P)
                        mm = pe.matmul(psA[h][:, tok], K[r % 2][:, tok], Q[RING[r]][h][:, tok],
                                       start=True, stop=True)
                    mm.then_inc(inner.sem, 1)

                def turn_keys(b, r):
                    load.xT_ready.wait(pe, b)
                    k_copied.wait(pe, b, r)
                    for c in range(NT):
                        tok = slice(c * P, (c + 1) * P)
                        mm = pe.transpose(load.psX[:, tok], K[r % 2][:, tok], G.ident[:])
                    mm.then_inc(k_turned.sem, 1)

                def states(b, r, c):
                    if c == 0:
                        k_copied.wait(pe, b, r + 1)
                    state_copied.wait(pe, b, 3 * r + c)
                    rhs = VA[:, c, 2 * r:2 * r + 2, :].rearrange("p h w -> p (h w)")
                    pe.matmul(psM[:, 0:2 * W_], Kt[r % 2][:, c, :], rhs, start=(c == 0), stop=(c == 2),
                              skip_group_check=True).then_inc(state.sem, 1)

                def turn_outputs(b, r):
                    divided.wait(pe, b, 6 * (r + 1))
                    if r == 0:
                        masked.wait(pe, b)
                    if r == 2:
                        qk_exped.wait(pe, b)
                    o_copied.wait(pe, b, r - 3)
                    for c in range(NT):
                        tok = slice(c * P, (c + 1) * P)
                        mm = pe.transpose(psO[r % 4][:, tok], o[:, c, r * P:(r + 1) * P], G.ident[:])
                    mm.then_inc(o_turned.sem, 1)

                def project_outputs(b, r):
                    o_copied.wait(pe, b, r + 1)
                    if r == 0:
                        divided.wait(pe, b, 45)
                    for t in range(NT):
                        mm = pe.matmul(psN[0][:, t * P:(t + 1) * P], oT[:, r, t:T:NT], Wo[:, r, :],
                                       start=(r == 0 and t == 0), stop=(r == PAIRS - 1), skip_group_check=True)
                    return mm

                def numerators(b, r, half):
                    if half == 0:
                        masked.wait(pe, b, 2 * r + 2)
                    state_copied.wait(pe, b, 3 * r + (1 if half == 0 else 3))
                    n = 2 * r + half
                    divided.wait(pe, b, 3 * (n - 1))
                    if n == 0:
                        post.summed.wait(pe, b - 1)
                    for i in range(2):
                        c = 2 * half + i
                        for h in range(2):
                            out = psN[half][:, (2 * i + h) * W_:(2 * i + h + 1) * W_]
                            mm = pe.matmul(out, AT[r % 2][h][:, c, :], VA[:, c, 2 * r + h, :],
                                           start=(i == 0 and h == 0), stop=(c == 0), skip_group_check=True)
                        if c:
                            mm = pe.matmul(psN[half][:, 2 * i * W_:(2 * i + 2) * W_],
                                           QQ[RING[r]][:, c * P:(c + 1) * P], S[r % 2][:, c - 1, :],
                                           start=False, stop=True, skip_group_check=True)
                    mm.then_inc(numbered.sem, 1)

                load.tensor(pe, 0)
                pe.wait_ge(loaded, 112)
                pe.wait_ge(cleared, 1)
                pe.wait_ge(cut_low, 3)
                with turns(pe, B) as b:
                    load.xT_ready.wait(pe, b)
                    project_pair(b, 0)
                    for n in range(8):
                        v_copied.wait(pe, b, n - 2)
                        tok, heads = slice((n // 2) * P, (n // 2 + 1) * P), slice((n % 2) * T, (n % 2 + 1) * T)
                        products(pe, psV[n % 3][:], load.xT.cut((slice(None), tok)), Wv.cut((slice(None), heads)),
                                 True, True).then_inc(v_made.sem, 1)
                    v_copied.wait(pe, b)
                    for r in range(PAIRS + 1):
                        if r + 1 < PAIRS:
                            project_pair(b, r + 1)
                        if r:
                            states(b, r - 1, 0)
                        if r < PAIRS:
                            inner_products(b, r, 0)
                        if r == PAIRS:
                            k_copied.wait(pe, b)
                            load.tensor(pe, b + 1)
                            turn_outputs(b, 0)
                        if r:
                            states(b, r - 1, 1)
                        if r < PAIRS:
                            inner_products(b, r, 1)
                        else:
                            numerators(b, r - 1, 0)
                            turn_outputs(b, 1)
                        if r:
                            states(b, r - 1, 2)
                        if r < PAIRS:
                            turn_keys(b, r)
                        else:
                            turn_outputs(b, 2)
                        if r:
                            if r < PAIRS:
                                numerators(b, r - 1, 0)
                            numerators(b, r - 1, 1)
                    turn_outputs(b, 3)
                    for r in range(PAIRS):
                        mm = project_outputs(b, r)
                        if r + 4 < PAIRS:
                            turn_outputs(b, r + 4)
                    mm.then_inc(projected.sem, 1)

            @block.scalar
            def _(act):
                def features(b, r, sides=range(2)):
                    for i in sides:
                        ps = (psQ, psK)[i]
                        qk_made.wait(act, b, 2 * r + i + 1)
                        phi.wait(act, b, 4 * r - (1 if i == 0 else 0))
                        act.activation(ex[i][:], ps[:], ACT.Exp).then_inc(qk_exped.sem, 1)
                        act.activation(re[i][:], ps[:], ACT.Relu).then_inc(qk_exped.sem, 1)

                def output_copy(b, r):
                    o_turned.wait(act, b, r + 1)
                    if r == 0:
                        projected.wait(act, b - 1)
                    act.activation(oT[:, r, :], psO[r % 4][:], ACT.Copy).then_inc(o_copied.sem, 1)

                def state_copy(b, r, c):
                    state.wait(act, b, 3 * r + c + 1)
                    numbered.wait(act, b, 2 * r - 2)
                    for h in range(2):
                        rows, cols = slice(DH * h, DH * (h + 1)), slice(W_ * h, W_ * (h + 1))
                        last = act.activation(S[r % 2][rows, c, cols], psM[rows, cols], ACT.Copy)
                    last.then_inc(state_copied.sem, 1)

                load.scalar(act, 0)
                act.wait_ge(cleared, 1)
                act.wait_ge(loaded, 112)
                for i, W in enumerate((Wq, Wk, Wv)):
                    act.activation(W.high[:], raw[i][:], ACT.Copy).then_inc(cut_high, 1)
                with turns(act, B) as b:
                    features(b, 0)
                    for n in range(8):
                        v_made.wait(act, b, n + 1)
                        if n == 0:
                            numbered.wait(act, b - 1)
                            state.wait(act, b - 1)
                        act.activation(VA[:, n // 2, 8 * (n % 2):8 * (n % 2) + 8, 0:DH],
                                       psV[n % 3][:].rearrange("p (h d) -> p h d", d=DH),
                                       ACT.Copy).then_inc(v_copied.sem, 1)
                    for r in range(PAIRS + 1):
                        if r + 1 < PAIRS:
                            features(b, r + 1, [0])
                        if r:
                            state_copy(b, r - 1, 0)
                        if r + 1 < PAIRS:
                            features(b, r + 1, [1])
                        if r:
                            if r == PAIRS:
                                output_copy(b, 0)
                            state_copy(b, r - 1, 1)
                            if r == PAIRS:
                                output_copy(b, 1)
                            state_copy(b, r - 1, 2)
                        if r < PAIRS:
                            k_turned.wait(act, b, r + 1)
                            state.wait(act, b, 3 * r - 3)
                            act.activation(Kt[r % 2][:], load.psX[:].rearrange("p (c d) -> p c d", c=NT),
                                           ACT.Copy).then_inc(k_copied.sem, 1)
                        if r == 1:
                            load.scalar(act, b + 1)
                    for r in range(2, PAIRS):
                        output_copy(b, r)

            @block.vector
            def _(dve):
                dve.wait_ge(loaded, 112)
                dve.wait_ge(cleared, 1)
                xT_users = [v_made, qk_made, k_copied]
                load.vector(dve, 0, xT_users)
                for i, W in enumerate((Wq, Wk, Wv)):
                    dve.wait_ge(cut_high, i + 1)
                    dve.tensor_tensor(W.low[:], raw[i][:], W.high[:].bitcast(F32), ALU.subtract).then_inc(cut_low, 1)
                with turns(dve, B) as b:
                    def features(r):
                        qk_exped.wait(dve, b, 4 * r + 2)
                        numbered.wait(dve, b, 2 * before(r) + 2)
                        for h in range(2):
                            rows = slice(DH * h, DH * (h + 1))
                            dve.scalar_tensor_tensor(out=Q[RING[r]][h][rows, :], in0=ex[0][rows, :], scalar=1.0,
                                                     in1=re[0][rows, :], op0=ALU.min, op1=ALU.add)\
                               .then_inc(phi.sem, 1)
                        dve.scalar_tensor_tensor(out=QQ[RING[r]][:], in0=ex[0][:], scalar=1.0, in1=re[0][:],
                                                 op0=ALU.min, op1=ALU.add).then_inc(phi.sem, 1)
                        qk_exped.wait(dve, b, 4 * r + 4)
                        inner.wait(dve, b, 2 * r - 2)
                        k_turned.wait(dve, b, r - 1)
                        dve.scalar_tensor_tensor(out=K[r % 2][:], in0=ex[1][:], scalar=1.0, in1=re[1][:],
                                                 op0=ALU.min, op1=ALU.add).then_inc(phi.sem, 1)

                    def mask(r):
                        for h in range(2):
                            inner.wait(dve, b, 2 * r + h + 1)
                            numbered.wait(dve, b, 2 * r - 2)
                            dve.tensor_tensor(AT[r % 2][h][:], psA[h][:].rearrange("p (c i) -> p c i", c=NT),
                                              causal[:].unsqueeze(1).broadcast_to([P, NT, P]), ALU.mult)\
                               .then_inc(masked.sem, 1)

                    def divide(r, half):
                        n = 2 * r + half
                        numbered.wait(dve, b, n + 1)
                        if n == 0:
                            o_turned.wait(dve, b - 1)
                        ps = psN[half][:, 0:4 * W_].rearrange("p (q w) -> p q w", w=W_)
                        dve.tensor_scalar(den[half][:], ps[:, :, DH:W_], EPS_DEN, None, ALU.max)\
                           .then_inc(divided.sem, 1)
                        divided.wait(dve, b, 3 * n + 1)
                        dve.reciprocal(den[half][:], den[half][:]).then_inc(divided.sem, 1)
                        divided.wait(dve, b, 3 * n + 2)
                        dst = o[:, 2 * half:2 * half + 2, r * P:(r + 1) * P].rearrange("p c (h d) -> p c h d", h=2)
                        num = psN[half][:, 0:4 * W_].rearrange("p (c h w) -> p c h w", c=2, h=2)
                        d4 = den[half][:].rearrange("p (c h) a -> p c h a", c=2)
                        dve.tensor_tensor(dst, num[:, :, :, 0:DH], d4.broadcast_to([P, 2, 2, DH]), ALU.mult)\
                           .then_inc(divided.sem, 1)

                    features(0)
                    for r in range(PAIRS + 1):
                        if r + 1 < PAIRS:
                            features(r + 1)
                        if r < PAIRS:
                            mask(r)
                        else:
                            load.vector(dve, b + 1, xT_users)
                        if r:
                            divide(r - 1, 0)
                            divide(r - 1, 1)
                    projected.wait(dve, b)
                    load.x_kept.wait(dve, b)
                    x1 = batch(G.X1, b)
                    dve.tensor_tensor(x1, psN[0][:].rearrange("p (t d) -> p t d", t=NT), batch(G.X, b), ALU.add)\
                       .then_inc(post.summed.sem, 1)
                    post.vector(dve, b, x1)



def gelu_stage(nc, G, tag, a):
    C = 4
    with ExitStack() as ctx:
        m = Stage(nc, ctx, tag)
        gain, offset = m.sb("gain", [P, 1]), m.sb("offset", [P, 1])
        load, post = Load(m, G, G.X1, affine=(gain, offset), split=True), Post(m, G)
        raw, W1, W2 = m.sb("raw", [P, C * P]), Pair(m, "W1", [P, C * P]), m.sb("W2", [P, C, P])
        cut_high, cut_low = m.sem("cut_high"), m.sem("cut_low")
        act_ = [m.sb(f"act{i}", [P, C, T]) for i in range(1)]
        psH = [m.ps(f"psH{i}", [P, T]) for i in range(2)]
        psY = m.ps("psY", [P, NT, P])
        hidden = m.flag("hidden", C)
        activated = m.flag("activated", C)
        projected = m.flag("projected", 1)
        base_ready = m.flag("base_ready", 1)
        loaded = m.sem("loaded")
        m.credit(ACT.Gelu)
        with nc.Block() as block:
            @block.sync
            def _(sp):
                col = lambda v: v.rearrange("(p a) -> p a", a=1)
                sp.dma_start(gain[:], col(a["L1_attn_ln2_g"])).then_inc(loaded, 16)
                sp.dma_start(offset[:], col(a["L1_attn_ln2_b"])).then_inc(loaded, 16)
                sp.dma_start(raw[:], a["L1_attn_Wf1"]).then_inc(loaded, 16)
                sp.dma_start(W2[:], a["L1_attn_Wf2"].rearrange("(c p) d -> p c d", p=P)).then_inc(loaded, 16)
                sp.wait_ge(loaded, 64)

            @block.scalar
            def _(act):
                load.scalar(act, 0)
                act.wait_ge(loaded, 64)
                act.activation(W1.high[:], raw[:], ACT.Copy).then_inc(cut_high, 1)
                with turns(act, B) as b:
                    load.scalar(act, b + 1)
                    for c in range(C):
                        hidden.wait(act, b, c + 1)
                        projected.wait(act, b - 1)
                        act.activation(act_[0][:, c, :], psH[c % 2][:], ACT.Gelu).then_inc(activated.sem, 1)

            @block.gpsimd
            def _(pool):
                def prepare(b):
                    x = batch(G.X, b)
                    pool.tensor_tensor(x, x, batch(G.X1, b), ALU.add).then_inc(base_ready.sem, 1)

                load.xs_ready.wait(pool, 0)
                pool.sem_inc(load.x_kept.sem, 1)
                prepare(0)
                with turns(pool, B) as b:
                    load.xs_ready.wait(pool, b + 1)
                    pool.sem_inc(load.x_kept.sem, 1)
                    prepare(b + 1)
                    post.pool(pool, b)

            @block.tensor
            def _(pe):
                load.tensor(pe, 0)
                pe.wait_ge(loaded, 64)
                pe.wait_ge(cut_low, 1)
                with turns(pe, B) as b:
                    load.xT_ready.wait(pe, b)
                    for c in range(C):
                        activated.wait(pe, b, c - 1)
                        products(pe, psH[c % 2][:], W1.cut((slice(None), slice(c * P, (c + 1) * P))),
                                 load.xT.cut((slice(None), slice(None))), True, True).then_inc(hidden.sem, 1)
                    load.tensor(pe, b + 1)
                    activated.wait(pe, b)
                    post.summed.wait(pe, b - 1)
                    for t in range(NT):
                        for c in range(C):
                            mm = pe.matmul(psY[:, t, :], act_[0][:, c, t:T:NT], W2[:, c, :],
                                           start=(c == 0), stop=(c == C - 1))
                    mm.then_inc(projected.sem, 1)

            @block.vector
            def _(dve):
                dve.wait_ge(loaded, 64)
                load.vector(dve, 0, [hidden])
                dve.wait_ge(cut_high, 1)
                dve.tensor_tensor(W1.low[:], raw[:], W1.high[:].bitcast(F32), ALU.subtract).then_inc(cut_low, 1)
                with turns(dve, B) as b:
                    load.vector(dve, b + 1, [hidden])
                    projected.wait(dve, b)
                    base_ready.wait(dve, b)
                    x = batch(G.X, b)
                    dve.tensor_tensor(x, psY[:], x, ALU.add).then_inc(post.summed.sem, 1)
                    post.vector(dve, b, x)


def ternary_stage(nc, G, tag, a):
    C, F = 4, 512
    with ExitStack() as ctx:
        m = Stage(nc, ctx, tag)
        load, post = Load(m, G, G.X, split=True), Post(m, G)
        Wfc, Wp = m.sb("Wfc", [P, F]), m.sb("Wp", [P, F])
        Wt = m.sb("Wt", [P, F], F32R)
        above, below = m.sb("above", [P, F]), m.sb("below", [P, F])
        size, half = m.sb("size", [P, 2]), m.sb("half", [P, 2, 2])
        ones = m.sb("ones", [P, P])
        gain, offset = m.sb("gain", [P, C]), m.sb("offset", [P, C])
        h = [m.sb(f"h{i}", [P, NT, F]) for i in range(2)]
        hT = m.sb("hT", [P, C, T])
        st, mv = m.sb("st", [P, NT, 6]), [m.sb(f"mvh{i}", [P, NT, 2]) for i in range(2)]
        rs, sh = ([m.sb(f"{n}{i}", [P, NT]) for i in range(2)] for n in ("rs", "sh"))
        psH = [m.ps(f"psH{i}", [P, F]) for i in range(2)]
        psT = [m.ps(f"psT{i}", [P, T]) for i in range(2)]
        psY = m.ps("psY", [P, NT, P])
        hidden = m.flag("hidden", NT)
        geluted = m.flag("geluted", NT)
        stat = m.flag("statted", NT)
        aggregated = m.flag("aggr", 1)
        scaled = m.flag("scaled", 4, lead=2)
        pool_passed = m.sem("pool_passed")
        normed = m.flag("normed", NT, lead=2)
        turned_h = m.flag("turned_h", C, lead=2)
        copied = m.flag("copied", C)
        projected = m.flag("projected", 1)
        loaded, prep, filled, summed = (m.sem(n) for n in ("loaded", "prep", "filled", "sizes"))
        m.credit(ACT.Gelu)

        def pairs(engine, body):
            with engine.Fori(0, B // 2) as half:
                for i in range(2):
                    body(2 * half + i, i)

        def to_signs(dve):
            dve.memset(ones[:], 1.0).then_inc(filled, 1)
            dve.wait_ge(loaded, 64)
            for i, w in enumerate((Wfc, Wp)):
                dve.tensor_reduce(size[:, i:i + 1], w[:], AX.X, ALU.add, apply_absolute_value=True)\
                   .then_inc(filled, 1)
            dve.wait_ge(summed, 1)
            dve.tensor_scalar(half[:, 0, :], psY[:, 0, 0:2], 1.0 / (P * F), 1e-6, ALU.mult, ALU.add)\
               .then_inc(prep, 1)
            dve.wait_ge(prep, 1)
            dve.tensor_scalar(half[:, 1, :], half[:, 0, :], -0.5, None, ALU.mult).then_inc(prep, 1)
            dve.wait_ge(prep, 2)
            dve.tensor_scalar(half[:, 0, :], half[:, 0, :], 0.5, None, ALU.mult).then_inc(prep, 1)
            dve.wait_ge(prep, 3)
            for i, w in enumerate((Wfc, Wp)):
                dve.wait_ge(prep, 3 + 3 * i)
                dve.tensor_scalar(above[:], w[:], half[:, 0, i:i + 1], None, ALU.is_gt).then_inc(prep, 1)
                dve.tensor_scalar(below[:], w[:], half[:, 1, i:i + 1], None, ALU.is_lt).then_inc(prep, 1)
                dve.wait_ge(prep, 5 + 3 * i)
                signs = Wt if w is Wfc else w
                dve.tensor_tensor(signs[:], above[:], below[:], ALU.subtract).then_inc(prep, 1)

        with nc.Block() as block:
            @block.sync
            def _(sp):
                sp.dma_start(Wfc[:], a["L1_ffn_W_fc"]).then_inc(loaded, 16)
                sp.dma_start(Wp[:].rearrange("p (c d) -> p c d", c=C),
                             a["L1_ffn_W_proj"].rearrange("(c p) d -> p c d", p=P)).then_inc(loaded, 16)
                sp.dma_start(gain[:], a["L1_ln_w"]).then_inc(loaded, 16)
                sp.dma_start(offset[:], a["L1_ln_b"]).then_inc(loaded, 16)
                sp.wait_ge(loaded, 64)

            @block.scalar
            def _(act):
                def first(b, i):
                    turned_h.wait(act, b - 2)
                    for t in range(NT):
                        hidden.wait(act, b, t + 1)
                        act.activation(h[i][:, t, :], psH[t % 2][:], ACT.Gelu).then_inc(geluted.sem, 1)

                def body(b, i):
                    scaled.wait(act, b)
                    for t in range(NT):
                        act.activation(h[i][:, t, :], h[i][:, t, :], ACT.Identity, scale=rs[i][:, t:t + 1],
                                       bias=sh[i][:, t:t + 1]).then_inc(normed.sem, 1)
                    first(b + 1, 1 - i)
                    load.scalar(act, b + 2)

                load.scalar(act, 0)
                first(0, 0)
                load.scalar(act, 1)
                pairs(act, body)

            @block.gpsimd
            def _(pool):
                def first(b, i):
                    c = Chain(scaled, pool, b)
                    aggregated.wait(pool, b)
                    normed.wait(pool, b - 2)
                    stand(pool, pool_passed)
                    c.step(pool.tensor_scalar(rs[i][:], mv[i][:, :, 1], LN_EPS, None, ALU.add))
                    c.wait()
                    c.step(pool.tensor_tensor(rs[i][:], rs[i][:], G.minus_half[:], ALU.pow))
                    c.wait()
                    c.step(pool.tensor_tensor(sh[i][:], mv[i][:, :, 0], rs[i][:], ALU.mult))
                    c.wait()
                    stand(pool, pool_passed)
                    c.step(pool.tensor_scalar(sh[i][:], sh[i][:], -1.0, None, ALU.mult))
                    c.end()

                def body(b, i):
                    first(b + 1, 1 - i)
                    load.pool(pool, b + 2)
                    post.pool(pool, b)

                load.pool(pool, 0)
                first(0, 0)
                load.pool(pool, 1)
                pairs(pool, body)

            @block.tensor
            def _(pe):
                def hidden_of(b, t):
                    if t == 0:
                        load.xT_ready.wait(pe, b)
                    geluted.wait(pe, b, t - 1)
                    low, high = load.xT.low[:, t:T:NT], load.xT.high[:, t:T:NT]
                    pe.matmul(psH[t % 2][:], low, Wt[:], start=True, stop=False, skip_group_check=True)
                    pe.matmul(psH[t % 2][:], high, Wt[:], start=False, stop=True, skip_group_check=True)\
                      .then_inc(hidden.sem, 1)

                def turn_h(b, i, c):
                    if c == 0:
                        normed.wait(pe, b)
                    copied.wait(pe, b, c - 1)
                    for t in range(NT):
                        mm = pe.transpose(psT[c % 2][:, t * P:(t + 1) * P], h[i][:, t, c * P:(c + 1) * P], G.ident[:])
                    mm.then_inc(turned_h.sem, 1)

                def body(b, i):
                    hidden_of(b + 1, 0)
                    hidden_of(b + 1, 1)
                    turn_h(b, i, 0)
                    turn_h(b, i, 1)
                    turn_h(b, i, 2)
                    hidden_of(b + 1, 2)
                    turn_h(b, i, 3)
                    hidden_of(b + 1, 3)
                    copied.wait(pe, b)
                    post.summed.wait(pe, b - 1)
                    for t in range(NT):
                        for c in range(C):
                            mm = pe.matmul(psY[:, t, :], hT[:, c, t * P:(t + 1) * P], Wp[:, c * P:(c + 1) * P],
                                           start=(c == 0), stop=(c == C - 1))
                    mm.then_inc(projected.sem, 1)
                    load.tensor(pe, b + 2)

                load.tensor(pe, 0)
                pe.wait_ge(filled, 3)
                pe.matmul(psY[:, 0, 0:2], ones[:], size[:], start=True, stop=True).then_inc(summed, 1)
                pe.wait_ge(prep, 6)
                for t in range(NT):
                    hidden_of(0, t)
                load.tensor(pe, 1)
                pe.wait_ge(prep, 9)
                pairs(pe, body)

            @block.vector
            def _(dve):
                def statistics(b, i, t):
                    geluted.wait(dve, b, t + 1)
                    stand(dve, post.passed)
                    dve.bn_stats(st[:, t, :], h[i][:, t, :]).then_inc(stat.sem, 1)

                def aggregate(b, i):
                    stat.wait(dve, b)
                    scaled.wait(dve, b - 2)
                    stand(dve, post.passed)
                    for t in range(NT):
                        last = dve.bn_aggr(mv[i][:, t, :], st[:, t, :])
                    last.then_inc(aggregated.sem, 1)

                def copy_h(b, c):
                    turned_h.wait(dve, b, c + 1)
                    projected.wait(dve, b - 1)
                    dve.tensor_scalar(hT[:, c, :], psT[c % 2][:], gain[:, c:c + 1], offset[:, c:c + 1],
                                      ALU.mult, ALU.add).then_inc(copied.sem, 1)

                def body(b, i):
                    copy_h(b, 0)
                    copy_h(b, 1)
                    statistics(b + 1, 1 - i, 0)
                    copy_h(b, 2)
                    statistics(b + 1, 1 - i, 1)
                    copy_h(b, 3)
                    statistics(b + 1, 1 - i, 2)
                    statistics(b + 1, 1 - i, 3)
                    aggregate(b + 1, 1 - i)
                    projected.wait(dve, b)
                    load.x_kept.wait(dve, b)
                    x = batch(G.X, b)
                    dve.tensor_tensor(x, psY[:], x, ALU.add).then_inc(post.summed.sem, 1)
                    load.vector(dve, b + 2, [hidden])
                    post.vector(dve, b, x)

                load.vector(dve, 0, [hidden])
                to_signs(dve)
                for t in range(NT):
                    statistics(0, 0, t)
                aggregate(0, 0)
                load.vector(dve, 1, [hidden])
                pairs(dve, body)


def fourier_stage(nc, G, tag, a, out):
    with ExitStack() as ctx:
        m = Stage(nc, ctx, tag)
        load, post = Load(m, G, G.X), Post(m, G)
        Wr, Wi, Cc, Ss = (m.sb(n, [P, P]) for n in ("Wr", "Wi", "cos", "sin"))
        minus_cos = m.sb("minus_cos", [P, P])
        Ur, nUi, M = (m.sb(n, [P, P]) for n in ("Ur", "nUi", "M"))
        bias = m.sb("bias", [P, P])
        y = m.sb("y", [P, B, NT, P])
        psM = m.ps("psM", [P, 3, P])
        psY = m.ps("psY", [P, NT, P])
        normed = m.flag("normed", 1)
        stored = m.sem("stored")
        projected = m.flag("projected", 1)
        loaded, made, kept = (m.sem(n) for n in ("loaded", "made", "kept"))
        m.credit(ACT.Identity)
        with nc.Block() as block:
            @block.sync
            def _(sp):
                for dst, n in ((Wr, "L3_ffn_w_freq_real"), (Wi, "L3_ffn_w_freq_imag"), (Cc, "c_cos"), (Ss, "c_sin")):
                    sp.dma_start(dst[:], a[n]).then_inc(loaded, 16)
                sp.dma_start(bias[:], a["L3_ffn_bias"].rearrange("(a n) -> a n", a=1).broadcast_to([P, P]))\
                  .then_inc(loaded, 16)
                sp.wait_ge(loaded, 80)
                dst = out.rearrange("b (p t) d -> b p t d", t=NT)
                with turns(sp, B) as b:
                    normed.wait(sp, b)
                    sp.dma_start(dst[bass.ds(b, 1), :, :, :].rearrange("a p t d -> p (a t) d"), batch(y, b))\
                      .then_inc(stored, 16)
                sp.wait_ge(stored, 16 * B)

            def make_matrix(pe):
                pe.wait_ge(loaded, 80)
                pe.wait_ge(kept, 1)
                pe.matmul(psM[:, 0, :], Wr[:], Cc[:], start=True, stop=False)
                pe.matmul(psM[:, 0, :], Wi[:], Ss[:], start=False, stop=True).then_inc(made, 1)
                pe.wait_ge(kept, 2)
                pe.matmul(psM[:, 1, :], Wr[:], Ss[:], start=True, stop=False)
                pe.matmul(psM[:, 1, :], Wi[:], minus_cos[:], start=False, stop=True).then_inc(made, 1)
                pe.wait_ge(kept, 3)
                pe.matmul(psM[:, 2, :], Ur[:], Cc[:], start=True, stop=False)
                pe.matmul(psM[:, 2, :], nUi[:], Ss[:], start=False, stop=True).then_inc(made, 1)

            def keep_matrix(dve):
                dve.wait_ge(loaded, 80)
                dve.tensor_scalar(minus_cos[:], Cc[:], -1.0, None, ALU.mult).then_inc(kept, 1)
                dve.wait_ge(made, 1)
                dve.tensor_copy(Ur[:], psM[:, 0, :]).then_inc(kept, 1)
                dve.wait_ge(made, 2)
                dve.tensor_copy(nUi[:], psM[:, 1, :]).then_inc(kept, 1)
                dve.wait_ge(made, 3)
                dve.tensor_scalar(M[:], psM[:, 2, :], 1.0 / P, None, ALU.mult).then_inc(kept, 1)

            @block.scalar
            def _(act):
                def finish(b):
                    post.rooted.wait(act, b)
                    for t in range(NT):
                        last = act.activation(batch(y, b)[:, t, :], batch(G.X, b)[:, t, :], ACT.Identity,
                                              scale=G.rstd[:, bass.ds(b, 1), t], bias=G.shift[:, bass.ds(b, 1), t])
                    last.then_inc(normed.sem, 1)

                load.scalar(act, 0)
                load.scalar(act, 1)
                with act.Fori(1, B) as b:
                    load.scalar(act, b + 1)
                    finish(b - 1)
                finish(B - 1)

            @block.gpsimd
            def _(pool):
                def prepare(b):
                    load.xs_ready.wait(pool, b)
                    pool.tensor_tensor(batch(G.X, b), load.xs[:], bias[:].unsqueeze(1).broadcast_to([P, NT, P]),
                                       ALU.add).then_inc(load.x_kept.sem, 1)

                pool.wait_ge(loaded, 80)
                prepare(0)
                with turns(pool, B) as b:
                    prepare(b + 1)
                    post.pool(pool, b)

            @block.tensor
            def _(pe):
                load.tensor(pe, 0)
                make_matrix(pe)
                pe.wait_ge(kept, 4)
                with turns(pe, B) as b:
                    load.xT_ready.wait(pe, b)
                    post.summed.wait(pe, b - 1)
                    for t in range(NT):
                        mm = pe.matmul(psY[:, t, :], load.xT[:, t:T:NT], M[:], start=True, stop=True)
                    mm.then_inc(projected.sem, 1)
                    load.tensor(pe, b + 1)

            @block.vector
            def _(dve):
                load.vector(dve, 0, [projected])
                keep_matrix(dve)
                with turns(dve, B) as b:
                    load.vector(dve, b + 1, [projected])
                    projected.wait(dve, b)
                    load.x_kept.wait(dve, b)
                    x = batch(G.X, b)
                    dve.tensor_tensor(x, psY[:], x, ALU.add).then_inc(post.summed.sem, 1)
                    post.vector(dve, b, x)



def constants():
    i = np.arange(P)
    t = np.arange(T)
    bf = mybir.dt.np(BF16)
    ones = np.ones(T)
    high, low = (t // 256) * 256, t % 256
    kdecay = np.stack([high, low, ones, ones])
    qdecay = np.stack([ones, ones, -high, -low])
    rep = lambda x: np.ascontiguousarray(np.broadcast_to(x[:, None, :], (4, H, T))).astype(bf)
    future = np.where(i[None, :] > i[:, None], MASKED, 0.0)
    tail = np.zeros((P - DECAY_ROWS - PARTS * PARTS * HD, T))
    ktail = tail.copy()
    ktail[MAX_ROW - P:][:PARTS] = 1.0
    masks = np.stack([future, future.T], axis=1).astype(bf)
    angle = 2 * np.pi * ((i[:, None] * i[None, :]) % P) / P
    return {
        "c_ident": np.eye(P, dtype=np.float32),
        "c_qdecay": rep(qdecay),
        "c_kdecay": rep(kdecay),
        "c_qtail": tail.astype(bf),
        "c_ktail": ktail.astype(bf),
        "c_masks": masks,
        "c_blocks": (i[:, None] // HD == i[None, :] // HD).astype(np.float32),
        "c_causal": (i[None, :] >= i[:, None]).astype(np.float32),
        "c_cos": np.cos(angle).astype(np.float32),
        "c_sin": np.sin(angle).astype(np.float32),
        "c_iota": np.ascontiguousarray(np.broadcast_to(np.arange(12, dtype=np.float32), (P, 12))),
    }


def layouts(x):
    out = dict(x)
    T_ = lambda w: np.ascontiguousarray(np.swapaxes(w, -1, -2))
    for name in ("L0_attn_Wq", "L0_attn_Wk", "L0_attn_Wv", "L0_attn_Wo", "L2_attn_Wq_w", "L2_attn_Wk_w",
                 "L2_attn_Wv_w", "L1_ffn_W_fc", "L1_ffn_W_proj", "L2_ffn_gate_w", "L2_ffn_w1", "L2_ffn_w2"):
        out[name] = T_(x[name])
    w, b = out.pop("L3_attn_w_qkv"), out.pop("L3_attn_b_qkv")
    for n, side in enumerate("qkv"):
        out[f"L3_w{side}"] = np.ascontiguousarray(w[:, n * P:(n + 1) * P])
        out[f"L3_b{side}"] = np.ascontiguousarray(b[n * P:(n + 1) * P])
    for side in "qv":
        out[f"L3_a{side}T"] = T_(out.pop(f"L3_attn_a_{side}"))
    out["L0_be1"] = np.ascontiguousarray(out.pop("L0_ffn_be1").reshape(12, 6, P).transpose(2, 0, 1))
    out["L0_bs1"] = T_(out.pop("L0_ffn_bs1").reshape(4, P))
    out["L0_b2"] = np.concatenate([out.pop("L0_ffn_be2"), out.pop("L0_ffn_bs2")[None]])
    out["L1_ln_w"], out["L1_ln_b"] = (T_(out.pop(f"L1_ffn_ln_{n}").reshape(4, P)) for n in "wb")
    return out


STAGES = ("A0", "M0", "L1", "T1", "A2", "M2", "A3", "F3")


def program(nc, a, out, stages=STAGES):
    Stage.left = []
    with ExitStack() as ctx:
        G = setup(nc, ctx, a)
        for s in stages:
            if s == "A0":
                attention_stage(nc, G, s, a, "decay")
            elif s == "A2":
                attention_stage(nc, G, s, a, "cross")
            elif s == "A3":
                attention_stage(nc, G, s, a, "lora")
            elif s == "M0":
                expert_stage(nc, G, s, a, True)
            elif s == "M2":
                expert_stage(nc, G, s, a, False)
            elif s == "L1":
                with nc.sbuf_tensor("X1", [P, B + 1, NT, P], F32) as G.X1:
                    linear_attention_stage(nc, G, s, a)
                    gelu_stage(nc, G, "F1", a)
            elif s == "T1":
                ternary_stage(nc, G, s, a)
            elif s == "F3":
                fourier_stage(nc, G, s, a, out)
        if stages[-1] != "F3":
            store(nc, G, out)


def store(nc, G, out):
    with ExitStack() as ctx:
        m = Stage(nc, ctx, "st")
        y = m.sb("y", [P, B, NT, P])
        ready, stored = m.sem("ready"), m.sem("stored")
        m.credit(ACT.Identity)
        with nc.Block() as block:
            @block.scalar
            def _(act):
                with turns(act, B) as b:
                    for t in range(NT):
                        last = act.activation(batch(y, b)[:, t, :], batch(G.X, b)[:, t, :], ACT.Identity,
                                              scale=G.rstd[:, bass.ds(b, 1), t], bias=G.shift[:, bass.ds(b, 1), t])
                    last.then_inc(ready, 1)

            @block.sync
            def _(sp):
                dst = out.rearrange("b (p t) d -> b p t d", t=NT)
                with turns(sp, B) as b:
                    sp.wait_ge(ready, b + 1)
                    sp.dma_start(dst[bass.ds(b, 1), :, :, :].rearrange("a p t d -> p (a t) d"), batch(y, b))\
                      .then_inc(stored, 16)
                sp.wait_ge(stored, 16 * B)


def kernel(**inputs):
    import concourse.bacc as bacc
    from concourse.bass_utils import run_bass_kernel_spmd

    arrays = {**layouts({k: np.asarray(v) for k, v in inputs.items()}), **constants()}
    nc = bacc.Bacc("TRN2", target_bir_lowering=False, num_devices=1)
    a = {n: nc.dram_tensor(n, v.shape, mybir.dt.from_np(v.dtype), kind="ExternalInput").ap()
         for n, v in arrays.items()}
    out = nc.dram_tensor("out", (B, T, P), F32, kind="ExternalOutput").ap()
    program(nc, a, out)
    return run_bass_kernel_spmd(nc, [arrays], core_ids=[0]).results[0]["out"]
```
